# Optimizing a Trainium2 kernel written in Bass

```python
import numpy as np
import jax
import jax.numpy as jnp

def _softmax(x, axis=-1):
    return jax.nn.softmax(x, axis=axis)

def _gelu(x):
    return jax.nn.gelu(x, approximate=True)

def _silu(x):
    return jax.nn.silu(x)

def _sigmoid(x):
    return jax.nn.sigmoid(x)

def _layernorm(x, axis=-1, eps=1e-05):
    m = jnp.mean(x, axis=axis, keepdims=True)
    v = jnp.var(x, axis=axis, keepdims=True)
    return (x - m) / jnp.sqrt(v + eps)

def _scatter_add(tgt, idx, src, axis=0):
    return tgt.at[idx].add(src)

def _segment_sum(src, seg, n):
    return jax.ops.segment_sum(src, seg, n)
kernel_name = 'mk_adaln_ffn_d2_seqx_r8_5d5998'

def setup_inputs(seed: int=0):
    np.random.seed(seed)
    _w = jnp.asarray

    def _rec_inputs():
        import jax
        import jax.numpy as jnp
        _rk = jax.random.key(seed)
        x = -0.0003929 + 0.9999 * jax.random.normal(jax.random.fold_in(_rk, 1), (64, 32, 512), jnp.float32)
        _lenS = 32 - jax.random.randint(jax.random.fold_in(_rk, 7), (64,), 0, max(1, 32 // 4) + 1, jnp.int32)
        _lenS2 = 32 - jax.random.randint(jax.random.fold_in(_rk, 8), (64,), 0, max(1, 32 // 4) + 1, jnp.int32)
        itok_B_8_3872 = jax.random.randint(jax.random.fold_in(_rk, 11), (64,), 8, 3873, jnp.int32)
        itok_B_2_6 = jax.random.randint(jax.random.fold_in(_rk, 12), (64,), 2, 7, jnp.int32)
        return (x, itok_B_8_3872, itok_B_2_6)
    x, itok_B_8_3872, itok_B_2_6 = _rec_inputs()

    def _L0_cond_setup():
        import math
        import jax, jax.numpy as jnp
        import numpy as np
        H, N, B, L = (32, 64, 16, 512)
        DT_MIN, DT_MAX = (0.001, 0.1)

        def _get_kernel(log_dt, C, log_A_real, A_imag, length):
            Cc = C[..., 0] + 1j * C[..., 1]
            dt = jnp.exp(log_dt)
            A = -jnp.exp(log_A_real) + 1j * A_imag
            dtA = A * dt[:, None]
            P = dtA[:, :, None] * jnp.arange(length, dtype=jnp.float32)
            Cs = Cc * (jnp.exp(dtA) - 1.0) / A
            K = 2.0 * jnp.einsum('hn,hnl->hl', Cs, jnp.exp(P)).real
            return K
        key = jax.random.key(seed)
        ks = jax.random.split(key, 6)
        u = jax.random.normal(ks[0], (B, H, L), dtype=jnp.float32)
        length = jax.random.randint(ks[1], (B,), 0, L)
        log_dt = jax.random.uniform(ks[2], (H,), dtype=jnp.float32) * (math.log(DT_MAX) - math.log(DT_MIN)) + math.log(DT_MIN)
        C = jax.random.normal(ks[3], (H, N, 2), dtype=jnp.float32)
        log_A_real = jnp.log(0.5 * jnp.ones((H, N), dtype=jnp.float32))
        A_imag = math.pi * jnp.broadcast_to(jnp.arange(N, dtype=jnp.float32), (H, N))
        D = jax.random.normal(ks[4], (H,), dtype=jnp.float32)
        return {'u': u, 'length': length, 'log_dt': log_dt, 'C': C, 'log_A_real': log_A_real, 'A_imag': A_imag, 'D': D}
    _L0_cond_all = _L0_cond_setup()
    _L0_cond_in = {k: v for k, v in _L0_cond_all.items() if k in ('log_dt', 'C', 'log_A_real', 'A_imag', 'D')}
    del _L0_cond_all

    def _L0_ffn_setup():
        import jax, jax.numpy as jnp
        import numpy as np
        B, S, IN, OUT = (4, 256, 512, 512)
        E, K, R = (8, 2, 16)
        CAP_FACTOR = 3.0
        ALPHA = 1.0 / R
        LN_EPS = 1e-05
        key = jax.random.key(seed)
        ks = jax.random.split(key, 6)
        return {'x': jax.random.normal(ks[0], (B, S, IN), dtype=jnp.float32), 'weight': jax.random.normal(ks[1], (OUT, IN), dtype=jnp.float32) * 0.02, 'lora_A': jax.random.normal(ks[2], (E, IN, R), dtype=jnp.float32) / np.sqrt(R), 'lora_B': jax.random.normal(ks[3], (E, R, OUT), dtype=jnp.float32) * 0.02, 'gw1': jax.random.normal(ks[4], (4 * E, IN), dtype=jnp.float32) * 0.02, 'gb1': jnp.zeros((4 * E,), dtype=jnp.float32), 'ln_gamma': jnp.ones((4 * E,), dtype=jnp.float32), 'ln_beta': jnp.zeros((4 * E,), dtype=jnp.float32), 'gw2': jax.random.normal(ks[5], (E, 4 * E), dtype=jnp.float32) * 0.02, 'gb2': jnp.zeros((E,), dtype=jnp.float32)}
    _L0_ffn_all = _L0_ffn_setup()
    _L0_ffn_in = {k: v for k, v in _L0_ffn_all.items() if k in ('weight', 'lora_A', 'lora_B', 'gw1', 'gb1', 'ln_gamma', 'ln_beta', 'gw2', 'gb2')}
    del _L0_ffn_all

    def _L1_cond_setup():
        import jax, jax.numpy as jnp
        import numpy as np
        B, N, H, F = (4, 64, 512, 1376)
        L, R, RANK = (1, 16, 16)
        SCALE = 0.5
        key = jax.random.key(seed)
        ks = jax.random.split(key, 12)
        nrm = lambda k, shape, fan: jax.random.normal(k, shape, jnp.float32) * fan ** (-0.5)
        inp = {'x': jax.random.normal(ks[0], (B, N, H), jnp.float32), 'W_gate': nrm(ks[1], (F, H), H), 'W_up': nrm(ks[2], (F, H), H), 'W_down': nrm(ks[3], (H, F), F), 'A_gate': nrm(ks[4], (L, R, RANK, H), H), 'B_gate': nrm(ks[5], (L, R, F, RANK), RANK), 'A_up': nrm(ks[6], (L, R, RANK, H), H), 'B_up': nrm(ks[7], (L, R, F, RANK), RANK), 'A_down': nrm(ks[8], (L, R, RANK, F), F), 'B_down': nrm(ks[9], (L, R, H, RANK), RANK), 'lora_indices': jax.random.randint(ks[10], (B,), 0, R), 'layer_idx': 0}
        return inp
    _L1_cond_all = _L1_cond_setup()
    _L1_cond_in = {k: v for k, v in _L1_cond_all.items() if k in ('W_gate', 'W_up', 'W_down', 'A_gate', 'B_gate', 'A_up', 'B_up', 'A_down', 'B_down')}
    del _L1_cond_all

    def _L1_ffn_setup():
        import jax, jax.numpy as jnp
        import numpy as np
        HIDDEN = 512
        MOE_INTER = 128
        SHARED_INTER = 512
        NUM_EXPERTS = 16
        TOP_K = 2

        def _moe_forward(x, gate_w, w_gate_up, w_down, shared_w_gate_up, shared_w_down):
            orig_shape = x.shape
            x2 = x.reshape(-1, orig_shape[-1])
            gu_s = x2 @ shared_w_gate_up.T
            g_s, u_s = jnp.split(gu_s, 2, axis=-1)
            shared_out = jax.nn.silu(g_s) * u_s @ shared_w_down.T
            logits = x2 @ gate_w.T
            probs = jax.nn.softmax(logits, axis=-1)
            topk_vals, topk_idx = jax.lax.top_k(probs, TOP_K)
            topk_vals = topk_vals / jnp.sum(topk_vals, axis=-1, keepdims=True)
            combine = jnp.sum(jax.nn.one_hot(topk_idx, NUM_EXPERTS, dtype=x2.dtype) * topk_vals[..., None], axis=1)
            gu = jnp.einsum('th,eih->eti', x2, w_gate_up)
            g, u = jnp.split(gu, 2, axis=-1)
            act = jax.nn.silu(g) * u
            out_e = jnp.einsum('eti,ehi->eth', act, w_down)
            moe_out = jnp.einsum('eth,te->th', out_e, combine)
            return (moe_out + shared_out).reshape(orig_shape)
        key = jax.random.key(seed)
        ks = jax.random.split(key, 6)
        s = 0.02
        hidden_states = jax.random.normal(ks[0], (2, 256, HIDDEN), dtype=jnp.float32)
        gate_w = jax.random.normal(ks[1], (NUM_EXPERTS, HIDDEN), dtype=jnp.float32) * s
        w_gate_up = jax.random.normal(ks[2], (NUM_EXPERTS, 2 * MOE_INTER, HIDDEN), dtype=jnp.float32) * s
        w_down = jax.random.normal(ks[3], (NUM_EXPERTS, HIDDEN, MOE_INTER), dtype=jnp.float32) * s
        shared_w_gate_up = jax.random.normal(ks[4], (2 * SHARED_INTER, HIDDEN), dtype=jnp.float32) * s
        shared_w_down = jax.random.normal(ks[5], (HIDDEN, SHARED_INTER), dtype=jnp.float32) * s
        return {'hidden_states': hidden_states, 'gate_w': gate_w, 'w_gate_up': w_gate_up, 'w_down': w_down, 'shared_w_gate_up': shared_w_gate_up, 'shared_w_down': shared_w_down}
    _L1_ffn_all = _L1_ffn_setup()
    _L1_ffn_in = {k: v for k, v in _L1_ffn_all.items() if k in ('gate_w', 'w_gate_up', 'w_down', 'shared_w_gate_up', 'shared_w_down')}
    del _L1_ffn_all
    return {'x': x, 'itok_B_8_3872': itok_B_8_3872, 'itok_B_2_6': itok_B_2_6, 'L0_cond_log_dt': _L0_cond_in['log_dt'], 'L0_cond_C': _L0_cond_in['C'], 'L0_cond_log_A_real': _L0_cond_in['log_A_real'], 'L0_cond_A_imag': _L0_cond_in['A_imag'], 'L0_cond_D': _L0_cond_in['D'], 'L0_ffn_weight': _L0_ffn_in['weight'], 'L0_ffn_lora_A': _L0_ffn_in['lora_A'], 'L0_ffn_lora_B': _L0_ffn_in['lora_B'], 'L0_ffn_gw1': _L0_ffn_in['gw1'], 'L0_ffn_gb1': _L0_ffn_in['gb1'], 'L0_ffn_ln_gamma': _L0_ffn_in['ln_gamma'], 'L0_ffn_ln_beta': _L0_ffn_in['ln_beta'], 'L0_ffn_gw2': _L0_ffn_in['gw2'], 'L0_ffn_gb2': _L0_ffn_in['gb2'], 'L1_cond_W_gate': _L1_cond_in['W_gate'], 'L1_cond_W_up': _L1_cond_in['W_up'], 'L1_cond_W_down': _L1_cond_in['W_down'], 'L1_cond_A_gate': _L1_cond_in['A_gate'], 'L1_cond_B_gate': _L1_cond_in['B_gate'], 'L1_cond_A_up': _L1_cond_in['A_up'], 'L1_cond_B_up': _L1_cond_in['B_up'], 'L1_cond_A_down': _L1_cond_in['A_down'], 'L1_cond_B_down': _L1_cond_in['B_down'], 'L1_ffn_gate_w': _L1_ffn_in['gate_w'], 'L1_ffn_w_gate_up': _L1_ffn_in['w_gate_up'], 'L1_ffn_w_down': _L1_ffn_in['w_down'], 'L1_ffn_shared_w_gate_up': _L1_ffn_in['shared_w_gate_up'], 'L1_ffn_shared_w_down': _L1_ffn_in['shared_w_down']}

def reference(x, itok_B_8_3872, itok_B_2_6, L0_cond_log_dt, L0_cond_C, L0_cond_log_A_real, L0_cond_A_imag, L0_cond_D, L0_ffn_weight, L0_ffn_lora_A, L0_ffn_lora_B, L0_ffn_gw1, L0_ffn_gb1, L0_ffn_ln_gamma, L0_ffn_ln_beta, L0_ffn_gw2, L0_ffn_gb2, L1_cond_W_gate, L1_cond_W_up, L1_cond_W_down, L1_cond_A_gate, L1_cond_B_gate, L1_cond_A_up, L1_cond_B_up, L1_cond_A_down, L1_cond_B_down, L1_ffn_gate_w, L1_ffn_w_gate_up, L1_ffn_w_down, L1_ffn_shared_w_gate_up, L1_ffn_shared_w_down):
    import jax
    import jax.numpy as jnp

    def _L0_cond_ref(u, length, log_dt, C, log_A_real, A_imag, D):
        import math
        import jax, jax.numpy as jnp
        import numpy as np
        H, N, B, L = (32, 64, 16, 512)
        DT_MIN, DT_MAX = (0.001, 0.1)

        def _get_kernel(log_dt, C, log_A_real, A_imag, length):
            Cc = C[..., 0] + 1j * C[..., 1]
            dt = jnp.exp(log_dt)
            A = -jnp.exp(log_A_real) + 1j * A_imag
            dtA = A * dt[:, None]
            P = dtA[:, :, None] * jnp.arange(length, dtype=jnp.float32)
            Cs = Cc * (jnp.exp(dtA) - 1.0) / A
            K = 2.0 * jnp.einsum('hn,hnl->hl', Cs, jnp.exp(P)).real
            return K
        Bq, Hq, Lq = u.shape
        mask = (jnp.arange(Lq) < length[:, None]).astype(u.dtype)
        u_m = u * mask[:, None, :]
        kernel = _get_kernel(log_dt, C, log_A_real, A_imag, Lq)
        n = 2 * Lq
        k_f = jnp.fft.rfft(kernel, n=n)
        u_f = jnp.fft.rfft(u_m, n=n)
        y = jnp.fft.irfft(u_f * k_f, n=n)[..., :Lq]
        y = y + u_m * D[:, None]
        return y * mask[:, None, :]

    def _L0_ffn_ref(x, weight, lora_A, lora_B, gw1, gb1, ln_gamma, ln_beta, gw2, gb2):
        import jax, jax.numpy as jnp
        import numpy as np
        B, S, IN, OUT = (4, 256, 512, 512)
        E, K, R = (8, 2, 16)
        CAP_FACTOR = 3.0
        ALPHA = 1.0 / R
        LN_EPS = 1e-05
        orig_shape = x.shape
        xf = x.reshape(-1, orig_shape[-1])
        N = xf.shape[0]
        capacity = int(CAP_FACTOR * N / E)
        h = xf @ gw1.T + gb1
        mu = jnp.mean(h, axis=-1, keepdims=True)
        var = jnp.mean((h - mu) ** 2, axis=-1, keepdims=True)
        h = (h - mu) * jax.lax.rsqrt(var + LN_EPS) * ln_gamma + ln_beta
        h = jax.nn.relu(h)
        gates = h @ gw2.T + gb2
        top_v, top_i = jax.lax.top_k(gates, K)
        top_g = jax.nn.softmax(top_v, axis=-1)
        onehot = (top_i[..., None] == jnp.arange(E)).astype(xf.dtype)
        counts = onehot.sum(axis=0)
        allowed = (counts <= capacity).astype(xf.dtype)
        w = jnp.einsum('nke,nk,ke->ne', onehot, top_g, allowed)
        main = xf @ weight.T
        tmp = jnp.einsum('ni,eir->enr', xf, lora_A)
        tmp = tmp * w.T[:, :, None]
        lora = jnp.einsum('enr,ero->no', tmp, lora_B) * ALPHA
        out = main + lora
        return out.reshape(*orig_shape[:-1], weight.shape[0])

    def _L1_cond_ref(x, W_gate, W_up, W_down, A_gate, B_gate, A_up, B_up, A_down, B_down, lora_indices, layer_idx):
        import jax, jax.numpy as jnp
        import numpy as np
        B, N, H, F = (4, 64, 512, 1376)
        L, R, RANK = (1, 16, 16)
        SCALE = 0.5

        def lora_add(base, inp, A, B):
            Ab = A[layer_idx][lora_indices]
            Bb = B[layer_idx][lora_indices]
            t = jnp.einsum('bri,bni->bnr', Ab, inp)
            return base + jnp.einsum('bor,bnr->bno', Bb, t) * SCALE
        gate = lora_add(jnp.einsum('bnh,fh->bnf', x, W_gate), x, A_gate, B_gate)
        up = lora_add(jnp.einsum('bnh,fh->bnf', x, W_up), x, A_up, B_up)
        act = jax.nn.silu(gate) * up
        down = lora_add(jnp.einsum('bnf,hf->bnh', act, W_down), act, A_down, B_down)
        return down

    def _L1_ffn_ref(hidden_states, gate_w, w_gate_up, w_down, shared_w_gate_up, shared_w_down):
        import jax, jax.numpy as jnp
        import numpy as np
        HIDDEN = 512
        MOE_INTER = 128
        SHARED_INTER = 512
        NUM_EXPERTS = 16
        TOP_K = 2

        def _moe_forward(x, gate_w, w_gate_up, w_down, shared_w_gate_up, shared_w_down):
            orig_shape = x.shape
            x2 = x.reshape(-1, orig_shape[-1])
            gu_s = x2 @ shared_w_gate_up.T
            g_s, u_s = jnp.split(gu_s, 2, axis=-1)
            shared_out = jax.nn.silu(g_s) * u_s @ shared_w_down.T
            logits = x2 @ gate_w.T
            probs = jax.nn.softmax(logits, axis=-1)
            topk_vals, topk_idx = jax.lax.top_k(probs, TOP_K)
            topk_vals = topk_vals / jnp.sum(topk_vals, axis=-1, keepdims=True)
            combine = jnp.sum(jax.nn.one_hot(topk_idx, NUM_EXPERTS, dtype=x2.dtype) * topk_vals[..., None], axis=1)
            gu = jnp.einsum('th,eih->eti', x2, w_gate_up)
            g, u = jnp.split(gu, 2, axis=-1)
            act = jax.nn.silu(g) * u
            out_e = jnp.einsum('eti,ehi->eth', act, w_down)
            moe_out = jnp.einsum('eth,te->th', out_e, combine)
            return (moe_out + shared_out).reshape(orig_shape)
        return _moe_forward(hidden_states, gate_w, w_gate_up, w_down, shared_w_gate_up, shared_w_down)
    x = x + _L0_ffn_ref(_L0_cond_ref(x, itok_B_8_3872, L0_cond_log_dt, L0_cond_C, L0_cond_log_A_real, L0_cond_A_imag, L0_cond_D), L0_ffn_weight, L0_ffn_lora_A, L0_ffn_lora_B, L0_ffn_gw1, L0_ffn_gb1, L0_ffn_ln_gamma, L0_ffn_ln_beta, L0_ffn_gw2, L0_ffn_gb2)
    x = x + _L1_ffn_ref(_L1_cond_ref(x, L1_cond_W_gate, L1_cond_W_up, L1_cond_W_down, L1_cond_A_gate, L1_cond_B_gate, L1_cond_A_up, L1_cond_B_up, L1_cond_A_down, L1_cond_B_down, itok_B_2_6, 0), L1_ffn_gate_w, L1_ffn_w_gate_up, L1_ffn_w_down, L1_ffn_shared_w_gate_up, L1_ffn_shared_w_down)
    return x

_drawn_inputs = setup_inputs


def setup_inputs(seed=0):
    import zlib

    import numpy as np

    out = dict(_drawn_inputs(seed))
    spreads = {'L0_cond_log_A_real': (-0.6931471824645996, 0.2),
     'L0_ffn_gb1': (0.0, 0.8),
     'L0_ffn_ln_gamma': (1.0, 0.6),
     'L0_ffn_ln_beta': (0.0, 0.8),
     'L0_ffn_gb2': (0.0, 0.311)}
    factors = {'L0_ffn_lora_A': 3.199, 'L0_ffn_lora_B': 3.179, 'L0_ffn_gw1': 3.453, 'L0_ffn_gw2': 3.491}
    for name, (base, spread) in spreads.items():
        noise = np.random.default_rng([zlib.crc32(name.encode()), seed]).standard_normal(out[name].shape)
        drawn = base * np.exp(spread * noise) if base else spread * noise
        out[name] = jnp.asarray(drawn.astype(out[name].dtype))
    for name, factor in factors.items():
        out[name] = (out[name] * factor).astype(out[name].dtype)
    return out
```

```python
import concourse.bass as bass
from concourse import mybir
from contextlib import ExitStack

F32 = mybir.dt.float32
F32R = mybir.dt.float32r
I32 = mybir.dt.int32
U32 = mybir.dt.uint32
ALU = mybir.AluOpType
ACT = mybir.ActivationFunctionType
AX_X = mybir.AxisListType.X

P = 128
B, H, D = 64, 32, 512
N = B * H
DC = D // P
NS = 64
RL, QL = 32, D // 32
NT, TW = N // 512, 512
NJ = N // P
BT = TW // H
E0, R0, G0 = 8, 16, 32
CAP0 = int(3.0 * N / E0)
F = 1376
FC = -(-F // P)
NA, RA = 16, 16
AC = NA * RA // P
E1, I1, S1 = 16, 128, 512
SC = S1 // P
NB = -(-((2 * N + E1 * (P - 1)) // P) // 4) * 4
GA_W = (DC + AC) * P
ST_W = 2 * GA_W + D + NA * RA
SH_W = 2 * DC * P + D
CH = 4
NG = H // CH
W0_W = DC * D + DC * P + D
KPW = D + P

AW = H * RL + H * QL + H
FW, CW = H * RL, H * QL

LOG2E = 1.4426950408889634
MAGIC = 12582912.0
LN2_HI, LN2_LO = 0.693359375, -2.12194440e-4
TWO_PI_HI, TWO_PI_LO = 6.28125, 0.0019353071795864769
PI_DOWN = 3.1415925


def conditioned_blocks(nc, x_heads, log_dt, s4_par, s4_d, lens, adapters, w0, gw1, gb1_d, lng_d, lnb_d,
                       gw2, gb2_d, w_la, w_st, w_bd, w_sh, gw_d, w_eg, w_ed, out):
    ctx = ExitStack()
    with ctx:
        def sem(name):
            return ctx.enter_context(nc.semaphore(name))

        base = -(-nc.sbuf_base // 32) * 32
        ctx.enter_context(nc.sbuf_tensor("arena", [P, 206 * 256], F32))

        def at(name, kb, cols, dt=F32):
            return nc.alloc_sbuf_tensor_at(name, [P, cols], dt, offset=base + int(kb * 1024))

        bank = [ctx.enter_context(nc.psum_tensor(f"bank{i}", [P, 512], F32)) for i in range(8)]

        ident = at("ident", 0, P)
        ones = at("ones", 0.5, P)
        before = at("before", 1, P)
        e_iota = at("e_iota", 1.5, E1)
        mask_len = at("mask_len", 1.75, DC * B)
        mask_ad = at("mask_ad", 2.75, AC * B)
        slot_u = at("slot_u", 3.25, 2 * NJ, U32)
        gate1 = at("gate1", 3.375, 2 * NJ)
        blk_e = at("blk_e", 3.5, NB, I32)
        tok_id = at("tok_id", 3.75, NJ, U32)
        slot_tok = at("slot_tok", 3.875, NB, U32)
        gwT = at("gwT", 4.25, DC * E1)
        gw1T = at("gw1T", 4.5, DC * G0)
        gb1 = at("gb1", 5, G0)
        lng = at("lng", 5.125, G0)
        lnb = at("lnb", 5.25, G0)
        gb2 = at("gb2", 5.375, E0)
        gw2bd = at("gw2bd", 5.5, 4 * E0)
        b_iota = at("b_iota", 5.75, NB)
        list_u = at("list_u", 6, 2 * NJ, U32)
        slot_b = at("slot_b", 6.125, 2 * NJ, U32)
        slot_bf = at("slot_bf", 6.25, 2 * NJ)
        xT = at("xT", 8, NG * DC * CH * B)
        yT = at("yT", 40, DC * N)
        y_hi = at("y_hi", 72, DC * TW, F32R)
        y_lo = at("y_lo", 80, DC * TW, F32R)
        toep = at("toep", 88, 2 * CH * D)
        w0_hi = at("w0_hi", 104, W0_W, F32R)
        w0_lo = at("w0_lo", 116, W0_W, F32R)
        w0_raw = at("w0_raw", 128, W0_W)
        lg = at("lg", 140, 2 * H)
        ai = at("ai", 140.25, H)
        cr = at("cr", 140.375, H)
        ci = at("ci", 140.5, H)
        sm = at("sm", 141, 24 * 2 * H)
        kx = at("kx", 147, 2 * H, I32)
        len_i = at("len_i", 147.25, B, I32)
        ad_i = at("ad_i", 147.5, B, I32)
        len_f = at("len_f", 147.75, B)
        ad_f = at("ad_f", 148, B)
        l_iota = at("l_iota", 148.25, DC)
        a_iota = at("a_iota", 148.3125, AC)
        a_int = at("a_int", 148.375, AC, I32)
        r_iota = at("r_iota", 148.5, RL)
        q_iota = at("q_iota", 148.625, QL)
        ang = at("ang", 149, AW)
        turn = at("turn", 155.25, AW)
        dec = at("dec", 161.5, FW + CW)
        sn = at("sn", 167.5, AW)
        sh = at("sh", 173.75, CW + H)
        coarse = at("coarse", 176, CW)
        coarse_b = at("coarse_b", 178, CW)
        uu = at("uu", 180, H)
        vv = at("vv", 180.125, H)
        k_sb = at("k_sb", 181, H * RL)
        d_pad = at("d_pad", 185, H * RL)
        d_row = at("d_row", 189, H)
        q_last = at("q_last", 189.125, QL)
        zeros = at("zeros", 189.25, P)
        phase = at("phase", 189.75, 2)
        hh = at("hh", 140, NJ * G0)
        hq = at("hq", 142, NJ * G0)
        hT = at("hT", 144, 4 * P)
        rs = at("rs", 146, 8 * NJ)
        ga = at("ga", 146.5, NJ * E0)
        mv = at("mv", 147, NJ * 8)
        mi = at("mi", 147.5, NJ * 8, U32)
        i2 = at("i2", 148, 2 * NJ)
        oh = at("oh", 148.125, 2 * NJ * E0)
        wk = at("wk", 149.125, 2 * NJ * E0)
        cn = at("cn", 150.125, 2 * E0)
        w_te = at("w_te", 150.25, NJ * E0)
        w_exp = at("w_exp", 190, NJ * E0 * R0)
        wT = at("wT", 152, N)
        t_f = at("t_f", 160, TW)
        t_hi = at("t_hi", 162, TW, F32R)
        t_lo = at("t_lo", 164, TW, F32R)
        x1_t = at("x1_t", 166, DC * TW)
        x1_tok = at("x1_tok", 88, 4 * D)
        x1T = at("x1T", 174, NT * DC * TW)
        cT = at("cT", 8, NT * DC * TW)
        x_hi = at("x_hi", 40, DC * TW, F32R)
        x_lo = at("x_lo", 48, DC * TW, F32R)
        act_hi = at("act_hi", 56, 2 * TW, F32R)
        act_lo = at("act_lo", 60, 2 * TW, F32R)
        silu_s = at("silu_s", 64, TW)
        prod_s = at("prod_s", 66, TW)
        ta_f = at("ta_f", 68, TW)
        st_hi = at("st_hi", 70, 2 * ST_W, F32R)
        st_lo = at("st_lo", 88, 2 * ST_W, F32R)
        st_raw = at("st_raw", 106, 2 * ST_W)
        td_lo = at("td_lo", 124, AC * TW, F32R)
        la_hi = at("la_hi", 128, DC * 2 * AC * P, F32R)
        la_raw = at("la_raw", 136, DC * 2 * AC * P)
        bd_hi = at("bd_hi", 136, AC * D, F32R)
        bd_lo = at("bd_lo", 140, AC * D, F32R)
        la_lo = at("la_lo", 144, DC * 2 * AC * P, F32R)
        ta_hi = at("ta_hi", 152, 2 * AC * TW, F32R)
        ta_lo = at("ta_lo", 160, 2 * AC * TW, F32R)
        td_hi = at("td_hi", 168, AC * TW, F32R)
        bd_raw = at("bd_raw", 168, AC * D)
        sw_hi = at("sw_hi", 70, 2 * SH_W, F32R)
        sw_lo = at("sw_lo", 82, 2 * SH_W, F32R)
        sw_raw = at("sw_raw", 94, 2 * SH_W)
        eg = at("eg", 106, E1 * DC * 2 * I1)
        ed = at("ed", 170, E1 * D)
        lgt = at("lgt", 170, NJ * E1)
        mv1 = at("mv1", 171, NJ * 8)
        mi1 = at("mi1", 171.5, NJ * 8, U32)
        j2 = at("j2", 172, 2 * NJ)
        dl = at("dl", 172.125, 2 * NJ)
        oh1 = at("oh1", 172.5, 2 * NJ * E1)
        ohs = at("ohs", 174.5, NJ * E1)
        sc_a = at("sc_a", 175.5, NJ * E1)
        sc_b = at("sc_b", 176.5, NJ * E1)
        pos1 = at("pos1", 177.5, NJ * E1)
        tot1 = at("tot1", 178.5, NJ * E1)
        ohp = at("ohp", 179.5, 2 * NJ * E1)
        nbk = at("nbk", 181.5, 8 * E1)
        nbi = at("nbi", 182, E1, I32)
        bcmp = at("bcmp", 182.25, NB * E1)
        ebf = at("ebf", 185.5, NB)
        slf = at("slf", 185.75, 2 * NJ)
        c_tok = at("c_tok", 190, 4 * D)
        xg = at("xg", 40, 4 * D)
        xgT = at("xgT", 48, 4 * DC * P)
        es = at("es", 56, 4 * I1)
        eh = at("eh", 58, 4 * I1)
        ehT = at("ehT", 60, 4 * P)
        ys = at("ys", 62, 4 * D)
        y1 = at("y1", 72, 4 * D)
        y2 = at("y2", 80, 4 * D)
        fin = at("fin", 88, 4 * D)

        kpad = nc.dram_tensor("kpad", (H, KPW), F32, kind="Internal").ap()
        x1_dram = nc.dram_tensor("x1_dram", (N, D), F32, kind="Internal").ap()
        c_dram = nc.dram_tensor("c_dram", (N, D), F32, kind="Internal").ap()
        y_dram = nc.dram_tensor("y_dram", (NB * P, D), F32, kind="Internal").ap()
        st_dram = nc.dram_tensor("st_dram", (NB * P, 1), U32, kind="Internal").ap()

        s4_in = sem("s4_in")
        small_in = sem("small_in")
        x_in = sem("x_in")
        w0_in = sem("w0_in")
        kpad_out = sem("kpad_out")
        toep_in = [sem(f"toep_in{i}") for i in range(2)]
        x1_out = [sem(f"x1_out{i}") for i in range(4)]
        la_in = sem("la_in")
        bd_in = sem("bd_in")
        st_in = [sem(f"st_in{i}") for i in range(2)]
        c_out = [sem(f"c_out{i}") for i in range(4)]
        sw_in = [sem(f"sw_in{i}") for i in range(2)]
        x1_in = sem("x1_in")
        eg_in = sem("eg_in")
        ed_in = sem("ed_in")
        list_zero = sem("list_zero")
        list_out = sem("list_out")
        list_in = sem("list_in")
        xg_in = [sem(f"xg_in{i}") for i in range(4)]
        y_out = [sem(f"y_out{i}") for i in range(4)]
        y1_in = [sem(f"y1_in{i}") for i in range(4)]
        y2_in = [sem(f"y2_in{i}") for i in range(4)]
        fin_out = [sem(f"fin_out{i}") for i in range(4)]
        dve_step = sem("dve_step")
        pool_step = sem("pool_step")
        act_step = sem("act_step")
        iota_done = sem("iota_done")
        a_ready = sem("a_ready")
        ang_ready = sem("ang_ready")
        tanh_done = sem("tanh_done")
        dec_mul = sem("dec_mul")
        dec_done = sem("dec_done")
        sin_done = sem("sin_done")
        table_done = sem("table_done")
        d_done = sem("d_done")
        k_ready = sem("k_ready")
        k_evac = sem("k_evac")
        const_done = sem("const_done")
        conv_done = sem("conv_done")
        conv_free = sem("conv_free")
        w0_split = sem("w0_split")
        w0_hi_done = sem("w0_hi_done")
        h_ready = sem("h_ready")
        var_done = sem("var_done")
        sqrt_done = sem("sqrt_done")
        h_norm = sem("h_norm")
        hT_ready = sem("hT_ready")
        hT_evac = sem("hT_evac")
        g_ready = sem("g_ready")
        oh_ready = sem("oh_ready")
        cnt_ready = sem("cnt_ready")
        dl_ready = sem("dl_ready")
        th_ready = sem("th_ready")
        w_ready = sem("w_ready")
        wexp_done = sem("wexp_done")
        wT_ready = sem("wT_ready")
        wT_evac = sem("wT_evac")
        yhi_done = sem("yhi_done")
        ysplit = sem("ysplit")
        y_used = sem("y_used")
        t_ready = sem("t_ready")
        tf_done = sem("tf_done")
        thi_done = sem("thi_done")
        tsplit = sem("tsplit")
        x1_ready = sem("x1_ready")
        x1t_done = sem("x1t_done")
        x1t_copied = sem("x1t_copied")
        x1tok_ready = sem("x1tok_ready")
        x1tok_evac = sem("x1tok_evac")
        la_hi_done = sem("la_hi_done")
        la_split = sem("la_split")
        bd_hi_done = sem("bd_hi_done")
        bd_split = sem("bd_split")
        xhi_done = sem("xhi_done")
        xsplit = sem("xsplit")
        ta_ready = sem("ta_ready")
        taf_done = sem("taf_done")
        tahi_done = sem("tahi_done")
        ta_split = sem("ta_split")
        st_hi_done = sem("st_hi_done")
        st_split = sem("st_split")
        st_used = sem("st_used")
        gate_ready = sem("gate_ready")
        silu_done = sem("silu_done")
        up_ready = sem("up_ready")
        prod_done = sem("prod_done")
        acthi_done = sem("acthi_done")
        act_split = sem("act_split")
        td_ready = sem("td_ready")
        c_ready = sem("c_ready")
        c_evac = sem("c_evac")
        lgt_ready = sem("lgt_ready")
        ctok_ready = sem("ctok_ready")
        ctok_evac = sem("ctok_evac")
        ohs_ready = sem("ohs_ready")
        pos_ready = sem("pos_ready")
        dl1_ready = sem("dl1_ready")
        th1_ready = sem("th1_ready")
        slots_ready = sem("slots_ready")
        blk_ready = sem("blk_ready")
        chi_done = sem("chi_done")
        csplit = sem("csplit")
        sw_hi_done = sem("sw_hi_done")
        sw_split = sem("sw_split")
        sgate_ready = sem("sgate_ready")
        ssilu_done = sem("ssilu_done")
        sup_ready = sem("sup_ready")
        sprod_done = sem("sprod_done")
        sacthi_done = sem("sacthi_done")
        sact_split = sem("sact_split")
        base_ready = sem("base_ready")
        base_done = sem("base_done")
        xgT_ready = sem("xgT_ready")
        xgT_evac = sem("xgT_evac")
        egu_ready = sem("egu_ready")
        es_done = sem("es_done")
        eh_done = sem("eh_done")
        ehT_ready = sem("ehT_ready")
        ehT_evac = sem("ehT_evac")
        ey_ready = sem("ey_ready")
        ys_done = sem("ys_done")
        fma1_done = sem("fma1_done")
        fma2_done = sem("fma2_done")

        S4_LOADS, SMALL_LOADS = 12, 10
        LQ = 3 * AC
        TANH, AR, DT, BR, T0, T1, T2, EM, SR, SI, IA, KF, RR, PP, CB, QR, QI = range(17)
        SD, VAR, TH, DL, MU, RC, T3 = range(7)

        def smv(i, w=H):
            return sm[:, 2 * H * i:2 * H * i + w]

        def rsv(i):
            return rs[:, NJ * i:NJ * (i + 1)]

        def fine(tile):
            return tile[:, 0:FW].rearrange("p (h r) -> p h r", h=H)

        def crs(tile, at0=0):
            return tile[:, at0:at0 + CW].rearrange("p (h q) -> p h q", h=H)

        def over_lags(col, n):
            return col.unsqueeze(2).broadcast_to([P, H, n])

        def over_heads(col):
            return col.unsqueeze(1).broadcast_to([P, H, col.shape[1]])
        GU, SGU = 2 * GA_W, 2 * DC * P

        CREDITS = {conv_free: 4, conv_done: 4, y_used: 1, tf_done: 1, x1t_done: 4, x1t_copied: 4, x1tok_ready: 1,
                   x1tok_evac: 2, up_ready: 1, silu_done: 1, prod_done: 1, c_evac: 4, st_split: 4, st_used: 2,
                   sup_ready: 1, ssilu_done: 1, sprod_done: 1, base_done: 4, sw_split: 4,
                   xgT_evac: 2, eh_done: 2, ehT_evac: 1, ys_done: 2}
        CREDITS.update({s: 16 for s in x1_out + y_out})

        block = ctx.enter_context(nc.Block())

        @block.sync
        def _(sp):
            sp.dma_start(lg[:, 0:H], log_dt.partition_broadcast(P)).then_inc(s4_in, 16)
            for half in (0, NS):
                sp.dma_start(lg[half:half + NS, H:2 * H], s4_par[0]).then_inc(s4_in, 16)
                sp.dma_start(ai[half:half + NS, :], s4_par[1]).then_inc(s4_in, 16)
                sp.dma_start(cr[half:half + NS, :], s4_par[2]).then_inc(s4_in, 16)
                sp.dma_start(ci[half:half + NS, :], s4_par[3]).then_inc(s4_in, 16)
            sp.dma_start(d_row[0:1, :], s4_d.unsqueeze(0)).then_inc(s4_in, 16)
            sp.dma_start(len_i[:, :], lens.partition_broadcast(P)).then_inc(s4_in, 16)
            sp.dma_start(ad_i[:, :], adapters.partition_broadcast(P)).then_inc(s4_in, 16)
            for g in range(NG):
                sp.dma_start(xT[:, g * DC * CH * B:(g + 1) * DC * CH * B], x_heads[g]).then_inc(x_in, 16)
            sp.dma_start(w0_raw[:, :], w0).then_inc(w0_in, 16)
            sp.dma_start(gw1T[:, :], gw1).then_inc(small_in, 16)
            sp.dma_start(gwT[:, :], gw_d).then_inc(small_in, 16)
            sp.dma_start(gb1[:, :], gb1_d.partition_broadcast(P)).then_inc(small_in, 16)
            sp.dma_start(lng[:, :], lng_d.partition_broadcast(P)).then_inc(small_in, 16)
            sp.dma_start(lnb[:, :], lnb_d.partition_broadcast(P)).then_inc(small_in, 16)
            sp.dma_start(gb2[:, :], gb2_d.partition_broadcast(P)).then_inc(small_in, 16)
            sp.wait_ge(const_done, 3)
            for i in range(4):
                sp.dma_start(gw2bd[G0 * i:G0 * (i + 1), E0 * i:E0 * (i + 1)], gw2).then_inc(small_in, 16)
            sp.dma_start(kpad[:, D:KPW], zeros[0:H, :]).then_inc(kpad_out, 16)
            sp.dma_start(st_dram.rearrange("(p b) o -> p (b o)", p=P), zeros[:, 0:NB].bitcast(U32)).then_inc(list_zero, 16)

            sp.wait_ge(k_evac, 2)
            sp.dma_start(kpad[:, 0:D].rearrange("h (q r) -> q h r", q=QL),
                         k_sb[0:QL, :].rearrange("q (h r) -> q h r", h=H)).then_inc(kpad_out, 16)
            sp.wait_ge(kpad_out, 32)
            with sp.Fori(0, NG // 2) as it:
                for u in range(2):
                    sp.wait_ge(conv_done, it * 4 + (2 * u + 2))
                    sp.dma_start(toep[:, u * CH * D:(u + 1) * CH * D].rearrange("p (h i) -> p h i", h=CH),
                                 bass.AP(kpad.tensor, (it * 2 + u) * (CH * KPW), [[1, P], [KPW, CH], [1, D]])
                                 ).then_inc(toep_in[u], 16)
            sp.wait_ge(wT_evac, 4)
            sp.wait_ge(w0_split, 1)
            sp.dma_start(la_raw[:, :], w_la).then_inc(la_in, 16)
            sp.wait_ge(x1_ready, 4 * NT)
            for q in x1_out:
                sp.wait_ge(q, 16 * NT + 16)
            with sp.Fori(0, NT // 2) as it:
                for s in range(2 * FC):
                    b = s % 2
                    sp.wait_ge(st_split, it * 4 * FC + (2 * s + 2))
                    sp.dma_start(st_raw[:, b * ST_W:(b + 1) * ST_W], w_st[s % FC]).then_inc(st_in[b], 16)
            sp.wait_ge(st_used, NT * FC + 2)
            with sp.Fori(0, NT // 2) as it:
                for s in range(2 * SC):
                    b = s % 2
                    sp.wait_ge(sw_split, it * 4 * SC + (2 * s + 2))
                    sp.dma_start(sw_raw[:, b * SH_W:(b + 1) * SH_W], w_sh[s % SC]).then_inc(sw_in[b], 16)
                    if s % SC == 2:
                        sp.wait_ge(csplit, it * 2 * DC + (s // SC + 1) * DC)
                        sp.dma_start(cT[:, bass.ds((it * 2 + s // SC) * (DC * TW), DC * TW)]
                                     .rearrange("p (s d) -> p s d", s=4),
                                     x1_dram[bass.ds((it * 2 + s // SC) * TW, TW), :]
                                     .rearrange("(s p) d -> p s d", p=P)).then_inc(x1_in, 16)
            with sp.Fori(0, NB // 4) as it:
                for u in range(4):
                    sp.wait_ge(ys_done, it * 4 + (u + 3))
                    sp.dma_start(y_dram[bass.ds((it * 4 + u) * P, P), :], ys[:, u * D:(u + 1) * D]).then_inc(y_out[u], 16)
            for j in range(NJ):
                sp.wait_ge(fma2_done, j + 1)
                sp.dma_start(out[j * P:(j + 1) * P, :], fin[:, (j % 4) * D:(j % 4 + 1) * D]).then_inc(fin_out[j % 4], 16)
            for u in range(4):
                sp.wait_ge(fin_out[u], 16 * NJ // 4)

        @block.gpsimd
        def _(pool):
            g = nc.gpsimd
            allow = dict(allow_small_or_imprecise_dtypes=True)
            for s, n in CREDITS.items():
                pool.sem_inc(s, n)
            count = [0]

            def link(ins):
                count[0] += 1
                ins.then_inc(pool_step, 1)
                pool.wait_ge(pool_step, count[0])

            g.iota(r_iota[:, :], pattern=[[-1, RL]], base=RL - 1, channel_multiplier=0, **allow).then_inc(iota_done, 1)
            g.iota(q_iota[:, :], pattern=[[-RL, QL]], base=RL * (QL - 1), channel_multiplier=0, **allow).then_inc(iota_done, 1)
            g.iota(l_iota[:, :], pattern=[[P, DC]], base=P - 1, channel_multiplier=-1, **allow).then_inc(iota_done, 1)
            g.iota(a_int[:, :], pattern=[[P, AC]], base=0, channel_multiplier=1).then_inc(iota_done, 1)
            pool.wait_ge(iota_done, 4)
            link(g.memset(phase[:, :], 0.0))
            link(g.memset(phase[0:NS, 0:1], 0.25))
            g.memset(phase[0:NS, 1:2], 1.5707963267948966).then_inc(iota_done, 1)
            pool.wait_ge(iota_done, 5)
            link(g.memset(d_pad[0:1, :], 0.0))
            link(g.memset(q_last[0:1, :], 0.0))
            link(g.memset(q_last[0:1, QL - 1:QL], 1.0))
            pool.wait_ge(s4_in, 16 * S4_LOADS)
            g.tensor_copy(d_pad[0:1, :].rearrange("p (h r) -> p h r", h=H)[:, :, RL - 1], d_row[0:1, :]).then_inc(d_done, 1)
            link(g.memset(gw2bd[:, :], 0.0))
            pool.sem_inc(const_done, 1)
            link(g.memset(zeros[:, :], 0.0))
            pool.sem_inc(const_done, 2)
            link(g.memset(ident[:, :], 0.0))
            link(g.affine_select(out=ident[:, :], in_=ident[:, :], compare_op=ALU.not_equal, fill=1.0, base=0,
                                 pattern=[[-1, P]], channel_multiplier=1))
            link(g.memset(ones[:, :], 1.0))
            link(g.affine_select(out=before[:, :], in_=ones[:, :], compare_op=ALU.is_gt, fill=0.0, base=0,
                                 pattern=[[1, P]], channel_multiplier=-1))
            link(g.iota(e_iota[:, :], pattern=[[1, E1]], base=0, channel_multiplier=0, **allow))
            link(g.iota(b_iota[:, :], pattern=[[1, NB]], base=0, channel_multiplier=0, **allow))
            link(g.iota(tok_id[:, :], pattern=[[P, NJ]], base=0, channel_multiplier=1))
            pool.sem_inc(const_done, 1)

            pool.wait_ge(w_ready, 1)
            g.tensor_copy(w_exp[:, :].rearrange("p (j r) -> p j r", r=R0),
                          w_te[:, :].unsqueeze(2).broadcast_to([P, NJ * E0, R0])).then_inc(wexp_done, 1)

            pool.wait_ge(c_ready, 4 * NT)
            g.dma_start(eg[:, :], w_eg).then_inc(eg_in, 16)
            pool.wait_ge(slots_ready, 1)
            pool.wait_ge(list_zero, 16)
            for k in range(2):
                for j in range(NJ):
                    g.indirect_dma_start(out=st_dram, out_offset=bass.IndirectOffsetOnAxis(list_u[:, k * NJ + j:k * NJ + j + 1], 0),
                                         in_=tok_id[:, j:j + 1], in_offset=None,
                                         bounds_check=NB * P - 1).then_inc(list_out, 16)
            pool.wait_ge(list_out, 32 * NJ)
            g.dma_start(slot_tok[:, :], st_dram.rearrange("(p b) o -> p (b o)", p=P)).then_inc(list_in, 16)
            pool.wait_ge(blk_ready, 1)
            for q in c_out:
                pool.wait_ge(q, 16 * NJ // 4)
            g.dma_start(ed[:, :], w_ed).then_inc(ed_in, 16)
            pool.wait_ge(list_in, 16)
            pool.wait_ge(base_done, NJ + 4)
            for b in range(NB):
                if b >= 4:
                    pool.wait_ge(xgT_ready, b - 3)
                g.indirect_dma_start(out=xg[:, (b % 4) * D:(b % 4 + 1) * D], out_offset=None, in_=c_dram,
                                     in_offset=bass.IndirectOffsetOnAxis(slot_tok[:, b:b + 1], 0),
                                     bounds_check=N - 1).then_inc(xg_in[b % 4], 16)
            for q in y_out:
                pool.wait_ge(q, 16 * (NB // 4 + 1))
            for j in range(NJ):
                u = j % 4
                if j >= 4:
                    pool.wait_ge(fma1_done, j - 3)
                g.indirect_dma_start(out=y1[:, u * D:(u + 1) * D], out_offset=None, in_=y_dram,
                                     in_offset=bass.IndirectOffsetOnAxis(slot_u[:, j:j + 1], 0),
                                     bounds_check=NB * P - 1).then_inc(y1_in[u], 16)
                if j >= 4:
                    pool.wait_ge(fma2_done, j - 3)
                g.indirect_dma_start(out=y2[:, u * D:(u + 1) * D], out_offset=None, in_=y_dram,
                                     in_offset=bass.IndirectOffsetOnAxis(slot_u[:, NJ + j:NJ + j + 1], 0),
                                     bounds_check=NB * P - 1).then_inc(y2_in[u], 16)

        @block.scalar
        def _(act):
            a = nc.scalar
            act.wait_ge(a_ready, 1)
            a.activation(smv(TANH), smv(AR), ACT.Tanh, scale=0.5).then_inc(tanh_done, 1)
            act.wait_ge(dec_mul, 1)
            a.activation(dec[:, :], dec[:, :], ACT.Exp).then_inc(dec_done, 1)
            act.wait_ge(ang_ready, 1)
            a.activation(sn[:, :], ang[:, :], ACT.Sin).then_inc(sin_done, 1)
            a.activation(sh[:, :], ang[:, FW:AW], ACT.Sin, scale=0.5).then_inc(sin_done, 1)
            act.wait_ge(w0_in, 16)
            a.copy(w0_hi[:, :], w0_raw[:, :]).then_inc(w0_hi_done, 1)
            act.wait_ge(var_done, 1)
            a.activation(rsv(SD), rsv(VAR), ACT.Sqrt).then_inc(sqrt_done, 1)
            act.wait_ge(dl_ready, 1)
            a.activation(rsv(TH), rsv(DL), ACT.Tanh, scale=0.5).then_inc(th_ready, 1)
            for i in range(4):
                act.wait_ge(wT_ready, i + 1)
                a.copy(wT[:, i * TW:(i + 1) * TW], bank[4 + i][:, :]).then_inc(wT_evac, 1)

            with act.Fori(0, NT) as t:
                act.wait_ge(y_used, t + 1)
                for c in range(DC):
                    a.copy(y_hi[:, c * TW:(c + 1) * TW], yT[:, bass.ds(t * TW + c * N, TW)]).then_inc(yhi_done, 1)
                act.wait_ge(tf_done, t + 2)
                a.copy(t_hi[:, :], t_f[:, :]).then_inc(thi_done, 1)
                for m in range(DC):
                    act.wait_ge(x1t_done, t * 4 + (m + 5))
                    a.copy(x1T[:, bass.ds(t * (DC * TW) + m * TW, TW)], x1_t[:, m * TW:(m + 1) * TW]).then_inc(x1t_copied, 1)
                for s in range(4):
                    act.wait_ge(x1tok_ready, t * 4 + (s + 2))
                    act.wait_ge(x1_out[s], t * 16 + 16)
                    a.copy(x1_tok[:, s * D:(s + 1) * D], bank[6 + s % 2][:, :]).then_inc(x1tok_evac, 1)
                    act.wait_ge(x1tok_evac, t * 4 + (s + 3))
                    act.dma_start(x1_dram[bass.ds(t * TW + s * P, P), :], x1_tok[:, s * D:(s + 1) * D]).then_inc(x1_out[s], 16)

            act.wait_ge(la_in, 16)
            act.wait_ge(x1_ready, 4 * NT)
            a.copy(la_hi[:, :], la_raw[:, :]).then_inc(la_hi_done, 1)
            act.wait_ge(x1tok_ready, 4 * NT + 1)
            act.wait_ge(x1t_copied, 4 * NT + 4)
            act.dma_start(bd_raw[:, :], w_bd).then_inc(bd_in, 16)

            act.wait_ge(bd_in, 16)
            act.wait_ge(la_split, 1)
            a.copy(bd_hi[:, :], bd_raw[:, :]).then_inc(bd_hi_done, 1)

            def down_lora_hi(it, u):
                for q in range(AC):
                    act.wait_ge(taf_done, it * (2 * LQ) + (LQ * u + 2 * AC + q + 1))
                    a.copy(td_hi[:, q * TW:(q + 1) * TW], ta_f[:, :]).then_inc(tahi_done, 1)

            def evac_c(it, u):
                for m in range(DC):
                    act.wait_ge(c_ready, it * (2 * DC) + (u * DC + m + 1))
                    a.copy(cT[:, bass.ds((it * 2 + u) * (DC * TW) + m * TW, TW)], bank[m][:, :]).then_inc(c_evac, 1)

            def split_x(t):
                for c in range(DC):
                    a.copy(x_hi[:, c * TW:(c + 1) * TW], x1T[:, bass.ds(t * (DC * TW) + c * TW, TW)]).then_inc(xhi_done, 1)

            def hi_gate_up(it, s):
                b = s % 2
                act.wait_ge(st_in[b], it * (16 * FC) + 16 * (s // 2 + 1))
                act.wait_ge(up_ready, it * (2 * FC) + max(s, 1))
                a.copy(st_hi[:, b * ST_W:b * ST_W + GU], st_raw[:, b * ST_W:b * ST_W + GU]).then_inc(st_hi_done, 1)

            with act.Fori(0, NT // 2) as it:
                hi_gate_up(it, 0)
                for u in range(2):
                    t = it * 2 + u
                    act.wait_ge(up_ready, it * (2 * FC) + (u * FC + 1))
                    split_x(t)
                    if u == 1:
                        down_lora_hi(it, 0)
                        evac_c(it, 0)
                    for q in range(2 * AC):
                        act.wait_ge(taf_done, it * (2 * LQ) + (LQ * u + q + 1))
                        a.copy(ta_hi[:, q * TW:(q + 1) * TW], ta_f[:, :]).then_inc(tahi_done, 1)
                    for f in range(FC):
                        s = u * FC + f
                        b = s % 2
                        act.wait_ge(st_used, it * (2 * FC) + (s + 1))
                        a.copy(st_hi[:, b * ST_W + GU:(b + 1) * ST_W],
                               st_raw[:, b * ST_W + GU:(b + 1) * ST_W]).then_inc(st_hi_done, 1)
                        act.wait_ge(gate_ready, it * (2 * FC) + (s + 1))
                        act.wait_ge(prod_done, it * (2 * FC) + (s + 1))
                        a.activation(silu_s[:, :], bank[6][:, :], ACT.Silu).then_inc(silu_done, 1)
                        if s + 1 < 2 * FC:
                            hi_gate_up(it, s + 1)
                        act.wait_ge(prod_done, it * (2 * FC) + (s + 2))
                        a.copy(act_hi[:, b * TW:(b + 1) * TW], prod_s[:, :]).then_inc(acthi_done, 1)
                down_lora_hi(it, 1)
                evac_c(it, 1)

            for j in range(NJ):
                u = j % 4
                act.wait_ge(ctok_ready, j + 1)
                if j >= 4:
                    act.wait_ge(c_out[u], 16 * (j // 4))
                a.copy(c_tok[:, u * D:(u + 1) * D], bank[j % 6][:, :]).then_inc(ctok_evac, 1)
                act.wait_ge(ctok_evac, j + 1)
                act.dma_start(c_dram[j * P:(j + 1) * P, :], c_tok[:, u * D:(u + 1) * D]).then_inc(c_out[u], 16)
            act.wait_ge(dl1_ready, 1)
            a.activation(dl[:, NJ:2 * NJ], dl[:, 0:NJ], ACT.Tanh, scale=0.5).then_inc(th1_ready, 1)

            def shared_hi_gate_up(it, s):
                b = s % 2
                act.wait_ge(sw_in[b], it * (16 * SC) + 16 * (s // 2 + 1))
                act.wait_ge(sup_ready, it * (2 * SC) + max(s, 1))
                a.copy(sw_hi[:, b * SH_W:b * SH_W + SGU], sw_raw[:, b * SH_W:b * SH_W + SGU]).then_inc(sw_hi_done, 1)

            with act.Fori(0, NT // 2) as it:
                shared_hi_gate_up(it, 0)
                for u in range(2):
                    t = it * 2 + u
                    act.wait_ge(sup_ready, it * (2 * SC) + (u * SC + 1))
                    for c in range(DC):
                        a.copy(x_hi[:, c * TW:(c + 1) * TW], cT[:, bass.ds(t * (DC * TW) + c * TW, TW)]).then_inc(chi_done, 1)
                    for i in range(SC):
                        s = u * SC + i
                        b = s % 2
                        act.wait_ge(sgate_ready, it * (2 * SC) + (s + 1))
                        act.wait_ge(sprod_done, it * (2 * SC) + (s + 1))
                        a.activation(silu_s[:, :], bank[4][:, :], ACT.Silu).then_inc(ssilu_done, 1)
                        a.copy(sw_hi[:, b * SH_W + SGU:(b + 1) * SH_W],
                               sw_raw[:, b * SH_W + SGU:(b + 1) * SH_W]).then_inc(sw_hi_done, 1)
                        if s + 1 < 2 * SC:
                            shared_hi_gate_up(it, s + 1)
                        act.wait_ge(sprod_done, it * (2 * SC) + (s + 2))
                        a.copy(act_hi[:, b * TW:(b + 1) * TW], prod_s[:, :]).then_inc(sacthi_done, 1)

            def evac_x(b4, u, k):
                act.wait_ge(xgT_ready, b4 + (u + 1))
                a.copy(xgT[:, (u % 4) * D:(u % 4 + 1) * D], bank[u % 2][:, :]).then_inc(xgT_evac, 1)

            def silu_e(b4, u):
                act.wait_ge(egu_ready, b4 + (u + 1))
                a.activation(es[:, (u % 4) * I1:(u % 4 + 1) * I1], bank[2 + u % 2][:, 0:I1], ACT.Silu).then_inc(es_done, 1)

            evac_x(0, 0, 0)
            evac_x(0, 1, 0)
            silu_e(0, 0)
            with act.Fori(0, NB // 4 - 1) as it:
                for u in range(4):
                    evac_x(it * 4, u + 2, 1)
                    silu_e(it * 4, u + 1)
            for u in range(4):
                if u < 2:
                    evac_x(NB - 4, u + 2, 1)
                if u < 3:
                    silu_e(NB - 4, u + 1)

        @block.vector
        def _(dve):
            v = nc.vector
            count = [0]

            def link(ins):
                count[0] += 1
                ins.then_inc(dve_step, 1)
                dve.wait_ge(dve_step, count[0])

            W = 2 * H
            dve.wait_ge(s4_in, 16 * S4_LOADS)
            kf, rr, pp = smv(KF, W), smv(RR, W), smv(PP, W)
            link(v.tensor_scalar(kf, lg[:, :], LOG2E, MAGIC, ALU.mult, ALU.add))
            link(v.tensor_scalar(kf, kf, -MAGIC, -126.0, ALU.add, ALU.max))
            link(v.scalar_tensor_tensor(out=rr, in0=kf, scalar=-LN2_HI, in1=lg[:, :], op0=ALU.mult, op1=ALU.add))
            link(v.scalar_tensor_tensor(out=rr, in0=kf, scalar=-LN2_LO, in1=rr, op0=ALU.mult, op1=ALU.add))
            link(v.tensor_scalar(pp, rr, 1.0 / 5040, None, ALU.mult))
            for c in (1.0 / 720, 1.0 / 120, 1.0 / 24, 1.0 / 6, 0.5, 1.0):
                link(v.scalar_tensor_tensor(out=pp, in0=pp, scalar=c, in1=rr, op0=ALU.add, op1=ALU.mult))
            link(v.tensor_scalar(kx[:, :], kf, 127.0, None, ALU.add))
            link(v.tensor_scalar(kx[:, :], kx[:, :], 23, None, ALU.logical_shift_left))
            link(v.scalar_tensor_tensor(out=pp, in0=pp, scalar=1.0, in1=kx[:, :].bitcast(F32), op0=ALU.add, op1=ALU.mult))
            dt, a_re = pp[:, 0:H], pp[:, H:W]
            link(v.scalar_tensor_tensor(out=smv(AR), in0=dt, scalar=-1.0, in1=a_re, op0=ALU.mult, op1=ALU.mult))
            v.tensor_tensor(smv(BR), dt, ai[:, :], ALU.mult).then_inc(a_ready, 1)
            dve.wait_ge(a_ready, 1)
            dve.wait_ge(iota_done, 5)
            br = smv(BR)
            v.tensor_tensor(fine(ang), over_lags(br, RL), over_heads(r_iota[:, :]), ALU.mult)
            v.tensor_tensor(crs(ang, FW), over_lags(br, QL), over_heads(q_iota[:, :]), ALU.mult)
            link(v.tensor_copy(ang[:, FW + CW:AW], br))
            v.tensor_scalar(turn[:, 0:FW], ang[:, 0:FW], 1.0 / 6.283185307179586, phase[:, 0:1], ALU.mult, ALU.add)
            link(v.tensor_scalar(turn[:, FW:AW], ang[:, FW:AW], 1.0 / 6.283185307179586, None, ALU.mult))
            link(v.tensor_scalar(turn[:, :], turn[:, :], MAGIC, None, ALU.add))
            link(v.tensor_scalar(turn[:, :], turn[:, :], -MAGIC, None, ALU.add))
            link(v.scalar_tensor_tensor(out=ang[:, :], in0=turn[:, :], scalar=-TWO_PI_HI, in1=ang[:, :], op0=ALU.mult, op1=ALU.add))
            link(v.scalar_tensor_tensor(out=ang[:, :], in0=turn[:, :], scalar=-TWO_PI_LO, in1=ang[:, :], op0=ALU.mult, op1=ALU.add))
            link(v.tensor_scalar(ang[:, 0:FW], ang[:, 0:FW], phase[:, 1:2], None, ALU.add))
            v.tensor_scalar(ang[:, :], ang[:, :], PI_DOWN, -PI_DOWN, ALU.min, ALU.max).then_inc(ang_ready, 1)
            v.tensor_tensor(fine(dec), over_lags(smv(AR), RL), over_heads(r_iota[:, :]), ALU.mult)
            v.tensor_tensor(crs(dec, FW), over_lags(smv(AR), QL), over_heads(q_iota[:, :]), ALU.mult).then_inc(dec_mul, 1)
            dve.wait_ge(tanh_done, 1)
            link(v.tensor_scalar(smv(T0), smv(TANH), -1.0, 1.0, ALU.mult, ALU.add))
            link(v.reciprocal(smv(T1), smv(T0)))
            link(v.scalar_tensor_tensor(out=smv(EM), in0=smv(TANH), scalar=2.0, in1=smv(T1), op0=ALU.mult, op1=ALU.mult))
            dve.wait_ge(sin_done, 2)
            shb, snb = sh[:, CW:CW + H], sn[:, FW + CW:AW]
            link(v.tensor_tensor(smv(T0), shb, shb, ALU.mult))
            link(v.tensor_scalar(smv(CB), smv(T0), -2.0, 1.0, ALU.mult, ALU.add))
            link(v.tensor_tensor(smv(T1), smv(EM), smv(CB), ALU.mult))
            link(v.scalar_tensor_tensor(out=smv(SR), in0=smv(T0), scalar=-2.0, in1=smv(T1), op0=ALU.mult, op1=ALU.add))
            link(v.scalar_tensor_tensor(out=smv(SI), in0=smv(EM), scalar=1.0, in1=snb, op0=ALU.add, op1=ALU.mult))
            link(v.tensor_tensor(smv(T0), cr[:, :], smv(SR), ALU.mult))
            link(v.tensor_tensor(smv(T1), ci[:, :], smv(SI), ALU.mult))
            link(v.tensor_tensor(smv(QR), smv(T0), smv(T1), ALU.subtract))
            link(v.tensor_tensor(smv(T0), cr[:, :], smv(SI), ALU.mult))
            link(v.tensor_tensor(smv(T1), ci[:, :], smv(SR), ALU.mult))
            link(v.tensor_tensor(smv(QI), smv(T0), smv(T1), ALU.add))
            link(v.tensor_tensor(smv(T0), a_re, a_re, ALU.mult))
            link(v.tensor_tensor(smv(T1), ai[:, :], ai[:, :], ALU.mult))
            link(v.tensor_tensor(smv(T0), smv(T0), smv(T1), ALU.add))
            link(v.reciprocal(smv(IA), smv(T0)))
            link(v.tensor_tensor(smv(T0), smv(QI), ai[:, :], ALU.mult))
            link(v.tensor_tensor(smv(T1), smv(QR), a_re, ALU.mult))
            link(v.tensor_tensor(smv(T0), smv(T0), smv(T1), ALU.subtract))
            link(v.scalar_tensor_tensor(out=smv(SR), in0=smv(T0), scalar=2.0, in1=smv(IA), op0=ALU.mult, op1=ALU.mult))
            link(v.tensor_tensor(smv(T0), smv(QR), ai[:, :], ALU.mult))
            link(v.tensor_tensor(smv(T1), smv(QI), a_re, ALU.mult))
            link(v.tensor_tensor(smv(T0), smv(T0), smv(T1), ALU.add))
            link(v.scalar_tensor_tensor(out=smv(SI), in0=smv(T0), scalar=-2.0, in1=smv(IA), op0=ALU.mult, op1=ALU.mult))
            lo, hi = slice(0, NS), slice(NS, P)
            csr, csi = sm[:, 2 * H * SR:2 * H * SR + H], sm[:, 2 * H * SI:2 * H * SI + H]
            v.tensor_copy(uu[lo, :], csr[lo, :])
            v.tensor_scalar(uu[hi, :], csi[hi, :], -1.0, None, ALU.mult)
            v.tensor_scalar(vv[lo, :], csi[lo, :], -1.0, None, ALU.mult)
            link(v.tensor_scalar(vv[hi, :], csr[hi, :], -1.0, None, ALU.mult))
            dve.wait_ge(dec_done, 1)
            link(v.tensor_tensor(coarse[:, :], sh[:, 0:CW], sh[:, 0:CW], ALU.mult))
            link(v.tensor_scalar(coarse[:, :], coarse[:, :], -2.0, 1.0, ALU.mult, ALU.add))
            link(v.tensor_tensor(crs(coarse), crs(coarse), over_lags(uu[:, :], QL), ALU.mult))
            link(v.tensor_tensor(crs(coarse_b), crs(sn, FW), over_lags(vv[:, :], QL), ALU.mult))
            link(v.tensor_tensor(coarse[:, :], coarse[:, :], coarse_b[:, :], ALU.add))
            link(v.tensor_tensor(coarse[:, :], coarse[:, :], dec[:, FW:FW + CW], ALU.mult))
            v.tensor_tensor(sn[:, 0:FW], sn[:, 0:FW], dec[:, 0:FW], ALU.mult).then_inc(table_done, 1)
            dve.wait_ge(table_done, 1)
            link(v.tensor_copy(len_f[:, :], len_i[:, :]))
            for m in range(DC):
                link(v.tensor_scalar(mask_len[:, m * B:(m + 1) * B], len_f[:, :], l_iota[:, m:m + 1], None, ALU.is_gt))
            link(v.tensor_copy(ad_f[:, :], ad_i[:, :]))
            link(v.tensor_scalar(a_int[:, :], a_int[:, :], 4, None, ALU.logical_shift_right))
            link(v.tensor_copy(a_iota[:, :], a_int[:, :]))
            for m in range(AC):
                link(v.tensor_scalar(mask_ad[:, m * B:(m + 1) * B], ad_f[:, :], a_iota[:, m:m + 1], 0.5, ALU.is_equal, ALU.mult))
            for i in range(2):
                dve.wait_ge(k_ready, 1)
                v.tensor_copy(k_sb[0:QL, i * 512:(i + 1) * 512], bank[i][0:QL, :]).then_inc(k_evac, 1)
            dve.wait_ge(w0_hi_done, 1)
            v.tensor_tensor(w0_lo[:, :], w0_raw[:, :], w0_hi[:, :].bitcast(F32), ALU.subtract).then_inc(w0_split, 1)

            mask_h = mask_len[:, :].rearrange("p (m b) -> p m b", m=DC).unsqueeze(1).broadcast_to([P, 2, DC, B])
            y_heads = yT[:, :].rearrange("p (m b h) -> p h m b", m=DC, b=B)
            with dve.Fori(0, NG // 2) as it:
                for u in range(2):
                    for pr in range(2):
                        dve.wait_ge(conv_done, it * 4 + (2 * u + pr + 5))
                        v.tensor_tensor(y_heads[:, bass.ds(it * (2 * CH) + (u * CH + 2 * pr), 2), :, :],
                                        bank[2 * u + pr][:, :].rearrange("p (h m b) -> p h m b", h=2, m=DC), mask_h,
                                        ALU.mult).then_inc(conv_free, 1)

            def h3(tile):
                return tile.rearrange("p (j k) -> p j k", j=NJ)

            def over_k(col, k):
                return col.unsqueeze(2).broadcast_to([P, NJ, k])

            def over_j(row):
                return row.unsqueeze(1).broadcast_to([P, NJ, row.shape[1]])

            dve.wait_ge(small_in, 16 * SMALL_LOADS)
            dve.wait_ge(h_ready, 1)
            link(v.tensor_tensor(h3(hh[:, :]), h3(bank[0][:, :]), over_j(gb1[:, :]), ALU.add))
            link(v.tensor_reduce(rsv(MU), h3(hh[:, :]), AX_X, ALU.add))
            link(v.tensor_scalar(rsv(MU), rsv(MU), 1.0 / G0, None, ALU.mult))
            link(v.tensor_tensor(h3(hh[:, :]), h3(hh[:, :]), over_k(rsv(MU), G0), ALU.subtract))
            link(v.tensor_tensor(hq[:, :], hh[:, :], hh[:, :], ALU.mult))
            link(v.tensor_reduce(rsv(VAR), h3(hq[:, :]), AX_X, ALU.add))
            v.tensor_scalar(rsv(VAR), rsv(VAR), 1.0 / G0, 1e-5, ALU.mult, ALU.add).then_inc(var_done, 1)
            dve.wait_ge(sqrt_done, 1)
            link(v.reciprocal(rsv(RC), rsv(SD)))
            link(v.tensor_tensor(rsv(T3), rsv(RC), rsv(RC), ALU.mult))
            link(v.tensor_tensor(rsv(T3), rsv(T3), rsv(VAR), ALU.mult))
            link(v.tensor_scalar(rsv(T3), rsv(T3), -0.5, 1.5, ALU.mult, ALU.add))
            link(v.tensor_tensor(rsv(RC), rsv(RC), rsv(T3), ALU.mult))
            link(v.tensor_tensor(h3(hh[:, :]), h3(hh[:, :]), over_k(rsv(RC), G0), ALU.mult))
            link(v.tensor_tensor(h3(hh[:, :]), h3(hh[:, :]), over_j(lng[:, :]), ALU.mult))
            link(v.tensor_tensor(h3(hh[:, :]), h3(hh[:, :]), over_j(lnb[:, :]), ALU.add))
            v.tensor_scalar(hh[:, :], hh[:, :], 0.0, None, ALU.max).then_inc(h_norm, 1)
            dve.wait_ge(hT_ready, 1)
            v.tensor_copy(hT[:, :], bank[1][:, :]).then_inc(hT_evac, 1)
            dve.wait_ge(g_ready, 1)
            link(v.tensor_tensor(h3(ga[:, :]), h3(bank[2][:, 0:NJ * E0]), over_j(gb2[:, :]), ALU.add))
            for j in range(NJ):
                last = v.max(mv[:, 8 * j:8 * j + 8], ga[:, E0 * j:E0 * j + E0])
            link(last)
            for j in range(NJ):
                last = v.max_index(mi[:, 8 * j:8 * j + 8], mv[:, 8 * j:8 * j + 8], ga[:, E0 * j:E0 * j + E0])
            link(last)
            mv3 = mv[:, :].rearrange("p (j k) -> p k j", k=8)
            link(v.tensor_copy(i2[:, :].rearrange("p (k j) -> p k j", k=2),
                               mi[:, :].rearrange("p (j k) -> p k j", k=8)[:, 0:2, :]))
            v.tensor_tensor(rsv(DL), mv3[:, 0, :], mv3[:, 1, :], ALU.subtract).then_inc(dl_ready, 1)
            v.tensor_tensor(oh[:, :].rearrange("p (x e) -> p x e", e=E0),
                            i2[:, :].unsqueeze(2).broadcast_to([P, 2 * NJ, E0]),
                            e_iota[:, 0:E0].unsqueeze(1).broadcast_to([P, 2 * NJ, E0]), ALU.is_equal).then_inc(oh_ready, 1)
            dve.wait_ge(th_ready, 1)
            dve.wait_ge(oh_ready, 1)
            link(v.tensor_scalar(i2[:, 0:NJ], rsv(TH), 0.5, 0.5, ALU.mult, ALU.add))
            link(v.tensor_scalar(i2[:, NJ:2 * NJ], rsv(TH), -0.5, 0.5, ALU.mult, ALU.add))
            link(v.tensor_tensor(wk[:, :].rearrange("p (x e) -> p x e", e=E0), oh[:, :].rearrange("p (x e) -> p x e", e=E0),
                                 i2[:, :].unsqueeze(2).broadcast_to([P, 2 * NJ, E0]), ALU.mult))
            dve.wait_ge(cnt_ready, 1)
            link(v.tensor_reduce(cn[:, :].rearrange("p (k e) -> p k e", k=2),
                                 bank[3][:, 0:2 * NJ * E0].rearrange("p (k j e) -> p k e j", k=2, j=NJ), AX_X, ALU.add))
            link(v.tensor_scalar(cn[:, :], cn[:, :], float(CAP0), 1.0 / R0, ALU.is_le, ALU.mult))
            for k in range(2):
                wk_k = h3(wk[:, k * NJ * E0:(k + 1) * NJ * E0])
                link(v.tensor_tensor(wk_k, wk_k, over_j(cn[:, k * E0:(k + 1) * E0]), ALU.mult))
            v.tensor_tensor(w_te[:, :], wk[:, 0:NJ * E0], wk[:, NJ * E0:2 * NJ * E0], ALU.add).then_inc(w_ready, 1)

            xh = xT[:, :].rearrange("p (g c h b) -> p g c h b", g=NG, c=DC, h=CH)
            with dve.Fori(0, NT) as t:
                for c in range(DC):
                    cs = slice(c * TW, (c + 1) * TW)
                    dve.wait_ge(yhi_done, t * DC + (c + 1))
                    v.tensor_tensor(y_lo[:, cs], yT[:, bass.ds(t * TW + c * N, TW)], y_hi[:, cs].bitcast(F32),
                                    ALU.subtract).then_inc(ysplit, 1)
                dve.wait_ge(wT_evac, 4)
                dve.wait_ge(t_ready, t + 1)
                v.tensor_tensor(t_f[:, :], bank[5][:, :], wT[:, bass.ds(t * TW, TW)], ALU.mult).then_inc(tf_done, 1)
                dve.wait_ge(thi_done, t + 1)
                v.tensor_tensor(t_lo[:, :], t_f[:, :], t_hi[:, :].bitcast(F32), ALU.subtract).then_inc(tsplit, 1)
                dve.wait_ge(x1tok_ready, t * 4 + 1)
                for m in range(DC):
                    dve.wait_ge(x1_ready, t * DC + (m + 1))
                    dve.wait_ge(x1t_copied, t * DC + (m + 1))
                    v.tensor_tensor(x1_t[:, m * TW:(m + 1) * TW].rearrange("p (b g h) -> p b g h", g=NG, h=CH),
                                    bank[m][:, :].rearrange("p (b g h) -> p b g h", g=NG, h=CH),
                                    xh[:, :, m, :, bass.ds(t * BT, BT)].rearrange("p g h b -> p b g h"),
                                    ALU.add).then_inc(x1t_done, 1)

            dve.wait_ge(la_hi_done, 1)
            v.tensor_tensor(la_lo[:, :], la_raw[:, :], la_hi[:, :].bitcast(F32), ALU.subtract).then_inc(la_split, 1)
            dve.wait_ge(bd_hi_done, 1)
            v.tensor_tensor(bd_lo[:, :], bd_raw[:, :], bd_hi[:, :].bitcast(F32), ALU.subtract).then_inc(bd_split, 1)

            def mask_lora(it, u, q, src):
                m = mask_ad[:, bass.ds(it * (2 * BT) + ((q % AC) * B + u * BT), BT)]
                v.tensor_tensor(ta_f[:, :].rearrange("p (b h) -> p b h", b=BT), src[:, :].rearrange("p (b h) -> p b h", b=BT),
                                m.unsqueeze(2).broadcast_to([P, BT, H]), ALU.mult).then_inc(taf_done, 1)

            def lora_lo(it, u, q, dst, hi_part):
                dve.wait_ge(tahi_done, it * (2 * LQ) + (LQ * u + q + 1))
                v.tensor_tensor(dst, ta_f[:, :], hi_part.bitcast(F32), ALU.subtract).then_inc(ta_split, 1)
                dve.wait_ge(ta_split, it * (2 * LQ) + (LQ * u + q + 1))

            def down_lora(it, u):
                for q in range(AC):
                    dve.wait_ge(td_ready, it * (2 * AC) + (u * AC + q + 1))
                    mask_lora(it, u, q, bank[4 + q])
                    lora_lo(it, u, 2 * AC + q, td_lo[:, q * TW:(q + 1) * TW], td_hi[:, q * TW:(q + 1) * TW])

            def lo_part(it, s, part, w):
                b = s % 2
                sl = slice(b * ST_W, b * ST_W + GU) if part == 0 else slice(b * ST_W + GU, (b + 1) * ST_W)
                n = 2 * s + part + 1
                dve.wait_ge(st_hi_done, it * (4 * FC) + n)
                v.tensor_tensor(st_lo[:, sl], st_raw[:, sl], st_hi[:, sl].bitcast(F32), ALU.subtract).then_inc(st_split, 1)

            TA_BANK = [bank[4], bank[5], bank[0], bank[1]]
            with dve.Fori(0, NT // 2) as it:
                lo_part(it, 0, 0, 0)
                for u in range(2):
                    t = it * 2 + u
                    for c in range(DC):
                        cs = slice(c * TW, (c + 1) * TW)
                        dve.wait_ge(xhi_done, t * DC + (c + 1))
                        v.tensor_tensor(x_lo[:, cs], x1T[:, bass.ds(t * (DC * TW) + c * TW, TW)], x_hi[:, cs].bitcast(F32),
                                        ALU.subtract).then_inc(xsplit, 1)
                    if u == 1:
                        down_lora(it, 0)
                    for q in range(2 * AC):
                        dve.wait_ge(ta_ready, it * (4 * AC) + (2 * AC * u + q + 1))
                        mask_lora(it, u, q, TA_BANK[q])
                        lora_lo(it, u, q, ta_lo[:, q * TW:(q + 1) * TW], ta_hi[:, q * TW:(q + 1) * TW])
                    for f in range(FC):
                        s = u * FC + f
                        b = s % 2
                        lo_part(it, s, 1, 0)
                        if s + 1 < 2 * FC:
                            lo_part(it, s + 1, 0, 0)
                        dve.wait_ge(up_ready, it * (2 * FC) + (s + 2))
                        dve.wait_ge(silu_done, it * (2 * FC) + (s + 2))
                        v.tensor_tensor(prod_s[:, :], bank[7][:, :], silu_s[:, :], ALU.mult).then_inc(prod_done, 1)
                        dve.wait_ge(acthi_done, it * (2 * FC) + (s + 1))
                        v.tensor_tensor(act_lo[:, b * TW:(b + 1) * TW], prod_s[:, :], act_hi[:, b * TW:(b + 1) * TW].bitcast(F32),
                                        ALU.subtract).then_inc(act_split, 1)
                        dve.wait_ge(act_split, it * (2 * FC) + (s + 1))
                down_lora(it, 1)

            dve.wait_ge(lgt_ready, 1)
            link(v.tensor_copy(lgt[:, :], bank[6][:, 0:NJ * E1]))
            for j in range(NJ):
                last = v.max(mv1[:, 8 * j:8 * j + 8], lgt[:, E1 * j:E1 * j + E1])
            link(last)
            for j in range(NJ):
                last = v.max_index(mi1[:, 8 * j:8 * j + 8], mv1[:, 8 * j:8 * j + 8], lgt[:, E1 * j:E1 * j + E1])
            link(last)
            link(v.tensor_copy(j2[:, :].rearrange("p (k j) -> p k j", k=2),
                               mi1[:, :].rearrange("p (j k) -> p k j", k=8)[:, 0:2, :]))
            link(v.tensor_tensor(oh1[:, :].rearrange("p (x e) -> p x e", e=E1),
                                 j2[:, :].unsqueeze(2).broadcast_to([P, 2 * NJ, E1]),
                                 e_iota[:, :].unsqueeze(1).broadcast_to([P, 2 * NJ, E1]), ALU.is_equal))
            v.tensor_tensor(ohs[:, :], oh1[:, 0:NJ * E1], oh1[:, NJ * E1:2 * NJ * E1], ALU.add).then_inc(ohs_ready, 1)
            mv4 = mv1[:, :].rearrange("p (j k) -> p k j", k=8)
            v.tensor_tensor(dl[:, 0:NJ], mv4[:, 0, :], mv4[:, 1, :], ALU.subtract).then_inc(dl1_ready, 1)
            dve.wait_ge(pos_ready, 2)
            v.tensor_copy(pos1[:, :], bank[7][:, 0:NJ * E1])
            link(v.tensor_copy(tot1[:, :], bank[7][:, NJ * E1:2 * NJ * E1]))
            src, dst = tot1, sc_a
            for d in (1, 2, 4, 8):
                w = d * E1
                v.tensor_copy(dst[:, 0:w], src[:, 0:w])
                link(v.tensor_tensor(dst[:, w:], src[:, w:], src[:, 0:NJ * E1 - w], ALU.add))
                src, dst = dst, (sc_b if dst is sc_a else sc_a)
            incl = src
            link(v.tensor_tensor(pos1[:, :], pos1[:, :], incl[:, :], ALU.add))
            link(v.tensor_tensor(pos1[:, :], pos1[:, :], tot1[:, :], ALU.subtract))
            cntv = incl[:, (NJ - 1) * E1:NJ * E1]
            link(v.tensor_scalar(nbi[:, :], cntv, float(P - 1), None, ALU.add))
            link(v.tensor_scalar(nbi[:, :], nbi[:, :], 7, None, ALU.logical_shift_right))
            nb = [nbk[:, i * E1:(i + 1) * E1] for i in range(8)]
            link(v.tensor_copy(nb[0], nbi[:, :]))
            si = 0
            for i, d in enumerate((1, 2, 4, 8)):
                v.tensor_copy(nb[i + 1][:, 0:d], nb[si][:, 0:d])
                link(v.tensor_tensor(nb[i + 1][:, d:], nb[si][:, d:], nb[si][:, 0:E1 - d], ALU.add))
                si = i + 1
            link(v.tensor_tensor(nb[5], nb[4], nb[0], ALU.subtract))
            link(v.tensor_scalar(nb[5], nb[5], float(P), None, ALU.mult))
            link(v.tensor_tensor(h3(pos1[:, :]), h3(pos1[:, :]), over_j(nb[5]), ALU.add))
            for k in range(2):
                link(v.tensor_tensor(ohp[:, k * NJ * E1:(k + 1) * NJ * E1], oh1[:, k * NJ * E1:(k + 1) * NJ * E1],
                                     pos1[:, :], ALU.mult))
            link(v.tensor_reduce(slf[:, :], ohp[:, :].rearrange("p (x e) -> p x e", e=E1), AX_X, ALU.add))
            link(v.tensor_copy(slot_u[:, :], slf[:, :]))
            link(v.tensor_scalar(slot_b[:, :], slot_u[:, :], 7, None, ALU.logical_shift_right))
            link(v.tensor_copy(slot_bf[:, :], slot_b[:, :]))
            link(v.tensor_scalar(slf[:, :], slf[:, :], float(NB), None, ALU.mult))
            v.scalar_tensor_tensor(out=list_u[:, :], in0=slot_bf[:, :], scalar=-float(P * NB - 1), in1=slf[:, :],
                                   op0=ALU.mult, op1=ALU.add).then_inc(slots_ready, 1)
            link(v.tensor_tensor(bcmp[:, :].rearrange("p (b e) -> p b e", e=E1),
                                 b_iota[:, :].unsqueeze(2).broadcast_to([P, NB, E1]),
                                 nb[4].unsqueeze(1).broadcast_to([P, NB, E1]), ALU.is_ge))
            link(v.tensor_reduce(ebf[:, :], bcmp[:, :].rearrange("p (b e) -> p b e", e=E1), AX_X, ALU.add))
            link(v.tensor_scalar(blk_e[:, :], ebf[:, :], float(E1 - 1), None, ALU.min))
            dve.wait_ge(th1_ready, 1)
            v.tensor_scalar(gate1[:, 0:NJ], dl[:, NJ:2 * NJ], 0.5, 0.5, ALU.mult, ALU.add)
            v.tensor_scalar(gate1[:, NJ:2 * NJ], dl[:, NJ:2 * NJ], -0.5, 0.5, ALU.mult, ALU.add).then_inc(blk_ready, 1)

            def shared_lo(it, s, part):
                b = s % 2
                sl = slice(b * SH_W, b * SH_W + SGU) if part == 0 else slice(b * SH_W + SGU, (b + 1) * SH_W)
                dve.wait_ge(sw_hi_done, it * (4 * SC) + (2 * s + part + 1))
                v.tensor_tensor(sw_lo[:, sl], sw_raw[:, sl], sw_hi[:, sl].bitcast(F32), ALU.subtract).then_inc(sw_split, 1)

            def shared_base(it, u, r):
                j = (it * 2 + u) * 4
                dve.wait_ge(x1_in, (it * 2 + u) * 16 + 16)
                dve.wait_ge(base_ready, j + (r + 1))
                row = cT[:, bass.ds(j * D + r * D, D)]
                v.tensor_tensor(row, bank[r][:, :], row, ALU.add).then_inc(base_done, 1)

            with dve.Fori(0, NT // 2) as it:
                shared_lo(it, 0, 0)
                for u in range(2):
                    t = it * 2 + u
                    for c in range(DC):
                        cs = slice(c * TW, (c + 1) * TW)
                        dve.wait_ge(chi_done, t * DC + (c + 1))
                        v.tensor_tensor(x_lo[:, cs], cT[:, bass.ds(t * (DC * TW) + c * TW, TW)], x_hi[:, cs].bitcast(F32),
                                        ALU.subtract).then_inc(csplit, 1)
                    if u == 1:
                        for s in range(4):
                            shared_base(it, 0, s)
                    for i in range(SC):
                        s = u * SC + i
                        b = s % 2
                        shared_lo(it, s, 1)
                        if s + 1 < 2 * SC:
                            shared_lo(it, s + 1, 0)
                        dve.wait_ge(sup_ready, it * (2 * SC) + (s + 2))
                        dve.wait_ge(ssilu_done, it * (2 * SC) + (s + 2))
                        v.tensor_tensor(prod_s[:, :], bank[5][:, :], silu_s[:, :], ALU.mult).then_inc(sprod_done, 1)
                        dve.wait_ge(sacthi_done, it * (2 * SC) + (s + 1))
                        v.tensor_tensor(act_lo[:, b * TW:(b + 1) * TW], prod_s[:, :], act_hi[:, b * TW:(b + 1) * TW].bitcast(F32),
                                        ALU.subtract).then_inc(sact_split, 1)
                        dve.wait_ge(sact_split, it * (2 * SC) + (s + 1))
                for s in range(4):
                    shared_base(it, 1, s)

            def act_e(b4, u):
                q = u % 4
                dve.wait_ge(es_done, b4 + (u + 1))
                v.tensor_tensor(eh[:, q * I1:(q + 1) * I1], bank[2 + u % 2][:, I1:2 * I1], es[:, q * I1:(q + 1) * I1],
                                ALU.mult).then_inc(eh_done, 1)

            def step_e(b4, u, bd4, nxt):
                q = u % 4
                dve.wait_ge(ehT_ready, b4 + (u + 1))
                v.tensor_copy(ehT[:, q * P:(q + 1) * P], bank[4][:, 0:P]).then_inc(ehT_evac, 1)
                if nxt:
                    act_e(b4, u + 1)
                dve.wait_ge(ey_ready, b4 + (u + 1))
                dve.wait_ge(y_out[q], bd4 + 16)
                v.tensor_copy(ys[:, q * D:(q + 1) * D], bank[5 + u % 2][:, :]).then_inc(ys_done, 1)

            act_e(0, 0)
            with dve.Fori(0, NB // 4 - 1) as it:
                for u in range(4):
                    step_e(it * 4, u, it * 16, True)
            for u in range(4):
                step_e(NB - 4, u, 16 * (NB // 4 - 1), u < 3)

            for j in range(NJ):
                u = j % 4
                us = slice(u * D, (u + 1) * D)
                dve.wait_ge(y1_in[u], 16 * (j // 4 + 1))
                if j >= 4:
                    dve.wait_ge(fin_out[u], 16 * (j // 4))
                v.scalar_tensor_tensor(out=fin[:, us], in0=y1[:, us], scalar=gate1[:, j:j + 1],
                                       in1=cT[:, j * D:(j + 1) * D], op0=ALU.mult, op1=ALU.add).then_inc(fma1_done, 1)
                dve.wait_ge(fma1_done, j + 1)
                dve.wait_ge(y2_in[u], 16 * (j // 4 + 1))
                v.scalar_tensor_tensor(out=fin[:, us], in0=y2[:, us], scalar=gate1[:, NJ + j:NJ + j + 1],
                                       in1=fin[:, us], op0=ALU.mult, op1=ALU.add).then_inc(fma2_done, 1)

        @block.tensor
        def _(pe):
            mm = nc.tensor.matmul

            def split3(o, w_hi, w_lo, x_hi_, x_lo_, start, stop):
                mm(o, w_hi, x_hi_, start=start, stop=False)
                mm(o, w_hi, x_lo_, start=False, stop=False)
                return mm(o, w_lo, x_hi_, start=False, stop=stop)

            pe.wait_ge(d_done, 1)
            pe.wait_ge(table_done, 1)
            for h in range(H):
                i, c = h // (H // 2), (h % (H // 2)) * RL
                mm(bank[i][0:QL, c:c + RL], q_last[0:1, :], d_pad[0:1, h * RL:(h + 1) * RL], start=True, stop=False)
                last = mm(bank[i][0:QL, c:c + RL], coarse[:, h * QL:(h + 1) * QL], sn[:, h * RL:(h + 1) * RL],
                          start=False, stop=True)
            last.then_inc(k_ready, 1)

            x5 = xT[:, :].rearrange("p (g c h b) -> p g c h b", g=NG, c=DC, h=CH)
            pe.wait_ge(k_evac, 2)
            pe.wait_ge(x_in, 16 * NG)
            with pe.Fori(0, NG // 2) as it:
                for u in range(2):
                    pe.wait_ge(toep_in[u], it * 16 + 16)
                    for pr in range(2):
                        pe.wait_ge(conv_free, it * 4 + (2 * u + pr + 1))
                        for h2 in range(2):
                            hh_ = 2 * pr + h2
                            for d in range(DC):
                                i0 = (u * CH + hh_) * D + D - P * (d + 1)
                                last = mm(bank[2 * u + pr][:, h2 * DC * B + d * B:(h2 + 1) * DC * B],
                                          toep[:, i0:i0 + P], x5[:, bass.ds(it * 2 + u, 1), 0:DC - d, hh_, :],
                                          start=(d == 0), stop=(d == DC - 1), skip_group_check=True)
                        last.then_inc(conv_done, 1)

            pe.wait_ge(conv_free, 2 * NG + 4)
            pe.wait_ge(small_in, 16 * SMALL_LOADS)
            for j in range(NJ):
                for m in range(DC):
                    last = mm(bank[0][:, G0 * j:G0 * (j + 1)], yT[:, m * N + j * P:m * N + (j + 1) * P],
                              gw1T[:, m * G0:(m + 1) * G0], start=(m == 0), stop=(m == DC - 1))
            last.then_inc(h_ready, 1)
            pe.wait_ge(const_done, 4)
            pe.wait_ge(h_norm, 1)
            for i in range(4):
                last = nc.tensor.transpose(bank[1][:, i * P:(i + 1) * P], hh[:, i * P:(i + 1) * P], ident[:, :])
            last.then_inc(hT_ready, 1)
            pe.wait_ge(hT_evac, 1)
            for i in range(4):
                last = mm(bank[2][:, 4 * E0 * i:4 * E0 * (i + 1)], hT[:, i * P:(i + 1) * P], gw2bd[:, :], start=True, stop=True)
            last.then_inc(g_ready, 1)
            pe.wait_ge(oh_ready, 1)
            mm(bank[3][:, 0:2 * NJ * E0], ones[:, :], oh[:, :], start=True, stop=True).then_inc(cnt_ready, 1)
            pe.wait_ge(wexp_done, 1)
            for j in range(NJ):
                last = nc.tensor.transpose(bank[4 + j // 4][:, (j % 4) * P:(j % 4 + 1) * P],
                                           w_exp[:, j * P:(j + 1) * P], ident[:, :])
                if j % 4 == 3:
                    last.then_inc(wT_ready, 1)

            def w0m(part, c, m):
                return part[:, c * D + m * P:c * D + (m + 1) * P]

            A0, B0 = DC * D, DC * D + DC * P
            pe.wait_ge(w0_split, 1)
            pe.wait_ge(wT_evac, 4)
            with pe.Fori(0, NT) as t:
                pe.wait_ge(tf_done, t + 1)
                for c in range(DC):
                    cs = slice(c * TW, (c + 1) * TW)
                    pe.wait_ge(ysplit, t * DC + (c + 1))
                    last = split3(bank[5][:, :], w0_hi[:, A0 + c * P:A0 + (c + 1) * P], w0_lo[:, A0 + c * P:A0 + (c + 1) * P],
                                  y_hi[:, cs], y_lo[:, cs], c == 0, c == DC - 1)
                last.then_inc(t_ready, 1)
                for m in range(DC):
                    pe.wait_ge(x1t_done, t * DC + (m + 1))
                    for c in range(DC):
                        cs = slice(c * TW, (c + 1) * TW)
                        last = split3(bank[m][:, :], w0m(w0_hi, c, m), w0m(w0_lo, c, m), y_hi[:, cs], y_lo[:, cs], c == 0, False)
                last.then_inc(y_used, 1)
                pe.wait_ge(tsplit, t + 1)
                for m in range(DC):
                    split3(bank[m][:, :], w0_hi[:, B0 + m * P:B0 + (m + 1) * P], w0_lo[:, B0 + m * P:B0 + (m + 1) * P],
                           t_hi[:, :], t_lo[:, :], False, True).then_inc(x1_ready, 1)
                pe.wait_ge(x1t_done, t * DC + (DC + 4))
                for s in range(4):
                    pe.wait_ge(x1tok_evac, t * 4 + (s + 1))
                    for m in range(DC):
                        last = nc.tensor.transpose(bank[6 + s % 2][:, m * P:(m + 1) * P],
                                                   x1_t[:, m * TW + s * P:m * TW + (s + 1) * P], ident[:, :])
                    last.then_inc(x1tok_ready, 1)

            pe.wait_ge(la_split, 1)
            pe.wait_ge(bd_split, 1)
            pe.wait_ge(x1tok_evac, 4 * NT + 2)

            def lora_a(it, u):
                t = it * 2 + u
                for q in range(2 * AC):
                    if q >= 2:
                        pe.wait_ge(c_evac, t * DC + (q - 1))
                    for c in range(DC):
                        if q == 0:
                            pe.wait_ge(xsplit, t * DC + (c + 1))
                        cs = slice(c * TW, (c + 1) * TW)
                        ls = slice((c * 2 * AC + q) * P, (c * 2 * AC + q + 1) * P)
                        last = split3([bank[4], bank[5], bank[0], bank[1]][q][:, :], la_hi[:, ls], la_lo[:, ls],
                                      x_hi[:, cs], x_lo[:, cs], c == 0, c == DC - 1)
                    last.then_inc(ta_ready, 1)

            def gate_or_up(it, s, which):
                b = s % 2
                u = s // FC
                for c in range(DC + AC):
                    w0c = b * ST_W + which * GA_W + c * P
                    ws = slice(w0c, w0c + P)
                    if c < DC:
                        cs = slice(c * TW, (c + 1) * TW)
                        xh_, xl_ = x_hi[:, cs], x_lo[:, cs]
                    else:
                        q = which * AC + c - DC
                        if s % FC == 0:
                            pe.wait_ge(ta_split, it * (2 * LQ) + (LQ * u + q + 1))
                        cs = slice(q * TW, (q + 1) * TW)
                        xh_, xl_ = ta_hi[:, cs], ta_lo[:, cs]
                    last = split3(bank[6 + which][:, :], st_hi[:, ws], st_lo[:, ws], xh_, xl_, c == 0, c == DC + AC - 1)
                return last

            def down(it, s):
                b = s % 2
                u, f = s // FC, s % FC
                pe.wait_ge(act_split, it * (2 * FC) + (s + 1))
                pe.wait_ge(st_split, it * (4 * FC) + (2 * s + 6))
                xs = slice(b * TW, (b + 1) * TW)
                for q in range(AC):
                    w0c = b * ST_W + GU + D + q * P
                    last = split3(bank[4 + q][:, :], st_hi[:, w0c:w0c + P], st_lo[:, w0c:w0c + P],
                                  act_hi[:, xs], act_lo[:, xs], f == 0, f == FC - 1)
                    if f == FC - 1:
                        last.then_inc(td_ready, 1)
                for m in range(DC):
                    if f == 0 and m >= 2:
                        pe.wait_ge(c_evac, (it * 2 + u) * DC + (m + 1))
                    w0c = b * ST_W + GU + m * P
                    last = split3(bank[m][:, :], st_hi[:, w0c:w0c + P], st_lo[:, w0c:w0c + P],
                                  act_hi[:, xs], act_lo[:, xs], f == 0, False)
                last.then_inc(st_used, 1)

            with pe.Fori(0, NT // 2) as it:
                for u in range(2):
                    lora_a(it, u)
                    for f in range(FC):
                        s = u * FC + f
                        pe.wait_ge(st_split, it * (4 * FC) + (2 * s + 5))
                        pe.wait_ge(silu_done, it * (2 * FC) + (s + 1))
                        gate_or_up(it, s, 0).then_inc(gate_ready, 1)
                        pe.wait_ge(prod_done, it * (2 * FC) + (s + 1))
                        gate_or_up(it, s, 1).then_inc(up_ready, 1)
                        if f:
                            down(it, s - 1)
                    down(it, u * FC + FC - 1)
                    for m in range(DC):
                        for q in range(AC):
                            if m == 0:
                                pe.wait_ge(ta_split, it * (2 * LQ) + (LQ * u + 2 * AC + q + 1))
                            ts = slice(q * TW, (q + 1) * TW)
                            bs = slice(q * D + m * P, q * D + (m + 1) * P)
                            last = split3(bank[m][:, :], bd_hi[:, bs], bd_lo[:, bs], td_hi[:, ts], td_lo[:, ts], False, q == AC - 1)
                        last.then_inc(c_ready, 1)

            def c_at(j, m):
                o = (j // 4) * DC * TW + m * TW + (j % 4) * P
                return cT[:, o:o + P]

            pe.wait_ge(c_evac, NT * DC + 4)
            for j in range(NJ):
                for m in range(DC):
                    last = mm(bank[6][:, E1 * j:E1 * (j + 1)], c_at(j, m), gwT[:, m * E1:(m + 1) * E1],
                              start=(m == 0), stop=(m == DC - 1))
            last.then_inc(lgt_ready, 1)
            for j in range(NJ):
                if j >= 6:
                    pe.wait_ge(ctok_evac, j - 5)
                for m in range(DC):
                    last = nc.tensor.transpose(bank[j % 6][:, m * P:(m + 1) * P], c_at(j, m), ident[:, :])
                last.then_inc(ctok_ready, 1)
            pe.wait_ge(ohs_ready, 1)
            mm(bank[7][:, 0:NJ * E1], before[:, :], ohs[:, :], start=True, stop=True).then_inc(pos_ready, 1)
            mm(bank[7][:, NJ * E1:2 * NJ * E1], ones[:, :], ohs[:, :], start=True, stop=True).then_inc(pos_ready, 1)

            pe.wait_ge(ctok_evac, NJ)

            def shared_down(it, s):
                b = s % 2
                u, i = s // SC, s % SC
                pe.wait_ge(sact_split, it * (2 * SC) + (s + 1))
                pe.wait_ge(sw_split, it * (4 * SC) + (2 * s + 6))
                ws = slice(b * SH_W + SGU, (b + 1) * SH_W)
                for r in range(4):
                    xs = slice(b * TW + r * P, b * TW + (r + 1) * P)
                    if i == 0:
                        pe.wait_ge(base_done, (it * 2 + u) * 4 + (r + 1))
                    mm(bank[r][:, :], act_hi[:, xs], sw_hi[:, ws], start=(i == 0), stop=False)
                    mm(bank[r][:, :], act_hi[:, xs], sw_lo[:, ws], start=False, stop=False)
                    last = mm(bank[r][:, :], act_lo[:, xs], sw_hi[:, ws], start=False, stop=(i == SC - 1))
                    if i == SC - 1:
                        last.then_inc(base_ready, 1)

            with pe.Fori(0, NT // 2) as it:
                for u in range(2):
                    for i in range(SC):
                        s = u * SC + i
                        b = s % 2
                        pe.wait_ge(sw_split, it * (4 * SC) + (2 * s + 5))
                        for which, free, ready in ((0, ssilu_done, sgate_ready), (1, sprod_done, sup_ready)):
                            pe.wait_ge(free, it * (2 * SC) + (s + 1))
                            for c in range(DC):
                                if i == 0 and which == 0:
                                    pe.wait_ge(csplit, (it * 2 + u) * DC + (c + 1))
                                cs = slice(c * TW, (c + 1) * TW)
                                w0c = b * SH_W + which * DC * P + c * P
                                last = split3(bank[4 + which][:, :], sw_hi[:, w0c:w0c + P], sw_lo[:, w0c:w0c + P],
                                              x_hi[:, cs], x_lo[:, cs], c == 0, c == DC - 1)
                            last.then_inc(ready, 1)
                        if i:
                            shared_down(it, s - 1)
                    shared_down(it, u * SC + SC - 1)

            pe.wait_ge(base_done, NJ + 4)
            pe.wait_ge(eg_in, 16)
            pe.wait_ge(ed_in, 16)
            pe.wait_ge(blk_ready, 1)

            def turn_x(b4, u, n16):
                q = u % 4
                pe.wait_ge(xg_in[q], n16)
                pe.wait_ge(xgT_evac, b4 + (u + 1))
                for c in range(DC):
                    last = nc.tensor.transpose(bank[u % 2][:, c * P:(c + 1) * P], xg[:, q * D + c * P:q * D + (c + 1) * P],
                                               ident[:, :])
                last.then_inc(xgT_ready, 1)

            def expert_of(b4, u):
                return pe.value_load(blk_e[0:1, bass.ds(b4 + u, 1)], min_val=0, max_val=E1 - 1)

            def gate_up_e(b4, u, e):
                q = u % 4
                pe.wait_ge(xgT_evac, b4 + (u + 3))
                pe.wait_ge(eh_done, b4 + (u + 1))
                for c in range(DC):
                    last = mm(bank[2 + u % 2][:, 0:2 * I1], xgT[:, q * D + c * P:q * D + (c + 1) * P],
                              eg[:, bass.ds(e * (DC * 2 * I1) + c * 2 * I1, 2 * I1)], start=(c == 0), stop=(c == DC - 1))
                last.then_inc(egu_ready, 1)

            def turn_h(b4, u):
                q = u % 4
                pe.wait_ge(eh_done, b4 + (u + 3))
                pe.wait_ge(ehT_evac, b4 + (u + 1))
                nc.tensor.transpose(bank[4][:, 0:P], eh[:, q * I1:(q + 1) * I1], ident[:, :]).then_inc(ehT_ready, 1)

            def down_e(b4, u, e):
                q = u % 4
                pe.wait_ge(ehT_evac, b4 + (u + 2))
                pe.wait_ge(ys_done, b4 + (u + 1))
                mm(bank[5 + u % 2][:, :], ehT[:, q * P:(q + 1) * P], ed[:, bass.ds(e * D, D)],
                   start=True, stop=True).then_inc(ey_ready, 1)

            turn_x(0, 0, 16)
            turn_x(0, 1, 16)
            gate_up_e(0, 0, expert_of(0, 0))
            with pe.Fori(0, NB // 4 - 1) as it:
                for u in range(4):
                    turn_x(it * 4, u + 2, it * 16 + 16 * (1 + (u + 2) // 4))
                    turn_h(it * 4, u)
                    gate_up_e(it * 4, u + 1, expert_of(it * 4, u + 1))
                    down_e(it * 4, u, expert_of(it * 4, u))
            for u in range(4):
                b4 = NB - 4
                if u < 2:
                    turn_x(b4, u + 2, 16 * (NB // 4))
                turn_h(b4, u)
                if u < 3:
                    gate_up_e(b4, u + 1, expert_of(b4, u + 1))
                down_e(b4, u, expert_of(b4, u))


def kernel(**inputs):
    import numpy as np
    import concourse.bacc as _bacc
    from concourse.bass_utils import run_bass_kernel_spmd as _run

    i = {k: np.asarray(v) for k, v in inputs.items()}
    c = np.ascontiguousarray

    def rows(a, flip=False):
        a = a.reshape(DC, P, -1)
        return (a[:, ::-1] if flip else a).transpose(1, 0, 2)

    def pad(a, n, axis=0):
        w = [(0, 0)] * a.ndim
        w[axis] = (0, n - a.shape[axis])
        return np.pad(a, w)

    x = i["x"]
    arrays = {}
    arrays["x_heads"] = c(x.transpose(1, 2, 0).reshape(NG, CH, DC, P, B).transpose(0, 3, 2, 1, 4)).reshape(NG, P, DC * CH * B)
    arrays["log_dt"] = c(i["L0_cond_log_dt"])
    arrays["s4_par"] = c(np.stack([i["L0_cond_log_A_real"].T, i["L0_cond_A_imag"].T,
                                   i["L0_cond_C"][..., 0].T, i["L0_cond_C"][..., 1].T]))
    arrays["s4_d"] = c(i["L0_cond_D"])
    arrays["lens"] = c(i["itok_B_8_3872"])
    arrays["adapters"] = c(i["itok_B_2_6"])
    la0 = i["L0_ffn_lora_A"].transpose(1, 0, 2).reshape(D, E0 * R0)
    arrays["w0"] = c(np.concatenate([rows(i["L0_ffn_weight"].T, True).reshape(P, -1), rows(la0, True).reshape(P, -1),
                                     i["L0_ffn_lora_B"].reshape(E0 * R0, D)], axis=1))
    arrays["gw1"] = c(rows(i["L0_ffn_gw1"].T, True)).reshape(P, -1)
    for k in ("gb1", "gb2"):
        arrays[k + "_d"] = c(i["L0_ffn_" + k])
    arrays["lng_d"], arrays["lnb_d"] = c(i["L0_ffn_ln_gamma"]), c(i["L0_ffn_ln_beta"])
    arrays["gw2"] = c(i["L0_ffn_gw2"].T)
    ag, au = (i["L1_cond_A_" + k][0].reshape(NA * RA, D).T for k in ("gate", "up"))
    arrays["w_la"] = c(np.concatenate([rows(ag), rows(au)], axis=2)).reshape(P, -1)
    FP = FC * P

    def stacked(k):
        w = pad(i["L1_cond_W_" + k].T, FP, 1).reshape(DC, P, FC, P)
        b = pad(i["L1_cond_B_" + k][0].transpose(0, 2, 1).reshape(NA * RA, F), FP, 1).reshape(AC, P, FC, P)
        return np.concatenate([w, b]).transpose(2, 1, 0, 3).reshape(FC, P, -1)

    wd = pad(i["L1_cond_W_down"].T, FP).reshape(FC, P, D)
    ad = pad(i["L1_cond_A_down"][0].reshape(NA * RA, F).T, FP).reshape(FC, P, NA * RA)
    arrays["w_st"] = c(np.concatenate([stacked("gate"), stacked("up"), wd, ad], axis=2))
    arrays["w_bd"] = c(i["L1_cond_B_down"][0].transpose(0, 2, 1).reshape(AC, P, D).transpose(1, 0, 2)).reshape(P, -1)
    sg = i["L1_ffn_shared_w_gate_up"].T.reshape(DC, P, 2, SC, P).transpose(3, 1, 2, 0, 4).reshape(SC, P, -1)
    arrays["w_sh"] = c(np.concatenate([sg, i["L1_ffn_shared_w_down"].T.reshape(SC, P, D)], axis=2))
    arrays["gw_d"] = c(rows(i["L1_ffn_gate_w"].T)).reshape(P, -1)
    arrays["w_eg"] = c(i["L1_ffn_w_gate_up"].transpose(2, 0, 1).reshape(DC, P, E1, 2 * I1).transpose(1, 2, 0, 3)).reshape(P, -1)
    arrays["w_ed"] = c(i["L1_ffn_w_down"].transpose(2, 0, 1)).reshape(P, -1)

    nc = _bacc.Bacc("TRN2", target_bir_lowering=False, num_devices=1)
    args = {n: nc.dram_tensor(n, a.shape, mybir.dt.from_np(a.dtype), kind="ExternalInput").ap() for n, a in arrays.items()}
    o = nc.dram_tensor("out", (N, D), F32, kind="ExternalOutput").ap()
    conditioned_blocks(nc, out=o, **args)
    r = _run(nc, [arrays], core_ids=[0])
    return r.results[0]["out"].reshape(B, H, D)
```

```python
import concourse.bass as bass
from concourse import mybir
from contextlib import ExitStack

F32 = mybir.dt.float32
F32R = mybir.dt.float32r
I32 = mybir.dt.int32
U32 = mybir.dt.uint32
ALU = mybir.AluOpType
ACT = mybir.ActivationFunctionType
AX_X = mybir.AxisListType.X

P = 128
B, H, D = 64, 32, 512
N = B * H
DC = D // P
NS = 64
RL, QL = 32, D // 32
NT, TW = N // 512, 512
NJ = N // P
BT = TW // H
E0, R0, G0 = 8, 16, 32
CAP0 = int(3.0 * N / E0)
F = 1376
FC = -(-F // P)
NA, RA = 16, 16
AC = NA * RA // P
E1, I1, S1 = 16, 128, 512
SC = S1 // P
NB = -(-((2 * N + E1 * (P - 1)) // P) // 4) * 4
GA_W = (DC + AC) * P
ST_W = 2 * GA_W + D + NA * RA
SH_W = 2 * DC * P + D
CH = 4
NG = H // CH
W0_W = DC * D + DC * P + D
KPW = D + P

AW = H * RL + H * QL + H
FW, CW = H * RL, H * QL

LOG2E = 1.4426950408889634
MAGIC = 12582912.0
LN2_HI, LN2_LO = 0.693359375, -2.12194440e-4
TWO_PI_HI, TWO_PI_LO = 6.28125, 0.0019353071795864769
PI_DOWN = 3.1415925


def conditioned_blocks(nc, x_heads, s4_par, s4_d, lens, adapters, w0, gw1, gb1_d, lng_d, lnb_d,
                       gw2, gb2_d, w_la, w_st, w_bd, w_sh, gw_d, w_eg, w_ed, out):
    ctx = ExitStack()
    with ctx:
        def sem(name):
            return ctx.enter_context(nc.semaphore(name))

        C_BUF = 6
        base = -(-nc.sbuf_base // 32) * 32
        ctx.enter_context(nc.sbuf_tensor("arena", [P, 206 * 256], F32))

        def at(name, kb, cols, dt=F32):
            return nc.alloc_sbuf_tensor_at(name, [P, cols], dt, offset=base + int(kb * 1024))

        bank = [ctx.enter_context(nc.psum_tensor(f"bank{i}", [P, 512], F32)) for i in range(8)]

        ident = at("ident", 0, P)
        ones = at("ones", 0.5, P)
        before = at("before", 1, P)
        e_iota = at("e_iota", 1.5, E1)
        mask_len = at("mask_len", 1.75, DC * B)
        mask_ad = at("mask_ad", 2.75, AC * B)
        slot_u = at("slot_u", 3.25, 2 * NJ, U32)
        gate1 = at("gate1", 3.375, 2 * NJ)
        blk_e = at("blk_e", 3.5, NB, I32)
        tok_id = at("tok_id", 3.75, NJ, U32)
        slot_tok = at("slot_tok", 3.875, NB, U32)
        gwT = at("gwT", 4.25, DC * E1)
        gw1T = at("gw1T", 4.5, DC * G0)
        gb1 = at("gb1", 5, G0)
        lng = at("lng", 5.125, G0)
        lnb = at("lnb", 5.25, G0)
        gb2 = at("gb2", 5.375, E0)
        gw2bd = at("gw2bd", 5.5, 4 * E0)
        b_iota = at("b_iota", 5.75, NB)
        list_u = at("list_u", 6, 2 * NJ, U32)
        slot_b = at("slot_b", 6.125, 2 * NJ)
        xT = at("xT", 8, NG * DC * CH * B)
        yT = at("yT", 40, DC * N)
        y_hi = at("y_hi", 72, DC * TW, F32R)
        y_lo = at("y_lo", 80, DC * TW, F32R)
        toep = at("toep", 88, 2 * CH * D)
        w0_hi = at("w0_hi", 104, W0_W, F32R)
        w0_lo = at("w0_lo", 116, W0_W, F32R)
        w0_raw = at("w0_raw", 128, W0_W)
        par = at("par", 140, 5 * H)
        lg, ai, cr, ci = par[:, 0:2 * H], par[:, 2 * H:3 * H], par[:, 3 * H:4 * H], par[:, 4 * H:5 * H]
        sm = at("sm", 141, 24 * 2 * H)
        kx = at("kx", 147, 2 * H, I32)
        len_i = at("len_i", 147.25, B, I32)
        ad_i = at("ad_i", 147.5, B, I32)
        len_f = at("len_f", 147.75, B)
        ad_f = at("ad_f", 148, B)
        l_iota = at("l_iota", 148.25, DC)
        a_iota = at("a_iota", 148.3125, AC)
        a_int = at("a_int", 148.375, AC, I32)
        r_iota = at("r_iota", 148.5, RL)
        q_iota = at("q_iota", 148.625, QL)
        ang = at("ang", 149, AW)
        turn = at("turn", 155.25, AW)
        dec = at("dec", 161.5, FW + CW)
        sn = at("sn", 167.5, AW)
        sh = at("sh", 173.75, CW + H)
        coarse = at("coarse", 176, CW)
        coarse_b = at("coarse_b", 178, CW)
        uu = at("uu", 180, H)
        vv = at("vv", 180.125, H)
        k_sb = at("k_sb", 181, H * RL)
        d_pad = at("d_pad", 185, H * RL)
        d_row = at("d_row", 189, H)
        fine_t = at("fine_t", 190.25, FW)
        zeros = at("zeros", 189.25, P)
        phase = at("phase", 189.75, 2)
        hf = at("hf", 152, N)
        hh = at("hh", 140, NJ * G0)
        hq = at("hq", 142, NJ * G0)
        hT = at("hT", 144, 4 * P)
        rs = at("rs", 146, 8 * NJ)
        ga = at("ga", 146.5, NJ * E0)
        mv = at("mv", 147, NJ * 8)
        mi = at("mi", 147.5, NJ * 8, U32)
        i2 = at("i2", 148, 2 * NJ)
        oh = at("oh", 148.125, 2 * NJ * E0)
        wk = at("wk", 149.125, 2 * NJ * E0)
        cn = at("cn", 150.125, 2 * E0)
        w_te = at("w_te", 150.25, NJ * E0)
        w_exp = at("w_exp", 190, NJ * E0 * R0)
        wT = at("wT", 152, N)
        t_f = at("t_f", 160, TW)
        t_hi = at("t_hi", 162, TW, F32R)
        t_lo = at("t_lo", 164, TW, F32R)
        x1_t = at("x1_t", 166, DC * TW)
        x1_tok = at("x1_tok", 88, 4 * D)
        x1T = at("x1T", 174, NT * DC * TW)
        cT = at("cT", 8, NT * DC * TW)
        x_hi = at("x_hi", 40, DC * TW, F32R)
        x_lo = at("x_lo", 48, DC * TW, F32R)
        act_hi = at("act_hi", 56, 2 * TW, F32R)
        act_lo = at("act_lo", 60, 2 * TW, F32R)
        silu_s = at("silu_s", 64, TW)
        prod_s = at("prod_s", 66, TW)
        ta_f = at("ta_f", 68, TW)
        st_hi = at("st_hi", 70, 2 * ST_W, F32R)
        st_lo = at("st_lo", 88, 2 * ST_W, F32R)
        st_raw = at("st_raw", 106, 2 * ST_W)
        td_lo = at("td_lo", 124, AC * TW, F32R)
        la_hi = at("la_hi", 128, DC * 2 * AC * P, F32R)
        bd_hi = at("bd_hi", 136, AC * D, F32R)
        bd_raw = at("bd_raw", 140, AC * D)
        bd_lo = at("bd_lo", 140, AC * D, F32R)
        la_raw = at("la_raw", 144, DC * 2 * AC * P)
        la_lo = at("la_lo", 144, DC * 2 * AC * P, F32R)
        ta_hi = at("ta_hi", 152, 2 * AC * TW, F32R)
        ta_lo = at("ta_lo", 160, 2 * AC * TW, F32R)
        td_hi = at("td_hi", 168, AC * TW, F32R)
        c_tok = at("c_tok", 56, C_BUF * D)
        sw_hi = at("sw_hi", 70, 2 * SH_W, F32R)
        sw_lo = at("sw_lo", 82, 2 * SH_W, F32R)
        sw_raw = at("sw_raw", 94, 2 * SH_W)
        eg = at("eg", 106, E1 * DC * 2 * I1)
        ed = at("ed", 170, E1 * D)
        lf = at("lf", 198, N)
        lgt = at("lgt", 170, NJ * E1)
        mv1 = at("mv1", 171, NJ * 8)
        mi1 = at("mi1", 171.5, NJ * 8, U32)
        j2 = at("j2", 172, 2 * NJ)
        dl = at("dl", 172.125, 2 * NJ)
        oh1 = at("oh1", 172.5, 2 * NJ * E1)
        ohs = at("ohs", 174.5, NJ * E1)
        sc_a = at("sc_a", 175.5, NJ * E1)
        sc_b = at("sc_b", 176.5, NJ * E1)
        pos1 = at("pos1", 177.5, NJ * E1)
        tot1 = at("tot1", 178.5, NJ * E1)
        ohp = at("ohp", 179.5, 2 * NJ * E1)
        nbk = at("nbk", 181.5, 8 * E1)
        bcmp = at("bcmp", 182.25, NB * E1)
        ebf = at("ebf", 185.5, NB)
        slf = at("slf", 185.75, 2 * NJ)
        xg = at("xg", 40, 4 * D)
        xgT = at("xgT", 48, 4 * DC * P)
        es = at("es", 56, 4 * I1)
        eh = at("eh", 58, 4 * I1)
        ehT = at("ehT", 60, 4 * P)
        ys = at("ys", 62, 4 * D)
        y1 = at("y1", 72, 4 * D)
        y2 = at("y2", 80, 4 * D)
        fin = at("fin", 88, 4 * D)

        kpad = nc.dram_tensor("kpad", (H, KPW), F32, kind="Internal").ap()
        x1_dram = nc.dram_tensor("x1_dram", (N, D), F32, kind="Internal").ap()
        c_dram = nc.dram_tensor("c_dram", (N, D), F32, kind="Internal").ap()
        y_dram = nc.dram_tensor("y_dram", (NB * P, D), F32, kind="Internal").ap()
        st_dram = nc.dram_tensor("st_dram", (NB * P, 1), U32, kind="Internal").ap()

        par_in = sem("par_in")
        ids_in = sem("ids_in")
        small_in = sem("small_in")
        x_in = sem("x_in")
        w0_in = sem("w0_in")
        kpad_out = sem("kpad_out")
        toep_in = [sem(f"toep_in{i}") for i in range(2)]
        x1_out = [sem(f"x1_out{i}") for i in range(4)]
        la_in = sem("la_in")
        bd_in = sem("bd_in")
        st_in = [sem(f"st_in{i}") for i in range(2)]
        c_out = [sem(f"c_out{i}") for i in range(C_BUF)]
        sw_in = [sem(f"sw_in{i}") for i in range(2)]
        x1_in = sem("x1_in")
        eg_in = sem("eg_in")
        ed_in = sem("ed_in")
        list_zero = sem("list_zero")
        list_out = sem("list_out")
        list_in = sem("list_in")
        xg_in = [sem(f"xg_in{i}") for i in range(4)]
        y_out = [sem(f"y_out{i}") for i in range(4)]
        y1_in = [sem(f"y1_in{i}") for i in range(4)]
        y2_in = [sem(f"y2_in{i}") for i in range(4)]
        fin_out = [sem(f"fin_out{i}") for i in range(4)]
        dve_step = sem("dve_step")
        pool_step = sem("pool_step")
        act_step = sem("act_step")
        iota_done = sem("iota_done")
        a_ready = sem("a_ready")
        ang_ready = sem("ang_ready")
        tanh_done = sem("tanh_done")
        dec_mul = sem("dec_mul")
        dec_done = sem("dec_done")
        sin_done = sem("sin_done")
        table_done = sem("table_done")
        d_done = sem("d_done")
        k_ready = sem("k_ready")
        k_evac = sem("k_evac")
        const_done = sem("const_done")
        conv_done = sem("conv_done")
        conv_free = sem("conv_free")
        w0_split = sem("w0_split")
        w0_hi_done = sem("w0_hi_done")
        hf_ready = sem("hf_ready")
        hf_evac = sem("hf_evac")
        h_ready = sem("h_ready")
        var_done = sem("var_done")
        sqrt_done = sem("sqrt_done")
        h_norm = sem("h_norm")
        hT_ready = sem("hT_ready")
        hT_evac = sem("hT_evac")
        g_ready = sem("g_ready")
        oh_ready = sem("oh_ready")
        cnt_ready = sem("cnt_ready")
        dl_ready = sem("dl_ready")
        th_ready = sem("th_ready")
        w_ready = sem("w_ready")
        wexp_done = sem("wexp_done")
        wT_ready = sem("wT_ready")
        wT_evac = sem("wT_evac")
        yhi_done = sem("yhi_done")
        ysplit = sem("ysplit")
        y_used = sem("y_used")
        t_ready = sem("t_ready")
        tf_done = sem("tf_done")
        thi_done = sem("thi_done")
        tsplit = sem("tsplit")
        x1_ready = sem("x1_ready")
        x1t_done = sem("x1t_done")
        x1t_copied = sem("x1t_copied")
        x1tok_ready = sem("x1tok_ready")
        x1tok_evac = sem("x1tok_evac")
        la_hi_done = sem("la_hi_done")
        la_split = sem("la_split")
        bd_hi_done = sem("bd_hi_done")
        bd_split = sem("bd_split")
        xhi_done = sem("xhi_done")
        xsplit = sem("xsplit")
        ta_ready = sem("ta_ready")
        taf_done = sem("taf_done")
        tahi_done = sem("tahi_done")
        ta_split = sem("ta_split")
        st_hi_done = sem("st_hi_done")
        st_split = sem("st_split")
        st_used = sem("st_used")
        gate_ready = sem("gate_ready")
        silu_done = sem("silu_done")
        up_ready = sem("up_ready")
        prod_done = sem("prod_done")
        acthi_done = sem("acthi_done")
        act_split = sem("act_split")
        td_ready = sem("td_ready")
        c_ready = sem("c_ready")
        c_evac = sem("c_evac")
        lf_ready = sem("lf_ready")
        lf_evac = sem("lf_evac")
        lgt_ready = sem("lgt_ready")
        ctok_ready = sem("ctok_ready")
        ctok_even = sem("ctok_even")
        ctok_odd = sem("ctok_odd")
        ohs_ready = sem("ohs_ready")
        pos_ready = sem("pos_ready")
        pos_evac = sem("pos_evac")
        dl1_ready = sem("dl1_ready")
        th1_ready = sem("th1_ready")
        blk_ready = sem("blk_ready")
        chi_done = sem("chi_done")
        csplit = sem("csplit")
        sw_hi_done = sem("sw_hi_done")
        sw_split = sem("sw_split")
        sgate_ready = sem("sgate_ready")
        ssilu_done = sem("ssilu_done")
        sup_ready = sem("sup_ready")
        sprod_done = sem("sprod_done")
        sacthi_done = sem("sacthi_done")
        sact_split = sem("sact_split")
        base_ready = sem("base_ready")
        base_done = sem("base_done")
        xgT_ready = sem("xgT_ready")
        xgT_evac = sem("xgT_evac")
        egu_ready = sem("egu_ready")
        es_done = sem("es_done")
        eh_done = sem("eh_done")
        ehT_ready = sem("ehT_ready")
        ehT_evac = sem("ehT_evac")
        ey_ready = sem("ey_ready")
        ys_done = sem("ys_done")
        fma1_done = sem("fma1_done")
        fma2_done = sem("fma2_done")

        SMALL_LOADS = 10
        EG_PARTS, ED_PARTS = NT * SC, 4
        LQ = 3 * AC
        TANH, AR, DT, BR, T0, T1, T2, EM, SR, SI, IA, KF, RR, PP, CB, QR, QI, ER, EI = range(19)
        SD, VAR, TH, DL, MU, RC, T3 = range(7)

        def smv(i, w=H):
            return sm[:, 2 * H * i:2 * H * i + w]

        def rsv(i):
            return rs[:, NJ * i:NJ * (i + 1)]

        def fine(tile):
            return tile[:, 0:FW].rearrange("p (h r) -> p h r", h=H)

        def crs(tile, at0=0):
            return tile[:, at0:at0 + CW].rearrange("p (h q) -> p h q", h=H)

        def over_lags(col, n):
            return col.unsqueeze(2).broadcast_to([P, H, n])

        def over_heads(col):
            return col.unsqueeze(1).broadcast_to([P, H, col.shape[1]])

        def h3(tile):
            return tile.rearrange("p (j k) -> p j k", j=NJ)

        def over_k(col, k):
            return col.unsqueeze(2).broadcast_to([P, NJ, k])

        def over_j(row):
            return row.unsqueeze(1).broadcast_to([P, NJ, row.shape[1]])

        def repeat_weights(copy, half):
            n = NJ * E0 // 2
            return copy(w_exp[:, half * n * R0:(half + 1) * n * R0].rearrange("p (j r) -> p j r", r=R0),
                        w_te[:, half * n:(half + 1) * n].unsqueeze(2).broadcast_to([P, n, R0]))

        h_bank = [bank[0], bank[1], bank[2], bank[7]]
        GU, SGU = 2 * GA_W, 2 * DC * P

        CREDITS = {conv_free: 4, conv_done: 4, y_used: 1, tf_done: 1, x1t_done: 4, x1t_copied: 4, x1tok_ready: 1,
                   x1tok_evac: 2, up_ready: 1, silu_done: 1, prod_done: 1, c_evac: 4, st_split: 4, st_used: 2,
                   sup_ready: 1, ssilu_done: 1, sprod_done: 1, base_done: 4, sw_split: 4,
                   xgT_evac: 2, eh_done: 2, ehT_evac: 1, ys_done: 2}
        CREDITS.update({s: 16 for s in x1_out + y_out})

        block = ctx.enter_context(nc.Block())

        @block.sync
        def _(sp):
            sp.dma_start(par[:, :], s4_par).then_inc(par_in, 16)
            for g in range(NG):
                sp.dma_start(xT[:, g * DC * CH * B:(g + 1) * DC * CH * B], x_heads[g]).then_inc(x_in, 16)
            sp.dma_start(w0_raw[:, :], w0).then_inc(w0_in, 16)
            sp.dma_start(gw1T[:, :], gw1).then_inc(small_in, 16)
            sp.dma_start(gwT[:, :], gw_d).then_inc(small_in, 16)
            sp.dma_start(gb1[:, :], gb1_d.partition_broadcast(P)).then_inc(small_in, 16)
            sp.dma_start(lng[:, :], lng_d.partition_broadcast(P)).then_inc(small_in, 16)
            sp.dma_start(lnb[:, :], lnb_d.partition_broadcast(P)).then_inc(small_in, 16)
            sp.dma_start(gb2[:, :], gb2_d.partition_broadcast(P)).then_inc(small_in, 16)
            sp.wait_ge(const_done, 3)
            for i in range(4):
                sp.dma_start(gw2bd[G0 * i:G0 * (i + 1), E0 * i:E0 * (i + 1)], gw2).then_inc(small_in, 16)
            sp.dma_start(kpad[:, D:KPW], zeros[0:H, :]).then_inc(kpad_out, 16)
            sp.dma_start(st_dram.rearrange("(p b) o -> p (b o)", p=P), zeros[:, 0:NB].bitcast(U32)).then_inc(list_zero, 16)

            sp.wait_ge(k_evac, 2)
            sp.dma_start(kpad[:, 0:D].rearrange("h (q r) -> q h r", q=QL),
                         k_sb[0:QL, :].rearrange("q (h r) -> q h r", h=H)).then_inc(kpad_out, 16)
            sp.wait_ge(kpad_out, 32)
            with sp.Fori(0, NG // 2) as it:
                for u in range(2):
                    sp.wait_ge(conv_done, it * 4 + (2 * u + 2))
                    sp.dma_start(toep[:, u * CH * D:(u + 1) * CH * D].rearrange("p (h i) -> p h i", h=CH),
                                 bass.AP(kpad.tensor, (it * 2 + u) * (CH * KPW), [[1, P], [KPW, CH], [1, D]])
                                 ).then_inc(toep_in[u], 16)
            sp.wait_ge(wT_evac, NT)
            sp.dma_start(la_raw[:, :], w_la).then_inc(la_in, 16)
            sp.dma_start(bd_raw[:, :], w_bd).then_inc(bd_in, 16)
            sp.wait_ge(x1_ready, 4 * NT)
            with sp.Fori(0, NT // 2) as it:
                for s in range(2 * FC):
                    b = s % 2
                    sp.wait_ge(st_split, it * 4 * FC + (2 * s + 2))
                    sp.dma_start(st_raw[:, b * ST_W:(b + 1) * ST_W], w_st[s % FC]).then_inc(st_in[b], 16)
            sp.wait_ge(st_used, NT * FC + 2)
            with sp.Fori(0, NT // 2) as it:
                for s in range(2 * SC):
                    b = s % 2
                    sp.wait_ge(sw_split, it * 4 * SC + (2 * s + 2))
                    sp.dma_start(sw_raw[:, b * SH_W:(b + 1) * SH_W], w_sh[s % SC]).then_inc(sw_in[b], 16)
                    if s % SC == 2:
                        sp.wait_ge(csplit, it * 2 * DC + (s // SC + 1) * DC)
                        sp.dma_start(cT[:, bass.ds((it * 2 + s // SC) * (DC * TW), DC * TW)]
                                     .rearrange("p (s d) -> p s d", s=4),
                                     x1_dram[bass.ds((it * 2 + s // SC) * TW, TW), :]
                                     .rearrange("(s p) d -> p s d", p=P)).then_inc(x1_in, 16)
            with sp.Fori(0, NB // 4) as it:
                for u in range(4):
                    sp.wait_ge(ys_done, it * 4 + (u + 3))
                    sp.dma_start(y_dram[bass.ds((it * 4 + u) * P, P), :], ys[:, u * D:(u + 1) * D]).then_inc(y_out[u], 16)
            for j in range(NJ):
                sp.wait_ge(fma2_done, j + 1)
                sp.dma_start(out[j * P:(j + 1) * P, :], fin[:, (j % 4) * D:(j % 4 + 1) * D]).then_inc(fin_out[j % 4], 16)
            for u in range(4):
                sp.wait_ge(fin_out[u], 16 * NJ // 4)

        @block.gpsimd
        def _(pool):
            g = nc.gpsimd
            allow = dict(allow_small_or_imprecise_dtypes=True)
            for s, n in CREDITS.items():
                pool.sem_inc(s, n)
            count = [0]

            def link(ins):
                count[0] += 1
                ins.then_inc(pool_step, 1)
                pool.wait_ge(pool_step, count[0])

            def fold(t, total):
                w = E1 // 2
                while w > 1:
                    link(g.tensor_tensor(t[:, :, 0:w], t[:, :, 0:w], t[:, :, w:2 * w], ALU.add))
                    w //= 2
                link(g.tensor_tensor(total, t[:, :, 0], t[:, :, 1], ALU.add))

            g.iota(r_iota[:, :], pattern=[[-1, RL]], base=RL - 1, channel_multiplier=0, **allow).then_inc(iota_done, 1)
            g.iota(q_iota[:, :], pattern=[[-RL, QL]], base=RL * (QL - 1), channel_multiplier=0, **allow).then_inc(iota_done, 1)
            g.iota(l_iota[:, :], pattern=[[P, DC]], base=P - 1, channel_multiplier=-1, **allow).then_inc(iota_done, 1)
            g.iota(a_int[:, :], pattern=[[P, AC]], base=0, channel_multiplier=1).then_inc(iota_done, 1)
            pool.wait_ge(iota_done, 4)
            link(g.memset(phase[:, :], 0.0))
            link(g.memset(phase[0:NS, 0:1], 0.25))
            g.memset(phase[0:NS, 1:2], 1.5707963267948966).then_inc(iota_done, 1)
            pool.wait_ge(iota_done, 5)
            link(g.memset(d_pad[0:QL, :], 0.0))
            pool.wait_ge(ids_in, 48)
            link(g.affine_select(out=d_row[0:QL, :], in_=d_row[0:QL, :], compare_op=ALU.is_ge, fill=0.0, base=1 - QL,
                                 pattern=[[0, H]], channel_multiplier=1))
            g.tensor_copy(d_pad[0:QL, :].rearrange("p (h r) -> p h r", h=H)[:, :, RL - 1], d_row[0:QL, :]).then_inc(d_done, 1)
            pool.wait_ge(sin_done, 1)
            pool.wait_ge(dec_done, 1)
            g.tensor_tensor(fine_t[:, :], sn[:, 0:FW], dec[:, 0:FW], ALU.mult).then_inc(table_done, 1)
            link(g.memset(gw2bd[:, :], 0.0))
            pool.sem_inc(const_done, 1)
            link(g.memset(zeros[:, :], 0.0))
            pool.sem_inc(const_done, 2)
            link(g.memset(ident[:, :], 0.0))
            link(g.affine_select(out=ident[:, :], in_=ident[:, :], compare_op=ALU.not_equal, fill=1.0, base=0,
                                 pattern=[[-1, P]], channel_multiplier=1))
            link(g.memset(ones[:, :], 1.0))
            link(g.affine_select(out=before[:, :], in_=ones[:, :], compare_op=ALU.is_gt, fill=0.0, base=0,
                                 pattern=[[1, P]], channel_multiplier=-1))
            link(g.iota(e_iota[:, :], pattern=[[1, E1]], base=0, channel_multiplier=0, **allow))
            link(g.iota(b_iota[:, :], pattern=[[1, NB]], base=0, channel_multiplier=0, **allow))
            link(g.iota(tok_id[:, :], pattern=[[P, NJ]], base=0, channel_multiplier=1))
            pool.sem_inc(const_done, 1)

            for j in range(1, NJ, 2):
                u = j % C_BUF
                pool.wait_ge(ctok_odd, j // 2 + 1)
                g.dma_start(c_dram[j * P:(j + 1) * P, :], c_tok[:, u * D:(u + 1) * D]).then_inc(c_out[u], 16)
            pool.wait_ge(pos_evac, 2)
            src, dst = tot1, sc_a
            for d in (1, 2, 4, 8):
                w = d * E1
                g.tensor_copy(dst[:, 0:w], src[:, 0:w])
                link(g.tensor_tensor(dst[:, w:], src[:, w:], src[:, 0:NJ * E1 - w], ALU.add))
                src, dst = dst, (sc_b if dst is sc_a else sc_a)
            incl = src
            link(g.tensor_tensor(pos1[:, :], pos1[:, :], incl[:, :], ALU.add))
            link(g.tensor_tensor(pos1[:, :], pos1[:, :], tot1[:, :], ALU.subtract))
            cntv = incl[:, (NJ - 1) * E1:NJ * E1]
            nb = [nbk[:, i * E1:(i + 1) * E1] for i in range(8)]
            link(g.tensor_scalar(nb[0], cntv, (P - 1) / 2, 1.0 / P, ALU.add, ALU.mult))
            link(g.tensor_scalar(nb[0], nb[0], MAGIC, None, ALU.add))
            link(g.tensor_scalar(nb[0], nb[0], -MAGIC, None, ALU.add))
            si = 0
            for i, d in enumerate((1, 2, 4, 8)):
                g.tensor_copy(nb[i + 1][:, 0:d], nb[si][:, 0:d])
                link(g.tensor_tensor(nb[i + 1][:, d:], nb[si][:, d:], nb[si][:, 0:E1 - d], ALU.add))
                si = i + 1
            link(g.tensor_tensor(nb[5], nb[4], nb[0], ALU.subtract))
            link(g.tensor_scalar(nb[5], nb[5], float(P), None, ALU.mult))
            link(g.tensor_tensor(h3(pos1[:, :]), h3(pos1[:, :]), over_j(nb[5]), ALU.add))
            for k in range(2):
                link(g.tensor_tensor(ohp[:, k * NJ * E1:(k + 1) * NJ * E1], oh1[:, k * NJ * E1:(k + 1) * NJ * E1],
                                     pos1[:, :], ALU.mult))
            fold(ohp[:, :].rearrange("p (x e) -> p x e", e=E1), slf[:, :])
            link(g.tensor_copy(slot_u[:, :], slf[:, :]))
            link(g.tensor_scalar(slot_b[:, :], slf[:, :], -(P - 1) / 2, 1.0 / P, ALU.add, ALU.mult))
            link(g.tensor_scalar(slot_b[:, :], slot_b[:, :], MAGIC, None, ALU.add))
            link(g.tensor_scalar(slot_b[:, :], slot_b[:, :], -MAGIC, -float(P * NB - 1), ALU.add, ALU.mult))
            link(g.tensor_scalar(slf[:, :], slf[:, :], float(NB), None, ALU.mult))
            link(g.tensor_tensor(slf[:, :], slf[:, :], slot_b[:, :], ALU.add))
            link(g.tensor_copy(list_u[:, :], slf[:, :]))
            pool.wait_ge(list_zero, 16)
            for k in range(2):
                for j in range(NJ):
                    g.indirect_dma_start(out=st_dram, out_offset=bass.IndirectOffsetOnAxis(list_u[:, k * NJ + j:k * NJ + j + 1], 0),
                                         in_=tok_id[:, j:j + 1], in_offset=None,
                                         bounds_check=NB * P - 1).then_inc(list_out, 16)
            link(g.tensor_tensor(bcmp[:, :].rearrange("p (b e) -> p b e", e=E1),
                                 b_iota[:, :].unsqueeze(2).broadcast_to([P, NB, E1]),
                                 nb[4].unsqueeze(1).broadcast_to([P, NB, E1]), ALU.subtract))
            link(g.tensor_scalar(bcmp[:, :], bcmp[:, :], 1.0, 0.0, ALU.add, ALU.max))
            link(g.tensor_scalar(bcmp[:, :], bcmp[:, :], 1.0, None, ALU.min))
            fold(bcmp[:, :].rearrange("p (b e) -> p b e", e=E1), ebf[:, :])
            link(g.tensor_scalar(blk_e[:, :], ebf[:, :], float(E1 - 1), None, ALU.min))
            pool.wait_ge(th1_ready, 1)
            link(g.tensor_scalar(gate1[:, 0:NJ], dl[:, NJ:2 * NJ], 0.5, 0.5, ALU.mult, ALU.add))
            g.tensor_scalar(gate1[:, NJ:2 * NJ], dl[:, NJ:2 * NJ], -0.5, 0.5, ALU.mult, ALU.add).then_inc(blk_ready, 1)
            pool.wait_ge(list_out, 32 * NJ)
            g.dma_start(slot_tok[:, :], st_dram.rearrange("(p b) o -> p (b o)", p=P)).then_inc(list_in, 16)
            pool.wait_ge(blk_ready, 1)
            for i, q in enumerate(c_out):
                pool.wait_ge(q, 16 * len(range(i, NJ, C_BUF)))
            for k in range(ED_PARTS):
                n = E1 * D // ED_PARTS
                pool.wait_ge(sup_ready, (k + 4) * NT * SC // (ED_PARTS + 4))
                g.dma_start(ed[:, k * n:(k + 1) * n], w_ed[:, k * n:(k + 1) * n]).then_inc(ed_in, 16)
            pool.wait_ge(list_in, 16)
            pool.wait_ge(base_done, NJ + 4)
            for b in range(NB):
                if b >= 4:
                    pool.wait_ge(xgT_ready, b - 3)
                g.indirect_dma_start(out=xg[:, (b % 4) * D:(b % 4 + 1) * D], out_offset=None, in_=c_dram,
                                     in_offset=bass.IndirectOffsetOnAxis(slot_tok[:, b:b + 1], 0),
                                     bounds_check=N - 1).then_inc(xg_in[b % 4], 16)
            for q in y_out:
                pool.wait_ge(q, 16 * (NB // 4 + 1))
            for j in range(NJ):
                u = j % 4
                if j >= 4:
                    pool.wait_ge(fma1_done, j - 3)
                g.indirect_dma_start(out=y1[:, u * D:(u + 1) * D], out_offset=None, in_=y_dram,
                                     in_offset=bass.IndirectOffsetOnAxis(slot_u[:, j:j + 1], 0),
                                     bounds_check=NB * P - 1).then_inc(y1_in[u], 16)
                if j >= 4:
                    pool.wait_ge(fma2_done, j - 3)
                g.indirect_dma_start(out=y2[:, u * D:(u + 1) * D], out_offset=None, in_=y_dram,
                                     in_offset=bass.IndirectOffsetOnAxis(slot_u[:, NJ + j:NJ + j + 1], 0),
                                     bounds_check=NB * P - 1).then_inc(y2_in[u], 16)

        @block.scalar
        def _(act):
            a = nc.scalar
            act.dma_start(len_i[:, :], lens.partition_broadcast(P)).then_inc(ids_in, 16)
            act.dma_start(ad_i[:, :], adapters.partition_broadcast(P)).then_inc(ids_in, 16)
            act.dma_start(d_row[0:QL, :], s4_d.partition_broadcast(QL)).then_inc(ids_in, 16)
            act.wait_ge(a_ready, 1)
            a.activation(smv(TANH), smv(AR), ACT.Tanh, scale=0.5).then_inc(tanh_done, 1)
            act.wait_ge(ang_ready, 1)
            a.activation(sn[:, :], ang[:, :], ACT.Sin).then_inc(sin_done, 1)
            a.activation(sh[:, :], ang[:, FW:AW], ACT.Sin, scale=0.5).then_inc(sin_done, 1)
            act.wait_ge(dec_mul, 1)
            a.activation(dec[:, :], dec[:, :], ACT.Exp).then_inc(dec_done, 1)
            act.wait_ge(w0_in, 16)
            a.copy(w0_hi[:, :], w0_raw[:, :]).then_inc(w0_hi_done, 1)
            def split_y(t):
                act.wait_ge(y_used, t + 1)
                for c in range(DC):
                    a.copy(y_hi[:, c * TW:(c + 1) * TW], yT[:, bass.ds(t * TW + c * N, TW)]).then_inc(yhi_done, 1)

            act.wait_ge(conv_free, 2 * NG + 4)
            split_y(0)
            act.wait_ge(var_done, 1)
            a.activation(rsv(SD), rsv(VAR), ACT.Sqrt).then_inc(sqrt_done, 1)
            act.wait_ge(dl_ready, 1)
            a.activation(rsv(TH), rsv(DL), ACT.Tanh, scale=0.5).then_inc(th_ready, 1)
            act.wait_ge(w_ready, 1)
            repeat_weights(a.copy, 1).then_inc(wexp_done, 1)
            for i in range(NT):
                act.wait_ge(wT_ready, i + 1)
                a.copy(wT[:, i * TW:(i + 1) * TW], bank[i % 3][:, :]).then_inc(wT_evac, 1)

            def finish_tile(t):
                act.wait_ge(tf_done, t + 2)
                a.copy(t_hi[:, :], t_f[:, :]).then_inc(thi_done, 1)
                if t is not NT - 1:
                    split_y(t + 1)
                else:
                    act.wait_ge(la_in, 16)
                    a.copy(la_hi[:, :], la_raw[:, :]).then_inc(la_hi_done, 1)
                    act.wait_ge(bd_in, 16)
                    a.copy(bd_hi[:, :], bd_raw[:, :]).then_inc(bd_hi_done, 1)
                for m in range(DC):
                    act.wait_ge(x1t_done, t * 4 + (m + 5))
                    a.copy(x1T[:, bass.ds(t * (DC * TW) + m * TW, TW)], x1_t[:, m * TW:(m + 1) * TW]).then_inc(x1t_copied, 1)
                for s in range(4):
                    act.wait_ge(x1tok_ready, t * 4 + (s + 2))
                    act.wait_ge(x1_out[s], t * 16 + 16)
                    a.copy(x1_tok[:, s * D:(s + 1) * D], bank[s % 2][:, :]).then_inc(x1tok_evac, 1)
                    act.wait_ge(x1tok_evac, t * 4 + (s + 3))
                    act.dma_start(x1_dram[bass.ds(t * TW + s * P, P), :], x1_tok[:, s * D:(s + 1) * D]).then_inc(x1_out[s], 16)

            with act.Fori(0, NT - 1) as t:
                finish_tile(t)
            finish_tile(NT - 1)

            def down_lora_hi(it, u):
                for q in range(AC):
                    act.wait_ge(taf_done, it * (2 * LQ) + (LQ * u + 2 * AC + q + 1))
                    a.copy(td_hi[:, q * TW:(q + 1) * TW], ta_f[:, :]).then_inc(tahi_done, 1)

            def evac_c(it, u):
                for m in range(DC):
                    act.wait_ge(c_ready, it * (2 * DC) + (u * DC + m + 1))
                    a.copy(cT[:, bass.ds((it * 2 + u) * (DC * TW) + m * TW, TW)], bank[m][:, :]).then_inc(c_evac, 1)

            def split_x(t):
                for c in range(DC):
                    a.copy(x_hi[:, c * TW:(c + 1) * TW], x1T[:, bass.ds(t * (DC * TW) + c * TW, TW)]).then_inc(xhi_done, 1)

            def hi_gate_up(it, s):
                b = s % 2
                act.wait_ge(st_in[b], it * (16 * FC) + 16 * (s // 2 + 1))
                act.wait_ge(up_ready, it * (2 * FC) + max(s, 1))
                a.copy(st_hi[:, b * ST_W:b * ST_W + GU], st_raw[:, b * ST_W:b * ST_W + GU]).then_inc(st_hi_done, 1)

            with act.Fori(0, NT // 2) as it:
                for u in range(2):
                    t = it * 2 + u
                    act.wait_ge(up_ready, it * (2 * FC) + (u * FC + 1))
                    split_x(t)
                    if u == 0:
                        hi_gate_up(it, 0)
                    else:
                        down_lora_hi(it, 0)
                        evac_c(it, 0)
                    for q in range(2 * AC):
                        act.wait_ge(taf_done, it * (2 * LQ) + (LQ * u + q + 1))
                        a.copy(ta_hi[:, q * TW:(q + 1) * TW], ta_f[:, :]).then_inc(tahi_done, 1)
                    for f in range(FC):
                        s = u * FC + f
                        b = s % 2
                        act.wait_ge(st_used, it * (2 * FC) + (s + 1))
                        a.copy(st_hi[:, b * ST_W + GU:(b + 1) * ST_W],
                               st_raw[:, b * ST_W + GU:(b + 1) * ST_W]).then_inc(st_hi_done, 1)
                        act.wait_ge(gate_ready, it * (2 * FC) + (s + 1))
                        act.wait_ge(prod_done, it * (2 * FC) + (s + 1))
                        a.activation(silu_s[:, :], bank[6][:, :], ACT.Silu).then_inc(silu_done, 1)
                        if s + 1 < 2 * FC:
                            hi_gate_up(it, s + 1)
                        act.wait_ge(prod_done, it * (2 * FC) + (s + 2))
                        a.copy(act_hi[:, b * TW:(b + 1) * TW], prod_s[:, :]).then_inc(acthi_done, 1)
                down_lora_hi(it, 1)
                evac_c(it, 1)

            for j in range(0, NJ, 2):
                u = j % C_BUF
                if j == 8:
                    act.wait_ge(dl1_ready, 1)
                    a.activation(dl[:, NJ:2 * NJ], dl[:, 0:NJ], ACT.Tanh, scale=0.5).then_inc(th1_ready, 1)
                act.wait_ge(ctok_ready, j + 1)
                if j >= C_BUF:
                    act.wait_ge(c_out[u], 16 * (j // C_BUF))
                a.copy(c_tok[:, u * D:(u + 1) * D], bank[1 + j % 6][:, :]).then_inc(ctok_even, 1)
                act.wait_ge(ctok_even, j // 2 + 1)
                act.dma_start(c_dram[j * P:(j + 1) * P, :], c_tok[:, u * D:(u + 1) * D]).then_inc(c_out[u], 16)
            def shared_hi_gate_up(it, s):
                b = s % 2
                act.wait_ge(sw_in[b], it * (16 * SC) + 16 * (s // 2 + 1))
                act.wait_ge(sup_ready, it * (2 * SC) + max(s, 1))
                a.copy(sw_hi[:, b * SH_W:b * SH_W + SGU], sw_raw[:, b * SH_W:b * SH_W + SGU]).then_inc(sw_hi_done, 1)

            with act.Fori(0, NT // 2) as it:
                shared_hi_gate_up(it, 0)
                for u in range(2):
                    t = it * 2 + u
                    act.wait_ge(sup_ready, it * (2 * SC) + (u * SC + 1))
                    for c in range(DC):
                        a.copy(x_hi[:, c * TW:(c + 1) * TW], cT[:, bass.ds(t * (DC * TW) + c * TW, TW)]).then_inc(chi_done, 1)
                    for i in range(SC):
                        s = u * SC + i
                        b = s % 2
                        part = E1 * DC * 2 * I1 // EG_PARTS
                        eg_part = bass.ds(it * (2 * SC * part) + s * part, part)
                        act.dma_start(eg[:, eg_part], w_eg[:, eg_part]).then_inc(eg_in, 16)
                        act.wait_ge(sgate_ready, it * (2 * SC) + (s + 1))
                        act.wait_ge(sprod_done, it * (2 * SC) + (s + 1))
                        if s == 0:
                            for j, q in enumerate(c_out):
                                act.wait_ge(q, 16 * len(range(j, NJ, C_BUF)))
                        a.activation(silu_s[:, :], bank[4][:, :], ACT.Silu).then_inc(ssilu_done, 1)
                        a.copy(sw_hi[:, b * SH_W + SGU:(b + 1) * SH_W],
                               sw_raw[:, b * SH_W + SGU:(b + 1) * SH_W]).then_inc(sw_hi_done, 1)
                        if s + 1 < 2 * SC:
                            shared_hi_gate_up(it, s + 1)
                        act.wait_ge(sprod_done, it * (2 * SC) + (s + 2))
                        a.copy(act_hi[:, b * TW:(b + 1) * TW], prod_s[:, :]).then_inc(sacthi_done, 1)

            def evac_x(b4, u, k):
                act.wait_ge(xgT_ready, b4 + (u + 1))
                a.copy(xgT[:, (u % 4) * D:(u % 4 + 1) * D], bank[u % 2][:, :]).then_inc(xgT_evac, 1)

            def silu_e(b4, u):
                act.wait_ge(egu_ready, b4 + (u + 1))
                a.activation(es[:, (u % 4) * I1:(u % 4 + 1) * I1], bank[2 + u % 2][:, 0:I1], ACT.Silu).then_inc(es_done, 1)

            evac_x(0, 0, 0)
            evac_x(0, 1, 0)
            silu_e(0, 0)
            with act.Fori(0, NB // 4 - 1) as it:
                for u in range(4):
                    evac_x(it * 4, u + 2, 1)
                    silu_e(it * 4, u + 1)
            for u in range(4):
                if u < 2:
                    evac_x(NB - 4, u + 2, 1)
                if u < 3:
                    silu_e(NB - 4, u + 1)

        @block.vector
        def _(dve):
            v = nc.vector
            count = [0]

            def link(ins):
                count[0] += 1
                ins.then_inc(dve_step, 1)
                dve.wait_ge(dve_step, count[0])

            W = 2 * H
            dve.wait_ge(par_in, 16)
            kf, rr, pp = smv(KF, W), smv(RR, W), smv(PP, W)
            link(v.tensor_scalar(kf, lg, LOG2E, MAGIC, ALU.mult, ALU.add))
            link(v.tensor_scalar(kf, kf, -MAGIC, -126.0, ALU.add, ALU.max))
            link(v.scalar_tensor_tensor(out=rr, in0=kf, scalar=-LN2_HI, in1=lg, op0=ALU.mult, op1=ALU.add))
            link(v.scalar_tensor_tensor(out=rr, in0=kf, scalar=-LN2_LO, in1=rr, op0=ALU.mult, op1=ALU.add))
            link(v.tensor_scalar(pp, rr, 1.0 / 5040, None, ALU.mult))
            for c in (1.0 / 720, 1.0 / 120, 1.0 / 24, 1.0 / 6, 0.5, 1.0):
                link(v.scalar_tensor_tensor(out=pp, in0=pp, scalar=c, in1=rr, op0=ALU.add, op1=ALU.mult))
            link(v.tensor_scalar(kx[:, :], kf, 127.0, None, ALU.add))
            link(v.tensor_scalar(kx[:, :], kx[:, :], 23, None, ALU.logical_shift_left))
            link(v.scalar_tensor_tensor(out=pp, in0=pp, scalar=1.0, in1=kx[:, :].bitcast(F32), op0=ALU.add, op1=ALU.mult))
            dt, a_re = pp[:, 0:H], pp[:, H:W]
            link(v.scalar_tensor_tensor(out=smv(AR), in0=dt, scalar=-1.0, in1=a_re, op0=ALU.mult, op1=ALU.mult))
            v.tensor_tensor(smv(BR), dt, ai, ALU.mult).then_inc(a_ready, 1)
            dve.wait_ge(a_ready, 1)
            dve.wait_ge(iota_done, 5)
            br = smv(BR)
            v.tensor_tensor(fine(ang), over_lags(br, RL), over_heads(r_iota[:, :]), ALU.mult)
            v.tensor_tensor(crs(ang, FW), over_lags(br, QL), over_heads(q_iota[:, :]), ALU.mult)
            link(v.tensor_copy(ang[:, FW + CW:AW], br))
            v.tensor_scalar(turn[:, 0:FW], ang[:, 0:FW], 1.0 / 6.283185307179586, phase[:, 0:1], ALU.mult, ALU.add)
            link(v.tensor_scalar(turn[:, FW:AW], ang[:, FW:AW], 1.0 / 6.283185307179586, None, ALU.mult))
            link(v.tensor_scalar(turn[:, :], turn[:, :], MAGIC, -MAGIC, ALU.add, ALU.add))
            link(v.scalar_tensor_tensor(out=ang[:, :], in0=turn[:, :], scalar=-TWO_PI_HI, in1=ang[:, :], op0=ALU.mult, op1=ALU.add))
            link(v.scalar_tensor_tensor(out=ang[:, :], in0=turn[:, :], scalar=-TWO_PI_LO, in1=ang[:, :], op0=ALU.mult, op1=ALU.add))
            link(v.tensor_scalar(ang[:, 0:FW], ang[:, 0:FW], phase[:, 1:2], None, ALU.add))
            v.tensor_scalar(ang[:, :], ang[:, :], PI_DOWN, -PI_DOWN, ALU.min, ALU.max).then_inc(ang_ready, 1)
            v.tensor_tensor(fine(dec), over_lags(smv(AR), RL), over_heads(r_iota[:, :]), ALU.mult)
            v.tensor_tensor(crs(dec, FW), over_lags(smv(AR), QL), over_heads(q_iota[:, :]), ALU.mult).then_inc(dec_mul, 1)
            link(v.tensor_tensor(smv(T0), a_re, a_re, ALU.mult))
            link(v.tensor_tensor(smv(T1), ai, ai, ALU.mult))
            link(v.tensor_tensor(smv(T0), smv(T0), smv(T1), ALU.add))
            link(v.reciprocal(smv(IA), smv(T0)))
            link(v.tensor_tensor(smv(T0), ci, ai, ALU.mult))
            link(v.tensor_tensor(smv(T1), cr, a_re, ALU.mult))
            link(v.tensor_tensor(smv(T0), smv(T0), smv(T1), ALU.subtract))
            link(v.scalar_tensor_tensor(out=smv(QR), in0=smv(T0), scalar=2.0, in1=smv(IA), op0=ALU.mult, op1=ALU.mult))
            link(v.tensor_tensor(smv(T0), cr, ai, ALU.mult))
            link(v.tensor_tensor(smv(T1), ci, a_re, ALU.mult))
            link(v.tensor_tensor(smv(T0), smv(T0), smv(T1), ALU.add))
            link(v.scalar_tensor_tensor(out=smv(QI), in0=smv(T0), scalar=-2.0, in1=smv(IA), op0=ALU.mult, op1=ALU.mult))
            dve.wait_ge(tanh_done, 1)
            link(v.tensor_scalar(smv(T0), smv(TANH), -1.0, 1.0, ALU.mult, ALU.add))
            link(v.reciprocal(smv(T1), smv(T0)))
            link(v.scalar_tensor_tensor(out=smv(EM), in0=smv(TANH), scalar=2.0, in1=smv(T1), op0=ALU.mult, op1=ALU.mult))
            dve.wait_ge(sin_done, 2)
            shb, snb = sh[:, CW:CW + H], sn[:, FW + CW:AW]
            link(v.tensor_tensor(smv(T0), shb, shb, ALU.mult))
            link(v.tensor_scalar(smv(CB), smv(T0), -2.0, 1.0, ALU.mult, ALU.add))
            link(v.tensor_tensor(smv(T1), smv(EM), smv(CB), ALU.mult))
            link(v.scalar_tensor_tensor(out=smv(ER), in0=smv(T0), scalar=-2.0, in1=smv(T1), op0=ALU.mult, op1=ALU.add))
            link(v.scalar_tensor_tensor(out=smv(EI), in0=smv(EM), scalar=1.0, in1=snb, op0=ALU.add, op1=ALU.mult))
            v.tensor_tensor(smv(T0), smv(QR), smv(ER), ALU.mult)
            link(v.tensor_tensor(smv(T1), smv(QI), smv(EI), ALU.mult))
            v.tensor_tensor(smv(T2), smv(QR), smv(EI), ALU.mult)
            link(v.tensor_tensor(smv(CB), smv(QI), smv(ER), ALU.mult))
            v.tensor_tensor(smv(SR), smv(T0), smv(T1), ALU.subtract)
            link(v.tensor_tensor(smv(SI), smv(T2), smv(CB), ALU.add))
            lo, hi = slice(0, NS), slice(NS, P)
            csr, csi = sm[:, 2 * H * SR:2 * H * SR + H], sm[:, 2 * H * SI:2 * H * SI + H]
            v.tensor_copy(uu[lo, :], csr[lo, :])
            v.tensor_scalar(uu[hi, :], csi[hi, :], -1.0, None, ALU.mult)
            v.tensor_scalar(vv[lo, :], csi[lo, :], -1.0, None, ALU.mult)
            link(v.tensor_scalar(vv[hi, :], csr[hi, :], -1.0, None, ALU.mult))
            dve.wait_ge(dec_done, 1)
            link(v.tensor_tensor(coarse[:, :], sh[:, 0:CW], sh[:, 0:CW], ALU.mult))
            link(v.tensor_scalar(coarse[:, :], coarse[:, :], -2.0, 1.0, ALU.mult, ALU.add))
            link(v.tensor_tensor(crs(coarse), crs(coarse), over_lags(uu[:, :], QL), ALU.mult))
            link(v.tensor_tensor(crs(coarse_b), crs(sn, FW), over_lags(vv[:, :], QL), ALU.mult))
            link(v.tensor_tensor(coarse[:, :], coarse[:, :], coarse_b[:, :], ALU.add))
            v.tensor_tensor(coarse[:, :], coarse[:, :], dec[:, FW:FW + CW], ALU.mult).then_inc(table_done, 1)
            dve.wait_ge(ids_in, 48)
            link(v.tensor_copy(len_f[:, :], len_i[:, :]))
            for m in range(DC):
                link(v.tensor_scalar(mask_len[:, m * B:(m + 1) * B], len_f[:, :], l_iota[:, m:m + 1], None, ALU.is_gt))
            link(v.tensor_copy(ad_f[:, :], ad_i[:, :]))
            link(v.tensor_scalar(a_int[:, :], a_int[:, :], 4, None, ALU.logical_shift_right))
            link(v.tensor_copy(a_iota[:, :], a_int[:, :]))
            for m in range(AC):
                link(v.tensor_scalar(mask_ad[:, m * B:(m + 1) * B], ad_f[:, :], a_iota[:, m:m + 1], 0.5, ALU.is_equal, ALU.mult))
            dve.wait_ge(d_done, 1)
            for i in range(2):
                dve.wait_ge(k_ready, i + 1)
                v.tensor_tensor(k_sb[0:QL, i * 512:(i + 1) * 512], bank[i][0:QL, :], d_pad[0:QL, i * 512:(i + 1) * 512],
                                ALU.add).then_inc(k_evac, 1)
            dve.wait_ge(w0_hi_done, 1)
            v.tensor_tensor(w0_lo[:, :], w0_raw[:, :], w0_hi[:, :].bitcast(F32), ALU.subtract).then_inc(w0_split, 1)

            mask_h = mask_len[:, :].rearrange("p (m b) -> p m b", m=DC).unsqueeze(1).broadcast_to([P, 2, DC, B])
            y_heads = yT[:, :].rearrange("p (m b h) -> p h m b", m=DC, b=B)
            with dve.Fori(0, NG // 2) as it:
                for u in range(2):
                    for pr in range(2):
                        dve.wait_ge(conv_done, it * 4 + (2 * u + pr + 5))
                        v.tensor_tensor(y_heads[:, bass.ds(it * (2 * CH) + (u * CH + 2 * pr), 2), :, :],
                                        bank[2 * u + pr][:, :].rearrange("p (h m b) -> p h m b", h=2, m=DC), mask_h,
                                        ALU.mult).then_inc(conv_free, 1)

            def split_y(t):
                for c in range(DC):
                    cs = slice(c * TW, (c + 1) * TW)
                    dve.wait_ge(yhi_done, t * DC + (c + 1))
                    v.tensor_tensor(y_lo[:, cs], yT[:, bass.ds(t * TW + c * N, TW)], y_hi[:, cs].bitcast(F32),
                                    ALU.subtract).then_inc(ysplit, 1)

            for t in range(NT):
                dve.wait_ge(hf_ready, t + 1)
                v.tensor_copy(hf[0:G0, t * TW:(t + 1) * TW], h_bank[t][0:G0, :]).then_inc(hf_evac, 1)
                if t == 0:
                    split_y(0)

            dve.wait_ge(small_in, 16 * SMALL_LOADS)
            dve.wait_ge(h_ready, 1)
            link(v.tensor_tensor(h3(hh[:, :]), h3(bank[0][:, :]), over_j(gb1[:, :]), ALU.add))
            link(v.tensor_reduce(rsv(MU), h3(hh[:, :]), AX_X, ALU.add))
            link(v.tensor_scalar(rsv(MU), rsv(MU), 1.0 / G0, None, ALU.mult))
            link(v.tensor_tensor(h3(hh[:, :]), h3(hh[:, :]), over_k(rsv(MU), G0), ALU.subtract))
            link(v.tensor_tensor(hq[:, :], hh[:, :], hh[:, :], ALU.mult))
            link(v.tensor_reduce(rsv(VAR), h3(hq[:, :]), AX_X, ALU.add))
            v.tensor_scalar(rsv(VAR), rsv(VAR), 1.0 / G0, 1e-5, ALU.mult, ALU.add).then_inc(var_done, 1)
            dve.wait_ge(sqrt_done, 1)
            link(v.reciprocal(rsv(RC), rsv(SD)))
            link(v.tensor_tensor(rsv(T3), rsv(RC), rsv(RC), ALU.mult))
            link(v.tensor_tensor(rsv(T3), rsv(T3), rsv(VAR), ALU.mult))
            link(v.tensor_scalar(rsv(T3), rsv(T3), -0.5, 1.5, ALU.mult, ALU.add))
            link(v.tensor_tensor(rsv(RC), rsv(RC), rsv(T3), ALU.mult))
            link(v.tensor_tensor(h3(hh[:, :]), h3(hh[:, :]), over_k(rsv(RC), G0), ALU.mult))
            link(v.tensor_tensor(h3(hh[:, :]), h3(hh[:, :]), over_j(lng[:, :]), ALU.mult))
            link(v.tensor_tensor(h3(hh[:, :]), h3(hh[:, :]), over_j(lnb[:, :]), ALU.add))
            v.tensor_scalar(hh[:, :], hh[:, :], 0.0, None, ALU.max).then_inc(h_norm, 1)
            dve.wait_ge(hT_ready, 1)
            v.tensor_copy(hT[:, :], bank[1][:, :]).then_inc(hT_evac, 1)
            dve.wait_ge(g_ready, 1)
            link(v.tensor_tensor(h3(ga[:, :]), h3(bank[2][:, 0:NJ * E0]), over_j(gb2[:, :]), ALU.add))
            for j in range(NJ):
                last = v.max(mv[:, 8 * j:8 * j + 8], ga[:, E0 * j:E0 * j + E0])
            link(last)
            for j in range(NJ):
                last = v.max_index(mi[:, 8 * j:8 * j + 8], mv[:, 8 * j:8 * j + 8], ga[:, E0 * j:E0 * j + E0])
            link(last)
            mv3 = mv[:, :].rearrange("p (j k) -> p k j", k=8)
            link(v.tensor_copy(i2[:, :].rearrange("p (k j) -> p k j", k=2),
                               mi[:, :].rearrange("p (j k) -> p k j", k=8)[:, 0:2, :]))
            v.tensor_tensor(rsv(DL), mv3[:, 0, :], mv3[:, 1, :], ALU.subtract).then_inc(dl_ready, 1)
            v.tensor_tensor(oh[:, :].rearrange("p (x e) -> p x e", e=E0),
                            i2[:, :].unsqueeze(2).broadcast_to([P, 2 * NJ, E0]),
                            e_iota[:, 0:E0].unsqueeze(1).broadcast_to([P, 2 * NJ, E0]), ALU.is_equal).then_inc(oh_ready, 1)
            dve.wait_ge(th_ready, 1)
            dve.wait_ge(oh_ready, 1)
            link(v.tensor_scalar(i2[:, 0:NJ], rsv(TH), 0.5, 0.5, ALU.mult, ALU.add))
            link(v.tensor_scalar(i2[:, NJ:2 * NJ], rsv(TH), -0.5, 0.5, ALU.mult, ALU.add))
            link(v.tensor_tensor(wk[:, :].rearrange("p (x e) -> p x e", e=E0), oh[:, :].rearrange("p (x e) -> p x e", e=E0),
                                 i2[:, :].unsqueeze(2).broadcast_to([P, 2 * NJ, E0]), ALU.mult))
            dve.wait_ge(cnt_ready, 1)
            link(v.tensor_reduce(cn[:, :].rearrange("p (k e) -> p k e", k=2),
                                 bank[2][:, NJ * E0:3 * NJ * E0].rearrange("p (k j e) -> p k e j", k=2, j=NJ), AX_X, ALU.add))
            link(v.tensor_scalar(cn[:, :], cn[:, :], float(CAP0), 1.0 / R0, ALU.is_le, ALU.mult))
            for k in range(2):
                wk_k = h3(wk[:, k * NJ * E0:(k + 1) * NJ * E0])
                link(v.tensor_tensor(wk_k, wk_k, over_j(cn[:, k * E0:(k + 1) * E0]), ALU.mult))
            v.tensor_tensor(w_te[:, :], wk[:, 0:NJ * E0], wk[:, NJ * E0:2 * NJ * E0], ALU.add).then_inc(w_ready, 1)
            dve.wait_ge(w_ready, 1)
            repeat_weights(v.tensor_copy, 0).then_inc(wexp_done, 1)

            xh = xT[:, :].rearrange("p (g c h b) -> p g c h b", g=NG, c=DC, h=CH)

            def finish_tile(t):
                dve.wait_ge(t_ready, t + 1)
                v.tensor_tensor(t_f[:, :], bank[3][:, :], wT[:, bass.ds(t * TW, TW)], ALU.mult).then_inc(tf_done, 1)
                dve.wait_ge(thi_done, t + 1)
                v.tensor_tensor(t_lo[:, :], t_f[:, :], t_hi[:, :].bitcast(F32), ALU.subtract).then_inc(tsplit, 1)
                if t is not NT - 1:
                    split_y(t + 1)
                else:
                    dve.wait_ge(la_hi_done, 1)
                    v.tensor_tensor(la_lo[:, :], la_raw[:, :], la_hi[:, :].bitcast(F32), ALU.subtract).then_inc(la_split, 1)
                    dve.wait_ge(bd_hi_done, 1)
                    v.tensor_tensor(bd_lo[:, :], bd_raw[:, :], bd_hi[:, :].bitcast(F32), ALU.subtract).then_inc(bd_split, 1)
                dve.wait_ge(x1tok_ready, t * 4 + 1)
                for m in range(DC):
                    dve.wait_ge(x1_ready, t * DC + (m + 1))
                    dve.wait_ge(x1t_copied, t * DC + (m + 1))
                    v.tensor_tensor(x1_t[:, m * TW:(m + 1) * TW].rearrange("p (b g h) -> p b g h", g=NG, h=CH),
                                    bank[4 + m][:, :].rearrange("p (b g h) -> p b g h", g=NG, h=CH),
                                    xh[:, :, m, :, bass.ds(t * BT, BT)].rearrange("p g h b -> p b g h"),
                                    ALU.add).then_inc(x1t_done, 1)

            dve.wait_ge(wT_evac, NT)
            with dve.Fori(0, NT - 1) as t:
                finish_tile(t)
            finish_tile(NT - 1)

            def mask_lora(it, u, q, src):
                m = mask_ad[:, bass.ds(it * (2 * BT) + ((q % AC) * B + u * BT), BT)]
                v.tensor_tensor(ta_f[:, :].rearrange("p (b h) -> p b h", b=BT), src[:, :].rearrange("p (b h) -> p b h", b=BT),
                                m.unsqueeze(2).broadcast_to([P, BT, H]), ALU.mult).then_inc(taf_done, 1)

            def lora_lo(it, u, q, dst, hi_part):
                dve.wait_ge(tahi_done, it * (2 * LQ) + (LQ * u + q + 1))
                v.tensor_tensor(dst, ta_f[:, :], hi_part.bitcast(F32), ALU.subtract).then_inc(ta_split, 1)
                dve.wait_ge(ta_split, it * (2 * LQ) + (LQ * u + q + 1))

            def down_lora(it, u):
                for q in range(AC):
                    dve.wait_ge(td_ready, it * (2 * AC) + (u * AC + q + 1))
                    mask_lora(it, u, q, bank[4 + q])
                    lora_lo(it, u, 2 * AC + q, td_lo[:, q * TW:(q + 1) * TW], td_hi[:, q * TW:(q + 1) * TW])

            def lo_part(it, s, part, w):
                b = s % 2
                sl = slice(b * ST_W, b * ST_W + GU) if part == 0 else slice(b * ST_W + GU, (b + 1) * ST_W)
                n = 2 * s + part + 1
                dve.wait_ge(st_hi_done, it * (4 * FC) + n)
                v.tensor_tensor(st_lo[:, sl], st_raw[:, sl], st_hi[:, sl].bitcast(F32), ALU.subtract).then_inc(st_split, 1)

            TA_BANK = [bank[4], bank[5], bank[0], bank[1]]
            with dve.Fori(0, NT // 2) as it:
                for u in range(2):
                    t = it * 2 + u
                    for c in range(DC):
                        cs = slice(c * TW, (c + 1) * TW)
                        dve.wait_ge(xhi_done, t * DC + (c + 1))
                        v.tensor_tensor(x_lo[:, cs], x1T[:, bass.ds(t * (DC * TW) + c * TW, TW)], x_hi[:, cs].bitcast(F32),
                                        ALU.subtract).then_inc(xsplit, 1)
                    if u == 0:
                        for q in x1_out:
                            dve.wait_ge(q, 16 * NT + 16)
                        lo_part(it, 0, 0, 0)
                    else:
                        down_lora(it, 0)
                    for q in range(2 * AC):
                        dve.wait_ge(ta_ready, it * (4 * AC) + (2 * AC * u + q + 1))
                        mask_lora(it, u, q, TA_BANK[q])
                        lora_lo(it, u, q, ta_lo[:, q * TW:(q + 1) * TW], ta_hi[:, q * TW:(q + 1) * TW])
                    for f in range(FC):
                        s = u * FC + f
                        b = s % 2
                        lo_part(it, s, 1, 0)
                        if s + 1 < 2 * FC:
                            lo_part(it, s + 1, 0, 0)
                        dve.wait_ge(up_ready, it * (2 * FC) + (s + 2))
                        dve.wait_ge(silu_done, it * (2 * FC) + (s + 2))
                        v.tensor_tensor(prod_s[:, :], bank[7][:, :], silu_s[:, :], ALU.mult).then_inc(prod_done, 1)
                        dve.wait_ge(acthi_done, it * (2 * FC) + (s + 1))
                        v.tensor_tensor(act_lo[:, b * TW:(b + 1) * TW], prod_s[:, :], act_hi[:, b * TW:(b + 1) * TW].bitcast(F32),
                                        ALU.subtract).then_inc(act_split, 1)
                        dve.wait_ge(act_split, it * (2 * FC) + (s + 1))
                down_lora(it, 1)

            for t in range(NT):
                dve.wait_ge(lf_ready, t + 1)
                v.tensor_copy(lf[0:E1, t * TW:(t + 1) * TW], bank[2 + t][0:E1, :]).then_inc(lf_evac, 1)
            dve.wait_ge(lgt_ready, 1)
            link(v.tensor_copy(lgt[:, :], bank[0][:, 0:NJ * E1]))
            for j in range(NJ):
                last = v.max(mv1[:, 8 * j:8 * j + 8], lgt[:, E1 * j:E1 * j + E1])
            link(last)
            for j in range(NJ):
                last = v.max_index(mi1[:, 8 * j:8 * j + 8], mv1[:, 8 * j:8 * j + 8], lgt[:, E1 * j:E1 * j + E1])
            link(last)
            link(v.tensor_copy(j2[:, :].rearrange("p (k j) -> p k j", k=2),
                               mi1[:, :].rearrange("p (j k) -> p k j", k=8)[:, 0:2, :]))
            link(v.tensor_tensor(oh1[:, :].rearrange("p (x e) -> p x e", e=E1),
                                 j2[:, :].unsqueeze(2).broadcast_to([P, 2 * NJ, E1]),
                                 e_iota[:, :].unsqueeze(1).broadcast_to([P, 2 * NJ, E1]), ALU.is_equal))
            v.tensor_tensor(ohs[:, :], oh1[:, 0:NJ * E1], oh1[:, NJ * E1:2 * NJ * E1], ALU.add).then_inc(ohs_ready, 1)
            mv4 = mv1[:, :].rearrange("p (j k) -> p k j", k=8)
            v.tensor_tensor(dl[:, 0:NJ], mv4[:, 0, :], mv4[:, 1, :], ALU.subtract).then_inc(dl1_ready, 1)
            for j in range(1, NJ, 2):
                u = j % C_BUF
                dve.wait_ge(ctok_ready, j + 1)
                if j >= C_BUF:
                    dve.wait_ge(c_out[u], 16 * (j // C_BUF))
                v.tensor_copy(c_tok[:, u * D:(u + 1) * D], bank[1 + j % 6][:, :]).then_inc(ctok_odd, 1)
            dve.wait_ge(pos_ready, 2)
            for which, dst in ((0, pos1), (1, tot1)):
                v.tensor_copy(dst[:, :], bank[7][:, which * NJ * E1:(which + 1) * NJ * E1]).then_inc(pos_evac, 1)
            def shared_lo(it, s, part):
                b = s % 2
                sl = slice(b * SH_W, b * SH_W + SGU) if part == 0 else slice(b * SH_W + SGU, (b + 1) * SH_W)
                dve.wait_ge(sw_hi_done, it * (4 * SC) + (2 * s + part + 1))
                v.tensor_tensor(sw_lo[:, sl], sw_raw[:, sl], sw_hi[:, sl].bitcast(F32), ALU.subtract).then_inc(sw_split, 1)

            def shared_base(it, u, r):
                j = (it * 2 + u) * 4
                dve.wait_ge(x1_in, (it * 2 + u) * 16 + 16)
                dve.wait_ge(base_ready, j + (r + 1))
                row = cT[:, bass.ds(j * D + r * D, D)]
                v.tensor_tensor(row, bank[r][:, :], row, ALU.add).then_inc(base_done, 1)

            with dve.Fori(0, NT // 2) as it:
                shared_lo(it, 0, 0)
                for u in range(2):
                    t = it * 2 + u
                    for c in range(DC):
                        cs = slice(c * TW, (c + 1) * TW)
                        dve.wait_ge(chi_done, t * DC + (c + 1))
                        v.tensor_tensor(x_lo[:, cs], cT[:, bass.ds(t * (DC * TW) + c * TW, TW)], x_hi[:, cs].bitcast(F32),
                                        ALU.subtract).then_inc(csplit, 1)
                    if u == 1:
                        for s in range(4):
                            shared_base(it, 0, s)
                    for i in range(SC):
                        s = u * SC + i
                        b = s % 2
                        shared_lo(it, s, 1)
                        if s + 1 < 2 * SC:
                            shared_lo(it, s + 1, 0)
                        dve.wait_ge(sup_ready, it * (2 * SC) + (s + 2))
                        dve.wait_ge(ssilu_done, it * (2 * SC) + (s + 2))
                        v.tensor_tensor(prod_s[:, :], bank[5][:, :], silu_s[:, :], ALU.mult).then_inc(sprod_done, 1)
                        dve.wait_ge(sacthi_done, it * (2 * SC) + (s + 1))
                        v.tensor_tensor(act_lo[:, b * TW:(b + 1) * TW], prod_s[:, :], act_hi[:, b * TW:(b + 1) * TW].bitcast(F32),
                                        ALU.subtract).then_inc(sact_split, 1)
                        dve.wait_ge(sact_split, it * (2 * SC) + (s + 1))
                for s in range(4):
                    shared_base(it, 1, s)

            def act_e(b4, u):
                q = u % 4
                dve.wait_ge(es_done, b4 + (u + 1))
                v.tensor_tensor(eh[:, q * I1:(q + 1) * I1], bank[2 + u % 2][:, I1:2 * I1], es[:, q * I1:(q + 1) * I1],
                                ALU.mult).then_inc(eh_done, 1)

            def step_e(b4, u, bd4, nxt):
                q = u % 4
                dve.wait_ge(ehT_ready, b4 + (u + 1))
                v.tensor_copy(ehT[:, q * P:(q + 1) * P], bank[4][:, 0:P]).then_inc(ehT_evac, 1)
                if nxt:
                    act_e(b4, u + 1)
                dve.wait_ge(ey_ready, b4 + (u + 1))
                dve.wait_ge(y_out[q], bd4 + 16)
                v.tensor_copy(ys[:, q * D:(q + 1) * D], bank[5 + u % 2][:, :]).then_inc(ys_done, 1)

            act_e(0, 0)
            with dve.Fori(0, NB // 4 - 1) as it:
                for u in range(4):
                    step_e(it * 4, u, it * 16, True)
            for u in range(4):
                step_e(NB - 4, u, 16 * (NB // 4 - 1), u < 3)

            for j in range(NJ):
                u = j % 4
                us = slice(u * D, (u + 1) * D)
                dve.wait_ge(y1_in[u], 16 * (j // 4 + 1))
                if j >= 4:
                    dve.wait_ge(fin_out[u], 16 * (j // 4))
                v.scalar_tensor_tensor(out=fin[:, us], in0=y1[:, us], scalar=gate1[:, j:j + 1],
                                       in1=cT[:, j * D:(j + 1) * D], op0=ALU.mult, op1=ALU.add).then_inc(fma1_done, 1)
                dve.wait_ge(fma1_done, j + 1)
                dve.wait_ge(y2_in[u], 16 * (j // 4 + 1))
                v.scalar_tensor_tensor(out=fin[:, us], in0=y2[:, us], scalar=gate1[:, NJ + j:NJ + j + 1],
                                       in1=fin[:, us], op0=ALU.mult, op1=ALU.add).then_inc(fma2_done, 1)

        @block.tensor
        def _(pe):
            mm = nc.tensor.matmul

            def split3(o, w_hi, w_lo, x_hi_, x_lo_, start, stop):
                mm(o, w_hi, x_hi_, start=start, stop=False)
                mm(o, w_hi, x_lo_, start=False, stop=False)
                return mm(o, w_lo, x_hi_, start=False, stop=stop)

            pe.wait_ge(table_done, 2)
            for h in range(H):
                i, c = h // (H // 2), (h % (H // 2)) * RL
                last = mm(bank[i][0:QL, c:c + RL], coarse[:, h * QL:(h + 1) * QL], fine_t[:, h * RL:(h + 1) * RL],
                          start=True, stop=True)
                if h % (H // 2) == H // 2 - 1:
                    last.then_inc(k_ready, 1)

            x5 = xT[:, :].rearrange("p (g c h b) -> p g c h b", g=NG, c=DC, h=CH)
            pe.wait_ge(k_evac, 2)
            pe.wait_ge(x_in, 16 * NG)
            with pe.Fori(0, NG // 2) as it:
                for u in range(2):
                    pe.wait_ge(toep_in[u], it * 16 + 16)
                    for pr in range(2):
                        pe.wait_ge(conv_free, it * 4 + (2 * u + pr + 1))
                        for h2 in range(2):
                            hh_ = 2 * pr + h2
                            for d in range(DC):
                                i0 = (u * CH + hh_) * D + D - P * (d + 1)
                                last = mm(bank[2 * u + pr][:, h2 * DC * B + d * B:(h2 + 1) * DC * B],
                                          toep[:, i0:i0 + P], x5[:, bass.ds(it * 2 + u, 1), 0:DC - d, hh_, :],
                                          start=(d == 0), stop=(d == DC - 1), skip_group_check=True)
                        last.then_inc(conv_done, 1)

            pe.wait_ge(conv_free, 2 * NG + 4)
            pe.wait_ge(small_in, 16 * SMALL_LOADS)
            for t in range(NT):
                for m in range(DC):
                    last = mm(h_bank[t][0:G0, :], gw1T[:, m * G0:(m + 1) * G0], yT[:, m * N + t * TW:m * N + (t + 1) * TW],
                              start=(m == 0), stop=(m == DC - 1))
                last.then_inc(hf_ready, 1)

            def w0m(part, c, m):
                return part[:, c * D + m * P:c * D + (m + 1) * P]

            A0, B0 = DC * D, DC * D + DC * P

            def lora_a0(t):
                pe.wait_ge(tf_done, t + 1)
                for c in range(DC):
                    cs = slice(c * TW, (c + 1) * TW)
                    pe.wait_ge(ysplit, t * DC + (c + 1))
                    last = split3(bank[3][:, :], w0_hi[:, A0 + c * P:A0 + (c + 1) * P], w0_lo[:, A0 + c * P:A0 + (c + 1) * P],
                                  y_hi[:, cs], y_lo[:, cs], c == 0, c == DC - 1)
                last.then_inc(t_ready, 1)

            def main_product(t):
                for m in range(DC):
                    pe.wait_ge(x1t_done, t * DC + (m + 1))
                    for c in range(DC):
                        cs = slice(c * TW, (c + 1) * TW)
                        last = split3(bank[4 + m][:, :], w0m(w0_hi, c, m), w0m(w0_lo, c, m), y_hi[:, cs], y_lo[:, cs],
                                      c == 0, False)
                last.then_inc(y_used, 1)

            def lora_b0(t):
                pe.wait_ge(tsplit, t + 1)
                for m in range(DC):
                    split3(bank[4 + m][:, :], w0_hi[:, B0 + m * P:B0 + (m + 1) * P], w0_lo[:, B0 + m * P:B0 + (m + 1) * P],
                           t_hi[:, :], t_lo[:, :], False, True).then_inc(x1_ready, 1)

            def turn_x1(t):
                pe.wait_ge(x1t_done, t * DC + (DC + 4))
                for s in range(4):
                    pe.wait_ge(x1tok_evac, t * 4 + (s + 1))
                    for m in range(DC):
                        last = nc.tensor.transpose(bank[s % 2][:, m * P:(m + 1) * P],
                                                   x1_t[:, m * TW + s * P:m * TW + (s + 1) * P], ident[:, :])
                    last.then_inc(x1tok_ready, 1)

            pe.wait_ge(w0_split, 1)
            lora_a0(0)
            pe.wait_ge(const_done, 4)
            for j in range(NJ):
                pe.wait_ge(hf_evac, j // 4 + 1)
                last = nc.tensor.transpose(bank[0][:, G0 * j:G0 * (j + 1)], hf[0:G0, j * P:(j + 1) * P], ident[0:G0, 0:G0])
            last.then_inc(h_ready, 1)
            pe.wait_ge(hf_evac, NT)
            main_product(0)
            pe.wait_ge(h_norm, 1)
            for i in range(4):
                last = nc.tensor.transpose(bank[1][:, i * P:(i + 1) * P], hh[:, i * P:(i + 1) * P], ident[:, :])
            last.then_inc(hT_ready, 1)
            pe.wait_ge(hT_evac, 1)
            for i in range(4):
                last = mm(bank[2][:, 4 * E0 * i:4 * E0 * (i + 1)], hT[:, i * P:(i + 1) * P], gw2bd[:, :], start=True, stop=True)
            last.then_inc(g_ready, 1)
            pe.wait_ge(oh_ready, 1)
            mm(bank[2][:, NJ * E0:3 * NJ * E0], ones[:, :], oh[:, :], start=True, stop=True).then_inc(cnt_ready, 1)
            pe.wait_ge(wexp_done, 2)
            for j in range(NJ):
                if j == 12:
                    pe.wait_ge(wT_evac, 1)
                last = nc.tensor.transpose(bank[(j // 4) % 3][:, (j % 4) * P:(j % 4 + 1) * P],
                                           w_exp[:, j * P:(j + 1) * P], ident[:, :])
                if j % 4 == 3:
                    last.then_inc(wT_ready, 1)

            pe.wait_ge(wT_evac, NT)
            with pe.Fori(0, NT - 1) as t:
                lora_b0(t)
                lora_a0(t + 1)
                turn_x1(t)
                main_product(t + 1)
            lora_b0(NT - 1)
            turn_x1(NT - 1)

            pe.wait_ge(la_split, 1)
            pe.wait_ge(x1tok_evac, 4 * NT + 2)

            def lora_a(it, u):
                t = it * 2 + u
                for q in range(2 * AC):
                    if q >= 2:
                        pe.wait_ge(c_evac, t * DC + (q - 1))
                    for c in range(DC):
                        if q == 0:
                            pe.wait_ge(xsplit, t * DC + (c + 1))
                        cs = slice(c * TW, (c + 1) * TW)
                        ls = slice((c * 2 * AC + q) * P, (c * 2 * AC + q + 1) * P)
                        last = split3([bank[4], bank[5], bank[0], bank[1]][q][:, :], la_hi[:, ls], la_lo[:, ls],
                                      x_hi[:, cs], x_lo[:, cs], c == 0, c == DC - 1)
                    last.then_inc(ta_ready, 1)

            def gate_or_up(it, s, which):
                b = s % 2
                u = s // FC
                for c in range(DC + AC):
                    w0c = b * ST_W + which * GA_W + c * P
                    ws = slice(w0c, w0c + P)
                    if c < DC:
                        cs = slice(c * TW, (c + 1) * TW)
                        xh_, xl_ = x_hi[:, cs], x_lo[:, cs]
                    else:
                        q = which * AC + c - DC
                        if s % FC == 0:
                            pe.wait_ge(ta_split, it * (2 * LQ) + (LQ * u + q + 1))
                        cs = slice(q * TW, (q + 1) * TW)
                        xh_, xl_ = ta_hi[:, cs], ta_lo[:, cs]
                    last = split3(bank[6 + which][:, :], st_hi[:, ws], st_lo[:, ws], xh_, xl_, c == 0, c == DC + AC - 1)
                return last

            def down(it, s):
                b = s % 2
                u, f = s // FC, s % FC
                pe.wait_ge(act_split, it * (2 * FC) + (s + 1))
                pe.wait_ge(st_split, it * (4 * FC) + (2 * s + 6))
                xs = slice(b * TW, (b + 1) * TW)
                for q in range(AC):
                    w0c = b * ST_W + GU + D + q * P
                    last = split3(bank[4 + q][:, :], st_hi[:, w0c:w0c + P], st_lo[:, w0c:w0c + P],
                                  act_hi[:, xs], act_lo[:, xs], f == 0, f == FC - 1)
                    if f == FC - 1:
                        last.then_inc(td_ready, 1)
                for m in range(DC):
                    if f == 0 and m >= 2:
                        pe.wait_ge(c_evac, (it * 2 + u) * DC + (m + 1))
                    w0c = b * ST_W + GU + m * P
                    last = split3(bank[m][:, :], st_hi[:, w0c:w0c + P], st_lo[:, w0c:w0c + P],
                                  act_hi[:, xs], act_lo[:, xs], f == 0, False)
                last.then_inc(st_used, 1)

            with pe.Fori(0, NT // 2) as it:
                for u in range(2):
                    lora_a(it, u)
                    for f in range(FC):
                        s = u * FC + f
                        pe.wait_ge(st_split, it * (4 * FC) + (2 * s + 5))
                        pe.wait_ge(silu_done, it * (2 * FC) + (s + 1))
                        gate_or_up(it, s, 0).then_inc(gate_ready, 1)
                        pe.wait_ge(prod_done, it * (2 * FC) + (s + 1))
                        gate_or_up(it, s, 1).then_inc(up_ready, 1)
                        if f:
                            down(it, s - 1)
                    down(it, u * FC + FC - 1)
                    for m in range(DC):
                        for q in range(AC):
                            if m == 0:
                                pe.wait_ge(bd_split, 1)
                                pe.wait_ge(ta_split, it * (2 * LQ) + (LQ * u + 2 * AC + q + 1))
                            ts = slice(q * TW, (q + 1) * TW)
                            bs = slice(q * D + m * P, q * D + (m + 1) * P)
                            last = split3(bank[m][:, :], bd_hi[:, bs], bd_lo[:, bs], td_hi[:, ts], td_lo[:, ts], False, q == AC - 1)
                        last.then_inc(c_ready, 1)

            def c_at(j, m):
                o = (j // 4) * DC * TW + m * TW + (j % 4) * P
                return cT[:, o:o + P]

            for t in range(NT):
                for m in range(DC):
                    if m == 0:
                        pe.wait_ge(c_evac, NT * DC + 4)
                    last = mm(bank[2 + t][0:E1, :], gwT[:, m * E1:(m + 1) * E1], cT[:, (t * DC + m) * TW:(t * DC + m + 1) * TW],
                              start=(m == 0), stop=(m == DC - 1))
                last.then_inc(lf_ready, 1)
            for j in range(NJ):
                if j == 1:
                    for i in range(NJ):
                        pe.wait_ge(lf_evac, i // 4 + 1)
                        last = nc.tensor.transpose(bank[0][:, E1 * i:E1 * (i + 1)], lf[0:E1, i * P:(i + 1) * P], ident[0:E1, 0:E1])
                    last.then_inc(lgt_ready, 1)
                if j >= 6:
                    pe.wait_ge([ctok_even, ctok_odd][j % 2], (j - 6) // 2 + 1)
                for m in range(DC):
                    last = nc.tensor.transpose(bank[1 + j % 6][:, m * P:(m + 1) * P], c_at(j, m), ident[:, :])
                last.then_inc(ctok_ready, 1)
            pe.wait_ge(ohs_ready, 1)
            mm(bank[7][:, 0:NJ * E1], before[:, :], ohs[:, :], start=True, stop=True).then_inc(pos_ready, 1)
            mm(bank[7][:, NJ * E1:2 * NJ * E1], ones[:, :], ohs[:, :], start=True, stop=True).then_inc(pos_ready, 1)

            pe.wait_ge(ctok_even, NJ // 2)
            pe.wait_ge(ctok_odd, NJ // 2)

            def shared_down(it, s):
                b = s % 2
                u, i = s // SC, s % SC
                pe.wait_ge(sact_split, it * (2 * SC) + (s + 1))
                pe.wait_ge(sw_split, it * (4 * SC) + (2 * s + 6))
                ws = slice(b * SH_W + SGU, (b + 1) * SH_W)
                for r in range(4):
                    xs = slice(b * TW + r * P, b * TW + (r + 1) * P)
                    if i == 0:
                        pe.wait_ge(base_done, (it * 2 + u) * 4 + (r + 1))
                    mm(bank[r][:, :], act_hi[:, xs], sw_hi[:, ws], start=(i == 0), stop=False)
                    mm(bank[r][:, :], act_hi[:, xs], sw_lo[:, ws], start=False, stop=False)
                    last = mm(bank[r][:, :], act_lo[:, xs], sw_hi[:, ws], start=False, stop=(i == SC - 1))
                    if i == SC - 1:
                        last.then_inc(base_ready, 1)

            with pe.Fori(0, NT // 2) as it:
                for u in range(2):
                    for i in range(SC):
                        s = u * SC + i
                        b = s % 2
                        pe.wait_ge(sw_split, it * (4 * SC) + (2 * s + 5))
                        for which, free, ready in ((0, ssilu_done, sgate_ready), (1, sprod_done, sup_ready)):
                            pe.wait_ge(free, it * (2 * SC) + (s + 1))
                            for c in range(DC):
                                if i == 0 and which == 0:
                                    pe.wait_ge(csplit, (it * 2 + u) * DC + (c + 1))
                                cs = slice(c * TW, (c + 1) * TW)
                                w0c = b * SH_W + which * DC * P + c * P
                                last = split3(bank[4 + which][:, :], sw_hi[:, w0c:w0c + P], sw_lo[:, w0c:w0c + P],
                                              x_hi[:, cs], x_lo[:, cs], c == 0, c == DC - 1)
                            last.then_inc(ready, 1)
                        if i:
                            shared_down(it, s - 1)
                    shared_down(it, u * SC + SC - 1)

            pe.wait_ge(base_done, NJ + 4)
            pe.wait_ge(eg_in, 16 * EG_PARTS)
            pe.wait_ge(ed_in, 16 * ED_PARTS)
            pe.wait_ge(blk_ready, 1)

            def turn_x(b4, u, n16):
                q = u % 4
                pe.wait_ge(xg_in[q], n16)
                pe.wait_ge(xgT_evac, b4 + (u + 1))
                for c in range(DC):
                    last = nc.tensor.transpose(bank[u % 2][:, c * P:(c + 1) * P], xg[:, q * D + c * P:q * D + (c + 1) * P],
                                               ident[:, :])
                last.then_inc(xgT_ready, 1)

            def expert_of(b4, u):
                return pe.value_load(blk_e[0:1, bass.ds(b4 + u, 1)], min_val=0, max_val=E1 - 1)

            def gate_up_e(b4, u, e):
                q = u % 4
                pe.wait_ge(xgT_evac, b4 + (u + 3))
                pe.wait_ge(eh_done, b4 + (u + 1))
                for c in range(DC):
                    last = mm(bank[2 + u % 2][:, 0:2 * I1], xgT[:, q * D + c * P:q * D + (c + 1) * P],
                              eg[:, bass.ds(e * (DC * 2 * I1) + c * 2 * I1, 2 * I1)], start=(c == 0), stop=(c == DC - 1))
                last.then_inc(egu_ready, 1)

            def turn_h(b4, u):
                q = u % 4
                pe.wait_ge(eh_done, b4 + (u + 3))
                pe.wait_ge(ehT_evac, b4 + (u + 1))
                nc.tensor.transpose(bank[4][:, 0:P], eh[:, q * I1:(q + 1) * I1], ident[:, :]).then_inc(ehT_ready, 1)

            def down_e(b4, u, e):
                q = u % 4
                pe.wait_ge(ehT_evac, b4 + (u + 2))
                pe.wait_ge(ys_done, b4 + (u + 1))
                mm(bank[5 + u % 2][:, :], ehT[:, q * P:(q + 1) * P], ed[:, bass.ds(e * D, D)],
                   start=True, stop=True).then_inc(ey_ready, 1)

            turn_x(0, 0, 16)
            turn_x(0, 1, 16)
            gate_up_e(0, 0, expert_of(0, 0))
            with pe.Fori(0, NB // 4 - 1) as it:
                e_next = expert_of(it * 4, 1)
                for u in range(4):
                    turn_x(it * 4, u + 2, it * 16 + 16 * (1 + (u + 2) // 4))
                    turn_h(it * 4, u)
                    gate_up_e(it * 4, u + 1, e_next)
                    e = expert_of(it * 4, u) if u == 0 else e_this
                    e_this = e_next
                    if u < 3:
                        e_next = expert_of(it * 4, u + 2)
                    down_e(it * 4, u, e)
            b4 = NB - 4
            e = [expert_of(b4, u) for u in range(4)]
            for u in range(4):
                if u < 2:
                    turn_x(b4, u + 2, 16 * (NB // 4))
                turn_h(b4, u)
                if u < 3:
                    gate_up_e(b4, u + 1, e[u + 1])
                down_e(b4, u, e[u])


def kernel(**inputs):
    import numpy as np
    import concourse.bacc as _bacc
    from concourse.bass_utils import run_bass_kernel_spmd as _run

    i = {k: np.asarray(v) for k, v in inputs.items()}
    c = np.ascontiguousarray

    def rows(a, flip=False):
        a = a.reshape(DC, P, -1)
        return (a[:, ::-1] if flip else a).transpose(1, 0, 2)

    def pad(a, n, axis=0):
        w = [(0, 0)] * a.ndim
        w[axis] = (0, n - a.shape[axis])
        return np.pad(a, w)

    x = i["x"]
    arrays = {}
    arrays["x_heads"] = c(x.transpose(1, 2, 0).reshape(NG, CH, DC, P, B).transpose(0, 3, 2, 1, 4)).reshape(NG, P, DC * CH * B)
    s4 = [np.broadcast_to(i["L0_cond_log_dt"], (NS, H)), i["L0_cond_log_A_real"].T, i["L0_cond_A_imag"].T,
          i["L0_cond_C"][..., 0].T, i["L0_cond_C"][..., 1].T]
    arrays["s4_par"] = c(np.tile(np.concatenate(s4, axis=1), (2, 1)))
    arrays["s4_d"] = c(i["L0_cond_D"])
    arrays["lens"] = c(i["itok_B_8_3872"])
    arrays["adapters"] = c(i["itok_B_2_6"])
    la0 = i["L0_ffn_lora_A"].transpose(1, 0, 2).reshape(D, E0 * R0)
    arrays["w0"] = c(np.concatenate([rows(i["L0_ffn_weight"].T, True).reshape(P, -1), rows(la0, True).reshape(P, -1),
                                     i["L0_ffn_lora_B"].reshape(E0 * R0, D)], axis=1))
    arrays["gw1"] = c(rows(i["L0_ffn_gw1"].T, True)).reshape(P, -1)
    for k in ("gb1", "gb2"):
        arrays[k + "_d"] = c(i["L0_ffn_" + k])
    arrays["lng_d"], arrays["lnb_d"] = c(i["L0_ffn_ln_gamma"]), c(i["L0_ffn_ln_beta"])
    arrays["gw2"] = c(i["L0_ffn_gw2"].T)
    ag, au = (i["L1_cond_A_" + k][0].reshape(NA * RA, D).T for k in ("gate", "up"))
    arrays["w_la"] = c(np.concatenate([rows(ag), rows(au)], axis=2)).reshape(P, -1)
    FP = FC * P

    def stacked(k):
        w = pad(i["L1_cond_W_" + k].T, FP, 1).reshape(DC, P, FC, P)
        b = pad(i["L1_cond_B_" + k][0].transpose(0, 2, 1).reshape(NA * RA, F), FP, 1).reshape(AC, P, FC, P)
        return np.concatenate([w, b]).transpose(2, 1, 0, 3).reshape(FC, P, -1)

    wd = pad(i["L1_cond_W_down"].T, FP).reshape(FC, P, D)
    ad = pad(i["L1_cond_A_down"][0].reshape(NA * RA, F).T, FP).reshape(FC, P, NA * RA)
    arrays["w_st"] = c(np.concatenate([stacked("gate"), stacked("up"), wd, ad], axis=2))
    arrays["w_bd"] = c(i["L1_cond_B_down"][0].transpose(0, 2, 1).reshape(AC, P, D).transpose(1, 0, 2)).reshape(P, -1)
    sg = i["L1_ffn_shared_w_gate_up"].T.reshape(DC, P, 2, SC, P).transpose(3, 1, 2, 0, 4).reshape(SC, P, -1)
    arrays["w_sh"] = c(np.concatenate([sg, i["L1_ffn_shared_w_down"].T.reshape(SC, P, D)], axis=2))
    arrays["gw_d"] = c(rows(i["L1_ffn_gate_w"].T)).reshape(P, -1)
    arrays["w_eg"] = c(i["L1_ffn_w_gate_up"].transpose(2, 0, 1).reshape(DC, P, E1, 2 * I1).transpose(1, 2, 0, 3)).reshape(P, -1)
    arrays["w_ed"] = c(i["L1_ffn_w_down"].transpose(2, 0, 1)).reshape(P, -1)

    nc = _bacc.Bacc("TRN2", target_bir_lowering=False, num_devices=1)
    args = {n: nc.dram_tensor(n, a.shape, mybir.dt.from_np(a.dtype), kind="ExternalInput").ap() for n, a in arrays.items()}
    o = nc.dram_tensor("out", (N, D), F32, kind="ExternalOutput").ap()
    conditioned_blocks(nc, out=o, **args)
    r = _run(nc, [arrays], core_ids=[0])
    return r.results[0]["out"].reshape(B, H, D)
```

```python
import concourse.bass as bass
from concourse import mybir
from contextlib import ExitStack

F32 = mybir.dt.float32
F32R = mybir.dt.float32r
I32 = mybir.dt.int32
U32 = mybir.dt.uint32
ALU = mybir.AluOpType
ACT = mybir.ActivationFunctionType
AX_X = mybir.AxisListType.X

P = 128
B, H, D = 64, 32, 512
N = B * H
DC = D // P
NS = 64
RL, QL = 32, D // 32
NT, TW = N // 512, 512
NJ = N // P
BT = TW // H
E0, R0, G0 = 8, 16, 32
CAP0 = int(3.0 * N / E0)
F = 1376
FC = -(-F // P)
NA, RA = 16, 16
AC = NA * RA // P
E1, I1, S1 = 16, 128, 512
SC = S1 // P
NB = (2 * N + E1 * (P - 1)) // P
BQ = (NB - 2) // 4
GB = P // RA
GT, NGR = BT // GB, B // GB
GW = GB * H
XW, BW = 2 * DC * P, 2 * P
GU = XW + GT * BW
ST_W = GU + D + NA * RA
SH_W = 2 * DC * P + D
CH = 4
NG = H // CH
W0_W = DC * D + DC * P + D
KPW = D + P

AW = H * RL + H * QL + H
FW, CW = H * RL, H * QL

LOG2E = 1.4426950408889634
MAGIC = 12582912.0
LN2_HI, LN2_LO = 0.693359375, -2.12194440e-4
PI_DOWN = 3.1415925


def conditioned_blocks(nc, x_heads, s4_par, s4_d, lens, adapters, w0, gw1, gb1_d, lng_d, lnb_d,
                       gw2, gb2_d, w_la, w_st, w_b, w_bd, ad_rows, w_sh, gw_d, w_eg, w_ed, out):
    ctx = ExitStack()
    with ctx:
        def sem(name):
            return ctx.enter_context(nc.semaphore(name))

        base = -(-nc.sbuf_base // 32) * 32
        ctx.enter_context(nc.sbuf_tensor("arena", [P, 206 * 256], F32))

        def at(name, kb, cols, dt=F32):
            return nc.alloc_sbuf_tensor_at(name, [P, cols], dt, offset=base + int(kb * 1024))

        bank = [ctx.enter_context(nc.psum_tensor(f"bank{i}", [P, 512], F32)) for i in range(8)]

        ident = at("ident", 0, P)
        ones = at("ones", 0.5, P)
        before = at("before", 1, P)
        e_iota = at("e_iota", 1.5, E1)
        mask_len = at("mask_len", 1.75, DC * B)
        mask_ad = at("mask_ad", 2.75, AC * B)
        slot_u = at("slot_u", 3.25, 2 * NJ, U32)
        gate1 = at("gate1", 3.375, 2 * NJ)
        blk_e = at("blk_e", 3.5, NB, I32)
        tok_id = at("tok_id", 3.75, NJ, U32)
        slot_tok = at("slot_tok", 3.875, NB, U32)
        gwT = at("gwT", 4.25, DC * E1)
        gw1T = at("gw1T", 4.5, DC * G0)
        gb1 = at("gb1", 5, G0)
        lng = at("lng", 5.125, G0)
        lnb = at("lnb", 5.25, G0)
        gb2 = at("gb2", 5.375, E0)
        gw2bd = at("gw2bd", 5.5, 4 * E0)
        b_iota = at("b_iota", 5.75, NB)
        list_u = at("list_u", 6, 2 * NJ, U32)
        slot_b = at("slot_b", 6.125, 2 * NJ)
        b_rows = at("b_rows", 6.25, FC * NGR, U32)
        same_r = at("same_r", 6.625, RA)
        own_b = at("own_b", 6.6875, GB)
        ad_rows_i = at("ad_rows_i", 6.75, NGR, I32)
        ad_rows_f = at("ad_rows_f", 6.8125, NGR)
        rank_i = at("rank_i", 6.875, 1, I32)
        rank_f = at("rank_f", 6.90625, 1)
        row_base = at("row_base", 6.9375, FC * NGR)
        xT = at("xT", 8, NG * DC * CH * B)
        yT = at("yT", 40, DC * N)
        y_hi = at("y_hi", 72, DC * TW, F32R)
        y_lo = at("y_lo", 80, DC * TW, F32R)
        toep = at("toep", 88, 2 * CH * D)
        w0_hi = at("w0_hi", 104, W0_W, F32R)
        w0_lo = at("w0_lo", 116, W0_W, F32R)
        w0_raw = at("w0_raw", 128, W0_W)
        par = at("par", 140, 5 * H)
        lg, ai, cr, ci = par[:, 0:2 * H], par[:, 2 * H:3 * H], par[:, 3 * H:4 * H], par[:, 4 * H:5 * H]
        sm = at("sm", 141, 24 * 2 * H)
        kx = at("kx", 147, 2 * H, I32)
        len_i = at("len_i", 147.25, B, I32)
        ad_i = at("ad_i", 147.5, B, I32)
        len_f = at("len_f", 147.75, B)
        ad_f = at("ad_f", 148, B)
        l_iota = at("l_iota", 148.25, DC)
        a_iota = at("a_iota", 148.3125, AC)
        a_int = at("a_int", 148.375, AC, I32)
        r_iota = at("r_iota", 148.5, RL)
        q_iota = at("q_iota", 148.625, QL)
        ang = at("ang", 149, AW)
        turn = at("turn", 155.25, AW)
        dec = at("dec", 161.5, FW + CW)
        sn = at("sn", 167.5, AW)
        sh = at("sh", 173.75, CW + H)
        coarse = at("coarse", 176, CW)
        coarse_b = at("coarse_b", 178, CW)
        uu = at("uu", 180, H)
        vv = at("vv", 180.125, H)
        k_sb = at("k_sb", 181, H * RL)
        d_pad = at("d_pad", 185, H * RL)
        d_row = at("d_row", 189, H)
        fine_t = at("fine_t", 190.25, FW)
        zeros = at("zeros", 189.25, P)
        phase = at("phase", 189.75, 1)
        hf = at("hf", 152, N)
        hh = at("hh", 140, NJ * G0)
        hq = at("hq", 142, NJ * G0)
        hT = at("hT", 144, 4 * P)
        rs = at("rs", 146, 8 * NJ)
        ga = at("ga", 146.5, NJ * E0)
        mv = at("mv", 147, NJ * 8)
        mi = at("mi", 147.5, NJ * 8, U32)
        i2 = at("i2", 148, 2 * NJ)
        oh = at("oh", 148.125, 2 * NJ * E0)
        wk = at("wk", 149.125, 2 * NJ * E0)
        cn = at("cn", 150.125, 2 * E0)
        w_te = at("w_te", 150.25, NJ * E0)
        w_exp = at("w_exp", 190, NJ * E0 * R0)
        wT = at("wT", 152, N)
        t_f = at("t_f", 160, TW)
        t_hi = at("t_hi", 162, TW, F32R)
        t_lo = at("t_lo", 164, TW, F32R)
        x1_t = at("x1_t", 166, DC * TW)
        x1_tok = at("x1_tok", 88, 4 * D)
        x1T = at("x1T", 174, NT * DC * TW)
        cT = at("cT", 8, NT * DC * TW)
        x_hi = at("x_hi", 40, DC * TW, F32R)
        x_lo = at("x_lo", 48, DC * TW, F32R)
        act_hi = at("act_hi", 56, 2 * TW, F32R)
        act_lo = at("act_lo", 60, 2 * TW, F32R)
        silu_s = at("silu_s", 64, TW)
        prod_s = at("prod_s", 66, TW)
        tc_f = at("tc_f", 68, TW)
        st_hi = at("st_hi", 70, 2 * ST_W, F32R)
        st_lo = at("st_lo", 88, 2 * ST_W, F32R)
        st_raw = at("st_raw", 106, 2 * ST_W)
        tc_lo = at("tc_lo", 124, 2 * TW, F32R)
        la_hi = at("la_hi", 128, DC * 2 * AC * P, F32R)
        bd_hi = at("bd_hi", 136, GT * D, F32R)
        bd_raw = at("bd_raw", 140, GT * D)
        bd_lo = at("bd_lo", 140, GT * D, F32R)
        la_raw = at("la_raw", 144, DC * 2 * AC * P)
        la_lo = at("la_lo", 144, DC * 2 * AC * P, F32R)
        sel = at("sel", 152, AC * GT * P, F32R)
        ra_hi = at("ra_hi", 160, AC * TW, F32R)
        ra_lo = at("ra_lo", 164, AC * TW, F32R)
        tc_hi = at("tc_hi", 168, 2 * TW, F32R)
        c_tok = at("c_tok", 122, NJ * D)
        sw_hi = at("sw_hi", 70, 2 * SH_W, F32R)
        sw_lo = at("sw_lo", 82, 2 * SH_W, F32R)
        sw_raw = at("sw_raw", 94, 2 * SH_W)
        eg = at("eg", 106, E1 * DC * 2 * I1)
        ed = at("ed", 170, E1 * D)
        lf = at("lf", 198, N)
        lgt = at("lgt", 170, NJ * E1)
        mv1 = at("mv1", 171, NJ * 8)
        mi1 = at("mi1", 171.5, NJ * 8, U32)
        j2 = at("j2", 172, 2 * NJ)
        dl = at("dl", 172.125, 2 * NJ)
        oh1 = at("oh1", 172.5, 2 * NJ * E1)
        ohs = at("ohs", 174.5, NJ * E1)
        sc_a = at("sc_a", 175.5, NJ * E1)
        sc_b = at("sc_b", 176.5, NJ * E1)
        pos1 = at("pos1", 177.5, NJ * E1)
        tot1 = at("tot1", 178.5, NJ * E1)
        ohp = at("ohp", 179.5, 2 * NJ * E1)
        nbk = at("nbk", 181.5, 8 * E1)
        bcmp = at("bcmp", 182.25, NB * E1)
        ebf = at("ebf", 185.5, NB)
        slf = at("slf", 185.75, 2 * NJ)
        xg = at("xg", 40, 4 * D)
        xgT = at("xgT", 48, 4 * DC * P)
        es = at("es", 56, 4 * I1)
        eh = at("eh", 58, 4 * I1)
        ehT = at("ehT", 60, 4 * P)
        ys = at("ys", 62, 4 * D)
        y1 = at("y1", 72, 4 * D)
        y2 = at("y2", 80, 4 * D)
        fin = at("fin", 88, 4 * D)

        kpad = nc.dram_tensor("kpad", (H, KPW), F32, kind="Internal").ap()
        x1_dram = nc.dram_tensor("x1_dram", (N, D), F32, kind="Internal").ap()
        c_dram = nc.dram_tensor("c_dram", (N, D), F32, kind="Internal").ap()
        y_dram = nc.dram_tensor("y_dram", (NB * P, D), F32, kind="Internal").ap()
        st_dram = nc.dram_tensor("st_dram", (NB * P, 1), U32, kind="Internal").ap()

        par_in = sem("par_in")
        ids_in = sem("ids_in")
        small_in = sem("small_in")
        x_in = sem("x_in")
        kpad_out = sem("kpad_out")
        toep_in = [sem(f"toep_in{i}") for i in range(4)]
        x1_out = [sem(f"x1_out{i}") for i in range(4)]
        la_in = sem("la_in")
        bd_in = sem("bd_in")
        b_in = [sem(f"b_in{i}") for i in range(2)]
        st_in = [sem(f"st_in{i}") for i in range(2)]
        c_out = [sem(f"c_out{i}") for i in range(2)]
        sw_in = [sem(f"sw_in{i}") for i in range(2)]
        x1_in = sem("x1_in")
        eg_in = sem("eg_in")
        ed_in = sem("ed_in")
        list_zero = sem("list_zero")
        list_out = sem("list_out")
        xg_in = [sem(f"xg_in{i}") for i in range(4)]
        y_out = [sem(f"y_out{i}") for i in range(4)]
        y12_in = [sem(f"y12_in{i}") for i in range(4)]
        fin_out = [sem(f"fin_out{i}") for i in range(4)]
        dve_step = sem("dve_step")
        pool_step = sem("pool_step")
        iota_done = sem("iota_done")
        a_ready = sem("a_ready")
        ang_ready = sem("ang_ready")
        tanh_done = sem("tanh_done")
        dec_mul = sem("dec_mul")
        dec_done = sem("dec_done")
        sin_done = sem("sin_done")
        table_done = sem("table_done")
        k_ready = sem("k_ready")
        k_evac = sem("k_evac")
        const_done = sem("const_done")
        conv_done = sem("conv_done")
        conv_free = sem("conv_free")
        w0_split = sem("w0_split")
        w0_hi_done = sem("w0_hi_done")
        hf_ready = sem("hf_ready")
        hf_evac = sem("hf_evac")
        h_ready = sem("h_ready")
        var_done = sem("var_done")
        sqrt_done = sem("sqrt_done")
        h_norm = sem("h_norm")
        hT_ready = sem("hT_ready")
        hT_evac = sem("hT_evac")
        g_ready = sem("g_ready")
        oh_ready = sem("oh_ready")
        cnt_ready = sem("cnt_ready")
        dl_ready = sem("dl_ready")
        th_ready = sem("th_ready")
        w_ready = sem("w_ready")
        wexp_done = sem("wexp_done")
        wT_ready = sem("wT_ready")
        wT_evac = sem("wT_evac")
        yhi_done = sem("yhi_done")
        ysplit = sem("ysplit")
        y_used = sem("y_used")
        t_ready = sem("t_ready")
        tf_done = sem("tf_done")
        thi_done = sem("thi_done")
        tsplit = sem("tsplit")
        x1_ready = sem("x1_ready")
        x1t_done = sem("x1t_done")
        x1t_copied = sem("x1t_copied")
        x1tok_ready = sem("x1tok_ready")
        x1tok_evac = sem("x1tok_evac")
        la_hi_done = sem("la_hi_done")
        la_split = sem("la_split")
        bd_hi_done = sem("bd_hi_done")
        bd_split = sem("bd_split")
        xhi_done = sem("xhi_done")
        xsplit = sem("xsplit")
        ra_ready = sem("ra_ready")
        ra_hi_done = sem("ra_hi_done")
        ra_split = sem("ra_split")
        sel_done = sem("sel_done")
        tc_ready = sem("tc_ready")
        tcf_done = sem("tcf_done")
        tc_hi_done = sem("tc_hi_done")
        tc_split = sem("tc_split")
        rows_done = sem("rows_done")
        st_hi_done = sem("st_hi_done")
        st_split = sem("st_split")
        st_used = sem("st_used")
        gate_ready = sem("gate_ready")
        silu_done = sem("silu_done")
        up_ready = sem("up_ready")
        prod_done = sem("prod_done")
        acthi_done = sem("acthi_done")
        act_split = sem("act_split")
        c_ready = sem("c_ready")
        c_evac = sem("c_evac")
        lf_ready = sem("lf_ready")
        lf_evac = sem("lf_evac")
        lgt_ready = sem("lgt_ready")
        ctok_ready = sem("ctok_ready")
        ctok_even = sem("ctok_even")
        ctok_odd = sem("ctok_odd")
        ohs_ready = sem("ohs_ready")
        pos_ready = sem("pos_ready")
        pos_evac = sem("pos_evac")
        blk_ready = sem("blk_ready")
        chi_done = sem("chi_done")
        csplit = sem("csplit")
        sw_hi_done = sem("sw_hi_done")
        sw_split = sem("sw_split")
        sw_used = sem("sw_used")
        sgate_ready = sem("sgate_ready")
        ssilu_done = sem("ssilu_done")
        sup_ready = sem("sup_ready")
        sprod_done = sem("sprod_done")
        sacthi_done = sem("sacthi_done")
        sact_split = sem("sact_split")
        base_ready = sem("base_ready")
        base_done = sem("base_done")
        xgT_ready = sem("xgT_ready")
        xgT_evac = sem("xgT_evac")
        egu_ready = sem("egu_ready")
        es_done = sem("es_done")
        eh_done = sem("eh_done")
        ehT_ready = sem("ehT_ready")
        ehT_evac = sem("ehT_evac")
        ey_ready = sem("ey_ready")
        ys_done = sem("ys_done")
        fma_done = sem("fma_done")
        d_done = sem("d_done")

        SMALL_LOADS = 10
        EG_PARTS, ED_PARTS = NT * SC, 4
        LQ, LK = 3 * AC, 3
        TANH, AR, BR, BR_TURNS, T0, T1, T2, EM, SR, SI, IA, KF, RR, PP, CB, QR, QI, ER, EI = range(19)
        SD, VAR, TH, DL, MU, RC, T3 = range(7)

        def smv(i, w=H):
            return sm[:, 2 * H * i:2 * H * i + w]

        def rsv(i):
            return rs[:, NJ * i:NJ * (i + 1)]

        def fine(tile):
            return tile[:, 0:FW].rearrange("p (h r) -> p h r", h=H)

        def crs(tile, at0=0):
            return tile[:, at0:at0 + CW].rearrange("p (h q) -> p h q", h=H)

        def over_lags(col, n):
            return col.unsqueeze(2).broadcast_to([P, H, n])

        def over_heads(col):
            return col.unsqueeze(1).broadcast_to([P, H, col.shape[1]])

        def h3(tile):
            return tile.rearrange("p (j k) -> p j k", j=NJ)

        def over_k(col, k):
            return col.unsqueeze(2).broadcast_to([P, NJ, k])

        def over_j(row):
            return row.unsqueeze(1).broadcast_to([P, NJ, row.shape[1]])

        def repeat_weights(copy, half):
            n = NJ * E0 // 2
            return copy(w_exp[:, half * n * R0:(half + 1) * n * R0].rearrange("p (j r) -> p j r", r=R0),
                        w_te[:, half * n:(half + 1) * n].unsqueeze(2).broadcast_to([P, n, R0]))

        RA_BANK = [bank[4], bank[5], bank[0], bank[1], bank[4], bank[5]]
        TC_BANK = [bank[2], bank[3], bank[6]]
        h_bank = [bank[0], bank[1], bank[2], bank[7]]
        SGU = 2 * DC * P

        CREDITS = {conv_free: 4, conv_done: 4, y_used: 1, tf_done: 1, x1t_done: 4, x1t_copied: 4, x1tok_ready: 1,
                   x1tok_evac: 2, up_ready: 1, silu_done: 1, prod_done: 1, c_evac: 4, st_split: 4, tc_ready: 1,
                   sup_ready: 1, ssilu_done: 1, sprod_done: 1, base_done: 4, sw_split: 4, sw_used: 1,
                   xgT_evac: 2, eh_done: 2, ehT_evac: 1, ys_done: 2}
        CREDITS.update({s: 16 for s in x1_out + y_out})

        block = ctx.enter_context(nc.Block())

        @block.sync
        def _(sp):
            sp.dma_start(par[:, :], s4_par).then_inc(par_in, 16)
            for g in range(NG):
                sp.dma_start(xT[:, g * DC * CH * B:(g + 1) * DC * CH * B], x_heads[g]).then_inc(x_in, 16)
            sp.dma_start(w0_raw[:, :], w0).then_inc(x_in, 16)
            sp.dma_start(gw1T[:, :], gw1).then_inc(small_in, 16)
            sp.dma_start(gwT[:, :], gw_d).then_inc(small_in, 16)
            sp.dma_start(gb1[:, :], gb1_d.partition_broadcast(P)).then_inc(small_in, 16)
            sp.dma_start(lng[:, :], lng_d.partition_broadcast(P)).then_inc(small_in, 16)
            sp.dma_start(lnb[:, :], lnb_d.partition_broadcast(P)).then_inc(small_in, 16)
            sp.dma_start(gb2[:, :], gb2_d.partition_broadcast(P)).then_inc(small_in, 16)
            sp.wait_ge(const_done, 3)
            for i in range(4):
                sp.dma_start(gw2bd[G0 * i:G0 * (i + 1), E0 * i:E0 * (i + 1)], gw2).then_inc(small_in, 16)
            sp.dma_start(kpad[:, D:KPW], zeros[0:H, :]).then_inc(kpad_out, 16)
            sp.dma_start(st_dram.rearrange("(p b) o -> p (b o)", p=P), zeros[:, 0:NB].bitcast(U32)).then_inc(list_zero, 16)

            sp.wait_ge(k_evac, 2)
            sp.dma_start(kpad[:, 0:D].rearrange("h (q r) -> q h r", q=QL),
                         k_sb[0:QL, :].rearrange("q (h r) -> q h r", h=H)).then_inc(kpad_out, 16)
            sp.wait_ge(kpad_out, 32)
            with sp.Fori(0, NG // 2) as it:
                for u in range(2):
                    sp.wait_ge(conv_done, it * 4 + (2 * u + 2))
                    for pr in range(2):
                        t0 = u * CH * D + pr * 2 * D
                        sp.dma_start(toep[:, t0:t0 + 2 * D].rearrange("p (h i) -> p h i", h=2),
                                     bass.AP(kpad.tensor, (it * 2 + u) * (CH * KPW) + pr * 2 * KPW, [[1, P], [KPW, 2], [1, D]])
                                     ).then_inc(toep_in[2 * u + pr], 16)
            sp.wait_ge(wT_evac, NT)
            sp.dma_start(la_raw[:, :], w_la).then_inc(la_in, 16)
            with sp.Fori(0, NT) as t:
                for s in range(4):
                    sp.wait_ge(x1tok_evac, t * 4 + (s + 3))
                    sp.dma_start(x1_dram[bass.ds(t * TW + s * P, P), :], x1_tok[:, s * D:(s + 1) * D]).then_inc(x1_out[s], 16)
            sp.wait_ge(x1_ready, 4 * NT)
            with sp.Fori(0, NT // 2) as it:
                for s in range(2 * FC):
                    b = s % 2
                    sp.wait_ge(st_split, it * 4 * FC + (2 * s + 2))
                    sp.dma_start(st_raw[:, b * ST_W:b * ST_W + XW], w_st[s % FC, :, 0:XW]).then_inc(st_in[b], 16)
                    sp.dma_start(st_raw[:, b * ST_W + GU:(b + 1) * ST_W], w_st[s % FC, :, XW:]).then_inc(st_in[b], 16)
            sp.wait_ge(c_ready, DC * NT)
            with sp.Fori(0, NT // 2) as it:
                for s in range(2 * SC):
                    b = s % 2
                    sp.wait_ge(sw_split, it * 4 * SC + (2 * s + 2))
                    sp.dma_start(sw_raw[:, b * SH_W:(b + 1) * SH_W], w_sh[s % SC]).then_inc(sw_in[b], 16)
                    if s % SC == 2:
                        sp.wait_ge(csplit, it * 2 * DC + (s // SC + 1) * DC)
                        sp.dma_start(cT[:, bass.ds((it * 2 + s // SC) * (DC * TW), DC * TW)]
                                     .rearrange("p (s d) -> p s d", s=4),
                                     x1_dram[bass.ds((it * 2 + s // SC) * TW, TW), :]
                                     .rearrange("(s p) d -> p s d", p=P)).then_inc(x1_in, 16)
            def store_y(b4, u):
                sp.wait_ge(ys_done, b4 + (u + 3))
                sp.dma_start(y_dram[bass.ds((b4 + u) * P, P), :], ys[:, u * D:(u + 1) * D]).then_inc(y_out[u], 16)

            with sp.Fori(0, BQ) as it:
                for u in range(4):
                    store_y(it * 4, u)
            for u in range(NB - 4 * BQ):
                store_y(4 * BQ, u)
            for j in range(NJ):
                sp.wait_ge(fma_done, 2 * j + 2)
                sp.dma_start(out[j * P:(j + 1) * P, :], fin[:, (j % 4) * D:(j % 4 + 1) * D]).then_inc(fin_out[j % 4], 16)
            for u in range(4):
                sp.wait_ge(fin_out[u], 16 * NJ // 4)

        @block.gpsimd
        def _(pool):
            g = nc.gpsimd
            allow = dict(allow_small_or_imprecise_dtypes=True)
            for s, n in CREDITS.items():
                pool.sem_inc(s, n)
            count = [0]

            def link(ins):
                count[0] += 1
                ins.then_inc(pool_step, 1)
                pool.wait_ge(pool_step, count[0])

            def fold(t, total):
                w = E1 // 2
                while w > 1:
                    link(g.tensor_tensor(t[:, :, 0:w], t[:, :, 0:w], t[:, :, w:2 * w], ALU.add))
                    w //= 2
                link(g.tensor_tensor(total, t[:, :, 0], t[:, :, 1], ALU.add))

            g.iota(r_iota[:, :], pattern=[[-1, RL]], base=RL - 1, channel_multiplier=0, **allow).then_inc(iota_done, 1)
            g.iota(q_iota[:, :], pattern=[[-RL, QL]], base=RL * (QL - 1), channel_multiplier=0, **allow).then_inc(iota_done, 1)
            g.iota(l_iota[:, :], pattern=[[P, DC]], base=P - 1, channel_multiplier=-1, **allow).then_inc(iota_done, 1)
            g.iota(a_int[:, :], pattern=[[P, AC]], base=0, channel_multiplier=1).then_inc(iota_done, 1)
            pool.wait_ge(iota_done, 4)
            link(g.memset(phase[:, :], 0.0))
            g.memset(phase[0:NS, :], 0.25).then_inc(iota_done, 1)
            pool.wait_ge(iota_done, 5)
            link(g.memset(d_pad[0:QL, :], 0.0))
            pool.wait_ge(ids_in, 64)
            link(g.affine_select(out=d_row[0:QL, :], in_=d_row[0:QL, :], compare_op=ALU.is_ge, fill=0.0, base=1 - QL,
                                 pattern=[[0, H]], channel_multiplier=1))
            g.tensor_copy(d_pad[0:QL, :].rearrange("p (h r) -> p h r", h=H)[:, :, RL - 1], d_row[0:QL, :]).then_inc(d_done, 1)
            pool.wait_ge(sin_done, 1)
            pool.wait_ge(dec_done, 1)
            g.tensor_tensor(fine_t[:, :], sn[:, 0:FW], dec[:, 0:FW], ALU.mult).then_inc(table_done, 1)
            link(g.memset(gw2bd[:, :], 0.0))
            pool.sem_inc(const_done, 1)
            link(g.memset(zeros[:, :], 0.0))
            pool.sem_inc(const_done, 2)
            link(g.memset(ident[:, :], 0.0))
            link(g.affine_select(out=ident[:, :], in_=ident[:, :], compare_op=ALU.not_equal, fill=1.0, base=0,
                                 pattern=[[-1, P]], channel_multiplier=1))
            link(g.memset(ones[:, :], 1.0))
            link(g.affine_select(out=before[:, :], in_=ones[:, :], compare_op=ALU.is_gt, fill=0.0, base=0,
                                 pattern=[[1, P]], channel_multiplier=-1))
            link(g.iota(e_iota[:, :], pattern=[[1, E1]], base=0, channel_multiplier=0, **allow))
            link(g.iota(b_iota[:, :], pattern=[[1, NB]], base=0, channel_multiplier=0, **allow))
            link(g.iota(rank_i[:, :], pattern=[[0, 1]], base=0, channel_multiplier=1))
            link(g.iota(row_base[:, :], pattern=[[NA * RA, FC], [0, NGR]], base=0, channel_multiplier=0, **allow))
            link(g.iota(tok_id[:, :], pattern=[[P, NJ]], base=0, channel_multiplier=1))
            pool.sem_inc(const_done, 1)

            pool.wait_ge(rows_done, 1)
            pool.wait_ge(x1_ready, 4 * NT)
            for n in range(NT * FC):
                t, f, b = n // FC, n % FC, n % 2
                pool.wait_ge(st_split, 2 * n + 2)
                for gr in range(GT):
                    col = f * NGR + t * GT + gr
                    c0 = b * ST_W + XW + gr * BW
                    g.indirect_dma_start(out=st_raw[:, c0:c0 + BW], out_offset=None, in_=w_b,
                                         in_offset=bass.IndirectOffsetOnAxis(b_rows[:, col:col + 1], 0),
                                         bounds_check=FC * NA * RA - 1).then_inc(b_in[b], 16)
                if f == 1:
                    if t:
                        pool.wait_ge(c_ready, DC * t)
                    for gr in range(GT):
                        col = t * GT + gr
                        g.indirect_dma_start(out=bd_raw[:, gr * D:(gr + 1) * D], out_offset=None, in_=w_bd,
                                             in_offset=bass.IndirectOffsetOnAxis(b_rows[:, col:col + 1], 0),
                                             bounds_check=NA * RA - 1).then_inc(bd_in, 16)
            for j in range(1, NJ, 2):
                pool.wait_ge(ctok_odd, j // 2 + 1)
                g.dma_start(c_dram[j * P:(j + 1) * P, :], c_tok[:, j * D:(j + 1) * D]).then_inc(c_out[1], 16)
            pool.wait_ge(pos_evac, 2)
            src, dst = tot1, sc_a
            for d in (1, 2, 4, 8):
                w = d * E1
                g.tensor_copy(dst[:, 0:w], src[:, 0:w])
                link(g.tensor_tensor(dst[:, w:], src[:, w:], src[:, 0:NJ * E1 - w], ALU.add))
                src, dst = dst, (sc_b if dst is sc_a else sc_a)
            incl = src
            link(g.tensor_tensor(pos1[:, :], pos1[:, :], incl[:, :], ALU.add))
            link(g.tensor_tensor(pos1[:, :], pos1[:, :], tot1[:, :], ALU.subtract))
            cntv = incl[:, (NJ - 1) * E1:NJ * E1]
            nb = [nbk[:, i * E1:(i + 1) * E1] for i in range(8)]
            link(g.tensor_scalar(nb[0], cntv, (P - 1) / 2, 1.0 / P, ALU.add, ALU.mult))
            link(g.tensor_scalar(nb[0], nb[0], MAGIC, None, ALU.add))
            link(g.tensor_scalar(nb[0], nb[0], -MAGIC, None, ALU.add))
            si = 0
            for i, d in enumerate((1, 2, 4, 8)):
                g.tensor_copy(nb[i + 1][:, 0:d], nb[si][:, 0:d])
                link(g.tensor_tensor(nb[i + 1][:, d:], nb[si][:, d:], nb[si][:, 0:E1 - d], ALU.add))
                si = i + 1
            link(g.tensor_tensor(nb[5], nb[4], nb[0], ALU.subtract))
            link(g.tensor_scalar(nb[5], nb[5], float(P), None, ALU.mult))
            link(g.tensor_tensor(h3(pos1[:, :]), h3(pos1[:, :]), over_j(nb[5]), ALU.add))
            for k in range(2):
                link(g.tensor_tensor(ohp[:, k * NJ * E1:(k + 1) * NJ * E1], oh1[:, k * NJ * E1:(k + 1) * NJ * E1],
                                     pos1[:, :], ALU.mult))
            fold(ohp[:, :].rearrange("p (x e) -> p x e", e=E1), slf[:, :])
            link(g.tensor_copy(slot_u[:, :], slf[:, :]))
            link(g.tensor_scalar(slot_b[:, :], slf[:, :], -(P - 1) / 2, 1.0 / P, ALU.add, ALU.mult))
            link(g.tensor_scalar(slot_b[:, :], slot_b[:, :], MAGIC, None, ALU.add))
            link(g.tensor_scalar(slot_b[:, :], slot_b[:, :], -MAGIC, -float(P * NB - 1), ALU.add, ALU.mult))
            link(g.tensor_scalar(slf[:, :], slf[:, :], float(NB), None, ALU.mult))
            link(g.tensor_tensor(slf[:, :], slf[:, :], slot_b[:, :], ALU.add))
            link(g.tensor_copy(list_u[:, :], slf[:, :]))
            pool.wait_ge(list_zero, 16)
            for k in range(2):
                for j in range(NJ):
                    g.indirect_dma_start(out=st_dram, out_offset=bass.IndirectOffsetOnAxis(list_u[:, k * NJ + j:k * NJ + j + 1], 0),
                                         in_=tok_id[:, j:j + 1], in_offset=None,
                                         bounds_check=NB * P - 1).then_inc(list_out, 16)
            link(g.tensor_tensor(bcmp[:, :].rearrange("p (b e) -> p b e", e=E1),
                                 b_iota[:, :].unsqueeze(2).broadcast_to([P, NB, E1]),
                                 nb[4].unsqueeze(1).broadcast_to([P, NB, E1]), ALU.subtract))
            link(g.tensor_scalar(bcmp[:, :], bcmp[:, :], 1.0, 0.0, ALU.add, ALU.max))
            link(g.tensor_scalar(bcmp[:, :], bcmp[:, :], 1.0, None, ALU.min))
            fold(bcmp[:, :].rearrange("p (b e) -> p b e", e=E1), ebf[:, :])
            link(g.tensor_scalar(blk_e[:, :], ebf[:, :], float(E1 - 1), None, ALU.min))
            pool.wait_ge(th_ready, 2)
            link(g.tensor_scalar(gate1[:, 0:NJ], dl[:, NJ:2 * NJ], 0.5, 0.5, ALU.mult, ALU.add))
            g.tensor_scalar(gate1[:, NJ:2 * NJ], dl[:, NJ:2 * NJ], -0.5, 0.5, ALU.mult, ALU.add).then_inc(blk_ready, 1)
            pool.wait_ge(list_out, 32 * NJ)
            g.dma_start(slot_tok[:, :], st_dram.rearrange("(p b) o -> p (b o)", p=P)).then_inc(list_out, 16)
            pool.wait_ge(blk_ready, 1)
            for q in c_out:
                pool.wait_ge(q, 16 * NJ // 2)
            for k in range(ED_PARTS):
                n = E1 * D // ED_PARTS
                pool.wait_ge(sup_ready, (k + 4) * NT * SC // (ED_PARTS + 4))
                g.dma_start(ed[:, k * n:(k + 1) * n], w_ed[:, k * n:(k + 1) * n]).then_inc(ed_in, 16)
            pool.wait_ge(list_out, 32 * NJ + 16)
            pool.wait_ge(sup_ready, NT * SC + 1)
            for b in range(NB):
                if b >= 4:
                    pool.wait_ge(xgT_ready, b - 3)
                g.indirect_dma_start(out=xg[:, (b % 4) * D:(b % 4 + 1) * D], out_offset=None, in_=c_dram,
                                     in_offset=bass.IndirectOffsetOnAxis(slot_tok[:, b:b + 1], 0),
                                     bounds_check=N - 1).then_inc(xg_in[b % 4], 16)
            for u, q in enumerate(y_out):
                pool.wait_ge(q, 16 * len(range(u, NB, 4)) + 16)
            for j in range(NJ):
                u = j % 4
                if j >= 4:
                    pool.wait_ge(fma_done, 2 * (j - 3) - 1)
                g.indirect_dma_start(out=y1[:, u * D:(u + 1) * D], out_offset=None, in_=y_dram,
                                     in_offset=bass.IndirectOffsetOnAxis(slot_u[:, j:j + 1], 0),
                                     bounds_check=NB * P - 1).then_inc(y12_in[u], 16)
                if j >= 4:
                    pool.wait_ge(fma_done, 2 * (j - 3))
                g.indirect_dma_start(out=y2[:, u * D:(u + 1) * D], out_offset=None, in_=y_dram,
                                     in_offset=bass.IndirectOffsetOnAxis(slot_u[:, NJ + j:NJ + j + 1], 0),
                                     bounds_check=NB * P - 1).then_inc(y12_in[u], 16)

        @block.scalar
        def _(act):
            a = nc.scalar
            act.dma_start(len_i[:, :], lens.partition_broadcast(P)).then_inc(ids_in, 16)
            act.dma_start(ad_i[:, :], adapters.partition_broadcast(P)).then_inc(ids_in, 16)
            act.dma_start(ad_rows_i[:, :], ad_rows).then_inc(ids_in, 16)
            act.dma_start(d_row[0:QL, :], s4_d.partition_broadcast(QL)).then_inc(ids_in, 16)
            act.wait_ge(a_ready, 1)
            a.activation(smv(TANH), smv(AR), ACT.Tanh, scale=0.5).then_inc(tanh_done, 1)
            act.wait_ge(ang_ready, 1)
            a.activation(sn[:, :], ang[:, :], ACT.Sin, scale=2 * PI_DOWN).then_inc(sin_done, 1)
            a.activation(sh[:, :], ang[:, FW:AW], ACT.Sin, scale=PI_DOWN).then_inc(sin_done, 1)
            act.wait_ge(dec_mul, 1)
            a.activation(dec[:, :], dec[:, :], ACT.Exp).then_inc(dec_done, 1)
            act.wait_ge(x_in, 16 * NG + 16)
            a.copy(w0_hi[:, :], w0_raw[:, :]).then_inc(w0_hi_done, 1)
            def split_y(t):
                act.wait_ge(y_used, t + 1)
                for c in range(DC):
                    a.copy(y_hi[:, c * TW:(c + 1) * TW], yT[:, bass.ds(t * TW + c * N, TW)]).then_inc(yhi_done, 1)

            act.wait_ge(conv_free, 2 * NG + 4)
            split_y(0)
            act.wait_ge(var_done, 1)
            a.activation(rsv(SD), rsv(VAR), ACT.Sqrt).then_inc(sqrt_done, 1)
            act.wait_ge(dl_ready, 1)
            a.activation(rsv(TH), rsv(DL), ACT.Tanh, scale=0.5).then_inc(th_ready, 1)
            act.wait_ge(w_ready, 1)
            repeat_weights(a.copy, 1).then_inc(wexp_done, 1)
            for i in range(NT):
                act.wait_ge(wT_ready, i + 1)
                a.copy(wT[:, i * TW:(i + 1) * TW], bank[i % 3][:, :]).then_inc(wT_evac, 1)

            def split_x(t):
                for c in range(DC):
                    a.copy(x_hi[:, c * TW:(c + 1) * TW], x1T[:, bass.ds(t * (DC * TW) + c * TW, TW)]).then_inc(xhi_done, 1)

            def finish_tile(t):
                act.wait_ge(tf_done, t + 2)
                a.copy(t_hi[:, :], t_f[:, :]).then_inc(thi_done, 1)
                if t is not NT - 1:
                    split_y(t + 1)
                else:
                    act.wait_ge(la_in, 16)
                    a.copy(la_hi[:, :], la_raw[:, :]).then_inc(la_hi_done, 1)
                    act.wait_ge(ysplit, NT * DC)
                    act.wait_ge(x1t_copied, DC + 4)
                    split_x(0)
                for m in range(DC):
                    act.wait_ge(x1t_done, t * 4 + (m + 5))
                    a.copy(x1T[:, bass.ds(t * (DC * TW) + m * TW, TW)], x1_t[:, m * TW:(m + 1) * TW]).then_inc(x1t_copied, 1)
                for s in range(4):
                    act.wait_ge(x1tok_ready, t * 4 + (s + 2))
                    act.wait_ge(x1_out[s], t * 16 + 16)
                    a.copy(x1_tok[:, s * D:(s + 1) * D], bank[s % 2][:, :]).then_inc(x1tok_evac, 1)

            with act.Fori(0, NT - 1) as t:
                finish_tile(t)
            finish_tile(NT - 1)

            def lora_hi(it, u, k, between=None):
                for q in range(AC):
                    act.wait_ge(ra_ready, it * (2 * LQ) + (LQ * u + AC * k + q + 1))
                    act.wait_ge(tc_ready, it * (2 * LK) + (LK * u + k + 1))
                    a.copy(ra_hi[:, q * TW:(q + 1) * TW], RA_BANK[AC * k + q][:, :]).then_inc(ra_hi_done, 1)
                if between:
                    between()
                act.wait_ge(tcf_done, it * (2 * LK) + (LK * u + k + 1))
                a.copy(tc_hi[:, (k % 2) * TW:(k % 2 + 1) * TW], tc_f[:, :]).then_inc(tc_hi_done, 1)

            def evac_c(it, u):
                for m in range(DC):
                    act.wait_ge(c_ready, it * (2 * DC) + (u * DC + m + 1))
                    a.copy(cT[:, bass.ds((it * 2 + u) * (DC * TW) + m * TW, TW)], bank[m][:, :]).then_inc(c_evac, 1)

            def hi_gate_up(it, s):
                b = s % 2
                act.wait_ge(st_in[b], it * (32 * FC) + 32 * (s // 2 + 1))
                act.wait_ge(b_in[b], it * (16 * GT * FC) + 16 * GT * (s // 2 + 1))
                act.wait_ge(up_ready, it * (2 * FC) + max(s, 1))
                a.copy(st_hi[:, b * ST_W:b * ST_W + GU], st_raw[:, b * ST_W:b * ST_W + GU]).then_inc(st_hi_done, 1)

            def hi_down(it, u, f):
                b = (u * FC + f) % 2
                if f >= 2:
                    act.wait_ge(st_used, (it * 2 + u) * (FC - 1) + (f - 1))
                a.copy(st_hi[:, b * ST_W + GU:(b + 1) * ST_W],
                       st_raw[:, b * ST_W + GU:(b + 1) * ST_W]).then_inc(st_hi_done, 1)

            def hi_step_1(it, u):
                hi_down(it, u, 0)
                hi_gate_up(it, u * FC + 1)

            def swiglu_pair(it, more):
                for u in range(2):
                    t = it * 2 + u
                    lora_hi(it, u, 0, lambda: hi_gate_up(it, u * FC))
                    lora_hi(it, u, 1, lambda: hi_step_1(it, u))
                    for f in range(FC):
                        s = u * FC + f
                        b = s % 2
                        if f:
                            hi_down(it, u, f)
                            if f + 1 < FC:
                                hi_gate_up(it, s + 1)
                        act.wait_ge(gate_ready, it * (2 * FC) + (s + 1))
                        act.wait_ge(prod_done, it * (2 * FC) + (s + 1))
                        a.activation(silu_s[:, :], bank[6][:, :], ACT.Silu).then_inc(silu_done, 1)
                        act.wait_ge(prod_done, it * (2 * FC) + (s + 2))
                        a.copy(act_hi[:, b * TW:(b + 1) * TW], prod_s[:, :]).then_inc(acthi_done, 1)
                        if f == 2:
                            act.wait_ge(bd_in, t * (16 * GT) + 16 * GT)
                            a.copy(bd_hi[:, :], bd_raw[:, :]).then_inc(bd_hi_done, 1)
                    lora_hi(it, u, 2)
                    if u == 0 or more:
                        act.wait_ge(up_ready, it * (2 * FC) + ((u + 1) * FC + 1))
                        split_x(t + 1)
                    evac_c(it, u)

            with act.Fori(0, NT // 2 - 1) as it:
                swiglu_pair(it, True)
            swiglu_pair(NT // 2 - 1, False)

            def shared_hi_gate_up(it, s):
                b = s % 2
                act.wait_ge(sw_in[b], it * (16 * SC) + 16 * (s // 2 + 1))
                act.wait_ge(sup_ready, it * (2 * SC) + max(s, 1))
                a.copy(sw_hi[:, b * SH_W:b * SH_W + SGU], sw_raw[:, b * SH_W:b * SH_W + SGU]).then_inc(sw_hi_done, 1)

            def shared_x_hi(t):
                for c in range(DC):
                    a.copy(x_hi[:, c * TW:(c + 1) * TW], cT[:, bass.ds(t * (DC * TW) + c * TW, TW)]).then_inc(chi_done, 1)

            act.wait_ge(c_evac, NT * DC + 4)
            shared_x_hi(0)
            shared_hi_gate_up(0, 0)
            for j in range(0, NJ, 2):
                if j == 12:
                    act.wait_ge(dl_ready, 2)
                    a.activation(dl[:, NJ:2 * NJ], dl[:, 0:NJ], ACT.Tanh, scale=0.5).then_inc(th_ready, 1)
                act.wait_ge(ctok_ready, j + 1)
                a.copy(c_tok[:, j * D:(j + 1) * D], bank[1 + j % 6][:, :]).then_inc(ctok_even, 1)
                act.wait_ge(ctok_even, j // 2 + 1)
                act.dma_start(c_dram[j * P:(j + 1) * P, :], c_tok[:, j * D:(j + 1) * D]).then_inc(c_out[0], 16)

            def shared_pair(it, more):
                for u in range(2):
                    t = it * 2 + u
                    if u == 1:
                        act.wait_ge(sup_ready, it * (2 * SC) + (SC + 1))
                        shared_x_hi(t)
                    for i in range(SC):
                        s = u * SC + i
                        b = s % 2
                        if s == 4:
                            for q in c_out:
                                act.wait_ge(q, 16 * NJ // 2)
                        part = E1 * DC * 2 * I1 // EG_PARTS
                        eg_part = bass.ds(it * (2 * SC * part) + s * part, part)
                        act.dma_start(eg[:, eg_part], w_eg[:, eg_part]).then_inc(eg_in, 16)
                        if i == 1:
                            act.wait_ge(base_done, t * DC + DC)
                        else:
                            act.wait_ge(sw_used, t * (SC - 1) + max(i, 1))
                        a.copy(sw_hi[:, b * SH_W + SGU:(b + 1) * SH_W],
                               sw_raw[:, b * SH_W + SGU:(b + 1) * SH_W]).then_inc(sw_hi_done, 1)
                        if s + 1 < 2 * SC:
                            shared_hi_gate_up(it, s + 1)
                        act.wait_ge(sgate_ready, it * (2 * SC) + (s + 1))
                        act.wait_ge(sprod_done, it * (2 * SC) + (s + 1))
                        a.activation(silu_s[:, :], bank[4][:, :], ACT.Silu).then_inc(ssilu_done, 1)
                        act.wait_ge(sprod_done, it * (2 * SC) + (s + 2))
                        a.copy(act_hi[:, b * TW:(b + 1) * TW], prod_s[:, :]).then_inc(sacthi_done, 1)
                if more:
                    shared_hi_gate_up(it + 1, 0)
                    act.wait_ge(sup_ready, it * (2 * SC) + (2 * SC + 1))
                    shared_x_hi(it * 2 + 2)

            with act.Fori(0, NT // 2 - 1) as it:
                shared_pair(it, True)
            shared_pair(NT // 2 - 1, False)

            def evac_x(b4, u):
                act.wait_ge(xgT_ready, b4 + (u + 1))
                a.copy(xgT[:, (u % 4) * D:(u % 4 + 1) * D], bank[u % 2][:, :]).then_inc(xgT_evac, 1)

            def silu_e(b4, u):
                act.wait_ge(egu_ready, b4 + (u + 1))
                a.activation(es[:, (u % 4) * I1:(u % 4 + 1) * I1], bank[2 + u % 2][:, 0:I1], ACT.Silu).then_inc(es_done, 1)

            evac_x(0, 0)
            evac_x(0, 1)
            silu_e(0, 0)
            with act.Fori(0, BQ) as it:
                for u in range(4):
                    evac_x(it * 4, u + 2)
                    silu_e(it * 4, u + 1)
            for u in range(NB - 4 * BQ):
                if 4 * BQ + u + 2 < NB:
                    evac_x(4 * BQ, u + 2)
                if 4 * BQ + u + 1 < NB:
                    silu_e(4 * BQ, u + 1)

        @block.vector
        def _(dve):
            v = nc.vector
            count = [0]

            def link(ins):
                count[0] += 1
                ins.then_inc(dve_step, 1)
                dve.wait_ge(dve_step, count[0])

            W = 2 * H
            dve.wait_ge(par_in, 16)
            kf, rr, pp = smv(KF, W), smv(RR, W), smv(PP, W)
            link(v.tensor_scalar(kf, lg, LOG2E, MAGIC, ALU.mult, ALU.add))
            link(v.tensor_scalar(kf, kf, -MAGIC, -126.0, ALU.add, ALU.max))
            link(v.scalar_tensor_tensor(out=rr, in0=kf, scalar=-LN2_HI, in1=lg, op0=ALU.mult, op1=ALU.add))
            link(v.scalar_tensor_tensor(out=rr, in0=kf, scalar=-LN2_LO, in1=rr, op0=ALU.mult, op1=ALU.add))
            link(v.tensor_scalar(pp, rr, 1.0 / 5040, None, ALU.mult))
            for c in (1.0 / 720, 1.0 / 120, 1.0 / 24, 1.0 / 6, 0.5, 1.0):
                link(v.scalar_tensor_tensor(out=pp, in0=pp, scalar=c, in1=rr, op0=ALU.add, op1=ALU.mult))
            link(v.tensor_scalar(kx[:, :], kf, 127.0, None, ALU.add))
            link(v.tensor_scalar(kx[:, :], kx[:, :], 23, None, ALU.logical_shift_left))
            link(v.scalar_tensor_tensor(out=pp, in0=pp, scalar=1.0, in1=kx[:, :].bitcast(F32), op0=ALU.add, op1=ALU.mult))
            dt, a_re = pp[:, 0:H], pp[:, H:W]
            link(v.scalar_tensor_tensor(out=smv(AR), in0=dt, scalar=-1.0, in1=a_re, op0=ALU.mult, op1=ALU.mult))
            v.tensor_tensor(smv(BR), dt, ai, ALU.mult).then_inc(a_ready, 1)
            dve.wait_ge(a_ready, 1)
            dve.wait_ge(iota_done, 5)
            brt = smv(BR_TURNS)
            link(v.tensor_scalar(brt, smv(BR), 1.0 / 6.283185307179586, None, ALU.mult))
            v.tensor_tensor(fine(ang), over_lags(brt, RL), over_heads(r_iota[:, :]), ALU.mult)
            v.tensor_tensor(crs(ang, FW), over_lags(brt, QL), over_heads(q_iota[:, :]), ALU.mult)
            link(v.tensor_copy(ang[:, FW + CW:AW], brt))
            link(v.tensor_scalar(ang[:, 0:FW], ang[:, 0:FW], phase[:, :], None, ALU.add))
            link(v.tensor_scalar(turn[:, :], ang[:, :], MAGIC, -MAGIC, ALU.add, ALU.add))
            v.tensor_tensor(ang[:, :], ang[:, :], turn[:, :], ALU.subtract).then_inc(ang_ready, 1)
            v.tensor_tensor(fine(dec), over_lags(smv(AR), RL), over_heads(r_iota[:, :]), ALU.mult)
            v.tensor_tensor(crs(dec, FW), over_lags(smv(AR), QL), over_heads(q_iota[:, :]), ALU.mult).then_inc(dec_mul, 1)
            link(v.tensor_tensor(smv(T0), a_re, a_re, ALU.mult))
            link(v.tensor_tensor(smv(T1), ai, ai, ALU.mult))
            link(v.tensor_tensor(smv(T0), smv(T0), smv(T1), ALU.add))
            link(v.reciprocal(smv(IA), smv(T0)))
            link(v.tensor_tensor(smv(T0), ci, ai, ALU.mult))
            link(v.tensor_tensor(smv(T1), cr, a_re, ALU.mult))
            link(v.tensor_tensor(smv(T0), smv(T0), smv(T1), ALU.subtract))
            link(v.scalar_tensor_tensor(out=smv(QR), in0=smv(T0), scalar=2.0, in1=smv(IA), op0=ALU.mult, op1=ALU.mult))
            link(v.tensor_tensor(smv(T0), cr, ai, ALU.mult))
            link(v.tensor_tensor(smv(T1), ci, a_re, ALU.mult))
            link(v.tensor_tensor(smv(T0), smv(T0), smv(T1), ALU.add))
            link(v.scalar_tensor_tensor(out=smv(QI), in0=smv(T0), scalar=-2.0, in1=smv(IA), op0=ALU.mult, op1=ALU.mult))
            dve.wait_ge(tanh_done, 1)
            link(v.tensor_scalar(smv(T0), smv(TANH), -1.0, 1.0, ALU.mult, ALU.add))
            link(v.reciprocal(smv(T1), smv(T0)))
            link(v.scalar_tensor_tensor(out=smv(EM), in0=smv(TANH), scalar=2.0, in1=smv(T1), op0=ALU.mult, op1=ALU.mult))
            dve.wait_ge(sin_done, 2)
            shb, snb = sh[:, CW:CW + H], sn[:, FW + CW:AW]
            link(v.tensor_tensor(smv(T0), shb, shb, ALU.mult))
            link(v.tensor_scalar(smv(CB), smv(T0), -2.0, 1.0, ALU.mult, ALU.add))
            link(v.tensor_tensor(smv(T1), smv(EM), smv(CB), ALU.mult))
            link(v.scalar_tensor_tensor(out=smv(ER), in0=smv(T0), scalar=-2.0, in1=smv(T1), op0=ALU.mult, op1=ALU.add))
            link(v.scalar_tensor_tensor(out=smv(EI), in0=smv(EM), scalar=1.0, in1=snb, op0=ALU.add, op1=ALU.mult))
            v.tensor_tensor(smv(T0), smv(QR), smv(ER), ALU.mult)
            link(v.tensor_tensor(smv(T1), smv(QI), smv(EI), ALU.mult))
            v.tensor_tensor(smv(T2), smv(QR), smv(EI), ALU.mult)
            link(v.tensor_tensor(smv(CB), smv(QI), smv(ER), ALU.mult))
            v.tensor_tensor(smv(SR), smv(T0), smv(T1), ALU.subtract)
            link(v.tensor_tensor(smv(SI), smv(T2), smv(CB), ALU.add))
            lo, hi = slice(0, NS), slice(NS, P)
            csr, csi = sm[:, 2 * H * SR:2 * H * SR + H], sm[:, 2 * H * SI:2 * H * SI + H]
            v.tensor_copy(uu[lo, :], csr[lo, :])
            v.tensor_scalar(uu[hi, :], csi[hi, :], -1.0, None, ALU.mult)
            v.tensor_scalar(vv[lo, :], csi[lo, :], -1.0, None, ALU.mult)
            link(v.tensor_scalar(vv[hi, :], csr[hi, :], -1.0, None, ALU.mult))
            dve.wait_ge(dec_done, 1)
            link(v.tensor_tensor(coarse[:, :], sh[:, 0:CW], sh[:, 0:CW], ALU.mult))
            link(v.tensor_scalar(coarse[:, :], coarse[:, :], -2.0, 1.0, ALU.mult, ALU.add))
            link(v.tensor_tensor(crs(coarse), crs(coarse), over_lags(uu[:, :], QL), ALU.mult))
            link(v.tensor_tensor(crs(coarse_b), crs(sn, FW), over_lags(vv[:, :], QL), ALU.mult))
            link(v.tensor_tensor(coarse[:, :], coarse[:, :], coarse_b[:, :], ALU.add))
            v.tensor_tensor(coarse[:, :], coarse[:, :], dec[:, FW:FW + CW], ALU.mult).then_inc(table_done, 1)
            dve.wait_ge(ids_in, 64)
            link(v.tensor_copy(len_f[:, :], len_i[:, :]))
            for m in range(DC):
                link(v.tensor_scalar(mask_len[:, m * B:(m + 1) * B], len_f[:, :], l_iota[:, m:m + 1], None, ALU.is_gt))
            link(v.tensor_copy(ad_f[:, :], ad_i[:, :]))
            link(v.tensor_scalar(a_int[:, :], a_int[:, :], 4, None, ALU.logical_shift_right))
            link(v.tensor_copy(a_iota[:, :], a_int[:, :]))
            for m in range(AC):
                link(v.tensor_scalar(mask_ad[:, m * B:(m + 1) * B], ad_f[:, :], a_iota[:, m:m + 1], None, ALU.is_equal))
            dve.wait_ge(d_done, 1)
            for i in range(2):
                dve.wait_ge(k_ready, i + 1)
                v.tensor_tensor(k_sb[0:QL, i * 512:(i + 1) * 512], bank[i][0:QL, :], d_pad[0:QL, i * 512:(i + 1) * 512],
                                ALU.add).then_inc(k_evac, 1)
            dve.wait_ge(w0_hi_done, 1)
            v.tensor_tensor(w0_lo[:, :], w0_raw[:, :], w0_hi[:, :].bitcast(F32), ALU.subtract).then_inc(w0_split, 1)

            dve.wait_ge(const_done, 4)
            link(v.tensor_scalar(own_b[:, :], e_iota[:, 0:GB], a_iota[:, 0:1], 0.5, ALU.is_equal, ALU.mult))
            link(v.tensor_scalar(rank_i[:, :], rank_i[:, :], RA - 1, None, ALU.bitwise_and))
            link(v.tensor_copy(rank_f[:, :], rank_i[:, :]))
            link(v.tensor_scalar(same_r[:, :], e_iota[:, 0:RA], rank_f[:, :], None, ALU.is_equal))
            link(v.tensor_copy(ad_rows_f[:, :], ad_rows_i[:, :]))
            link(v.tensor_scalar(ad_rows_f[:, :], ad_rows_f[:, :], float(RA), rank_f[:, :], ALU.mult, ALU.add))
            v.tensor_tensor(b_rows[:, :].rearrange("p (f g) -> p f g", f=FC), row_base[:, :].rearrange("p (f g) -> p f g", f=FC),
                            ad_rows_f[:, :].unsqueeze(1).broadcast_to([P, FC, NGR]), ALU.add).then_inc(rows_done, 1)

            mask_h = mask_len[:, :].rearrange("p (m b) -> p m b", m=DC).unsqueeze(1).broadcast_to([P, 2, DC, B])
            y_heads = yT[:, :].rearrange("p (m b h) -> p h m b", m=DC, b=B)
            with dve.Fori(0, NG // 2) as it:
                for u in range(2):
                    for pr in range(2):
                        dve.wait_ge(conv_done, it * 4 + (2 * u + pr + 5))
                        v.tensor_tensor(y_heads[:, bass.ds(it * (2 * CH) + (u * CH + 2 * pr), 2), :, :],
                                        bank[2 * u + pr][:, :].rearrange("p (h m b) -> p h m b", h=2, m=DC), mask_h,
                                        ALU.mult).then_inc(conv_free, 1)

            def split_y(t):
                for c in range(DC):
                    cs = slice(c * TW, (c + 1) * TW)
                    dve.wait_ge(yhi_done, t * DC + (c + 1))
                    v.tensor_tensor(y_lo[:, cs], yT[:, bass.ds(t * TW + c * N, TW)], y_hi[:, cs].bitcast(F32),
                                    ALU.subtract).then_inc(ysplit, 1)

            for t in range(NT):
                dve.wait_ge(hf_ready, t + 1)
                v.tensor_copy(hf[0:G0, t * TW:(t + 1) * TW], h_bank[t][0:G0, :]).then_inc(hf_evac, 1)
                if t == 0:
                    split_y(0)

            dve.wait_ge(small_in, 16 * SMALL_LOADS)
            dve.wait_ge(h_ready, 1)
            link(v.tensor_tensor(h3(hh[:, :]), h3(bank[0][:, :]), over_j(gb1[:, :]), ALU.add))
            link(v.tensor_reduce(rsv(MU), h3(hh[:, :]), AX_X, ALU.add))
            link(v.tensor_scalar(rsv(MU), rsv(MU), 1.0 / G0, None, ALU.mult))
            link(v.tensor_tensor(h3(hh[:, :]), h3(hh[:, :]), over_k(rsv(MU), G0), ALU.subtract))
            link(v.tensor_tensor(hq[:, :], hh[:, :], hh[:, :], ALU.mult))
            link(v.tensor_reduce(rsv(VAR), h3(hq[:, :]), AX_X, ALU.add))
            v.tensor_scalar(rsv(VAR), rsv(VAR), 1.0 / G0, 1e-5, ALU.mult, ALU.add).then_inc(var_done, 1)
            dve.wait_ge(sqrt_done, 1)
            link(v.reciprocal(rsv(RC), rsv(SD)))
            link(v.tensor_tensor(rsv(T3), rsv(RC), rsv(RC), ALU.mult))
            link(v.tensor_tensor(rsv(T3), rsv(T3), rsv(VAR), ALU.mult))
            link(v.tensor_scalar(rsv(T3), rsv(T3), -0.5, 1.5, ALU.mult, ALU.add))
            link(v.tensor_tensor(rsv(RC), rsv(RC), rsv(T3), ALU.mult))
            link(v.tensor_tensor(h3(hh[:, :]), h3(hh[:, :]), over_k(rsv(RC), G0), ALU.mult))
            link(v.tensor_tensor(h3(hh[:, :]), h3(hh[:, :]), over_j(lng[:, :]), ALU.mult))
            link(v.tensor_tensor(h3(hh[:, :]), h3(hh[:, :]), over_j(lnb[:, :]), ALU.add))
            v.tensor_scalar(hh[:, :], hh[:, :], 0.0, None, ALU.max).then_inc(h_norm, 1)
            dve.wait_ge(hT_ready, 1)
            v.tensor_copy(hT[:, :], bank[1][:, :]).then_inc(hT_evac, 1)
            dve.wait_ge(g_ready, 1)
            link(v.tensor_tensor(h3(ga[:, :]), h3(bank[2][:, 0:NJ * E0]), over_j(gb2[:, :]), ALU.add))
            for j in range(NJ):
                last = v.max(mv[:, 8 * j:8 * j + 8], ga[:, E0 * j:E0 * j + E0])
            link(last)
            for j in range(NJ):
                last = v.max_index(mi[:, 8 * j:8 * j + 8], mv[:, 8 * j:8 * j + 8], ga[:, E0 * j:E0 * j + E0])
            link(last)
            mv3 = mv[:, :].rearrange("p (j k) -> p k j", k=8)
            link(v.tensor_copy(i2[:, :].rearrange("p (k j) -> p k j", k=2),
                               mi[:, :].rearrange("p (j k) -> p k j", k=8)[:, 0:2, :]))
            v.tensor_tensor(rsv(DL), mv3[:, 0, :], mv3[:, 1, :], ALU.subtract).then_inc(dl_ready, 1)
            v.tensor_tensor(oh[:, :].rearrange("p (x e) -> p x e", e=E0),
                            i2[:, :].unsqueeze(2).broadcast_to([P, 2 * NJ, E0]),
                            e_iota[:, 0:E0].unsqueeze(1).broadcast_to([P, 2 * NJ, E0]), ALU.is_equal).then_inc(oh_ready, 1)
            dve.wait_ge(th_ready, 1)
            dve.wait_ge(oh_ready, 1)
            link(v.tensor_scalar(i2[:, 0:NJ], rsv(TH), 0.5, 0.5, ALU.mult, ALU.add))
            link(v.tensor_scalar(i2[:, NJ:2 * NJ], rsv(TH), -0.5, 0.5, ALU.mult, ALU.add))
            link(v.tensor_tensor(wk[:, :].rearrange("p (x e) -> p x e", e=E0), oh[:, :].rearrange("p (x e) -> p x e", e=E0),
                                 i2[:, :].unsqueeze(2).broadcast_to([P, 2 * NJ, E0]), ALU.mult))
            dve.wait_ge(cnt_ready, 1)
            link(v.tensor_reduce(cn[:, :].rearrange("p (k e) -> p k e", k=2),
                                 bank[2][:, NJ * E0:3 * NJ * E0].rearrange("p (k j e) -> p k e j", k=2, j=NJ), AX_X, ALU.add))
            link(v.tensor_scalar(cn[:, :], cn[:, :], float(CAP0), 1.0 / R0, ALU.is_le, ALU.mult))
            for k in range(2):
                wk_k = h3(wk[:, k * NJ * E0:(k + 1) * NJ * E0])
                link(v.tensor_tensor(wk_k, wk_k, over_j(cn[:, k * E0:(k + 1) * E0]), ALU.mult))
            v.tensor_tensor(w_te[:, :], wk[:, 0:NJ * E0], wk[:, NJ * E0:2 * NJ * E0], ALU.add).then_inc(w_ready, 1)
            dve.wait_ge(w_ready, 1)
            repeat_weights(v.tensor_copy, 0).then_inc(wexp_done, 1)

            xh = xT[:, :].rearrange("p (g c h b) -> p g c h b", g=NG, c=DC, h=CH)

            def split_x(t):
                for c in range(DC):
                    cs = slice(c * TW, (c + 1) * TW)
                    dve.wait_ge(xhi_done, t * DC + (c + 1))
                    v.tensor_tensor(x_lo[:, cs], x1T[:, bass.ds(t * (DC * TW) + c * TW, TW)], x_hi[:, cs].bitcast(F32),
                                    ALU.subtract).then_inc(xsplit, 1)

            def finish_tile(t):
                dve.wait_ge(t_ready, t + 1)
                v.tensor_tensor(t_f[:, :], bank[3][:, :], wT[:, bass.ds(t * TW, TW)], ALU.mult).then_inc(tf_done, 1)
                dve.wait_ge(thi_done, t + 1)
                v.tensor_tensor(t_lo[:, :], t_f[:, :], t_hi[:, :].bitcast(F32), ALU.subtract).then_inc(tsplit, 1)
                if t is not NT - 1:
                    split_y(t + 1)
                else:
                    dve.wait_ge(la_hi_done, 1)
                    v.tensor_tensor(la_lo[:, :], la_raw[:, :], la_hi[:, :].bitcast(F32), ALU.subtract).then_inc(la_split, 1)
                    split_x(0)
                dve.wait_ge(x1tok_ready, t * 4 + 1)
                for m in range(DC):
                    dve.wait_ge(x1_ready, t * DC + (m + 1))
                    dve.wait_ge(x1t_copied, t * DC + (m + 1))
                    v.tensor_tensor(x1_t[:, m * TW:(m + 1) * TW].rearrange("p (b g h) -> p b g h", g=NG, h=CH),
                                    bank[4 + m][:, :].rearrange("p (b g h) -> p b g h", g=NG, h=CH),
                                    xh[:, :, m, :, bass.ds(t * BT, BT)].rearrange("p g h b -> p b g h"),
                                    ALU.add).then_inc(x1t_done, 1)

            dve.wait_ge(wT_evac, NT)
            with dve.Fori(0, NT - 1) as t:
                finish_tile(t)
            finish_tile(NT - 1)

            def lora_lo(it, u, k, between=None):
                for q in range(AC):
                    dve.wait_ge(ra_hi_done, it * (2 * LQ) + (LQ * u + AC * k + q + 1))
                    qs = slice(q * TW, (q + 1) * TW)
                    v.tensor_tensor(ra_lo[:, qs], RA_BANK[AC * k + q][:, :], ra_hi[:, qs].bitcast(F32),
                                    ALU.subtract).then_inc(ra_split, 1)
                if between:
                    between()
                n = it * (2 * LK) + (LK * u + k + 1)
                dve.wait_ge(tc_ready, it * (2 * LK) + (LK * u + k + 2))
                v.tensor_tensor(tc_f[:, :].rearrange("p (g b h) -> p g b h", g=GT, b=GB),
                                TC_BANK[k][:, :].rearrange("p (g b h) -> p g b h", g=GT, b=GB),
                                own_b[:, :].unsqueeze(1).unsqueeze(3).broadcast_to([P, GT, GB, H]), ALU.mult).then_inc(tcf_done, 1)
                dve.wait_ge(tc_hi_done, n)
                ks = slice((k % 2) * TW, (k % 2 + 1) * TW)
                v.tensor_tensor(tc_lo[:, ks], tc_f[:, :], tc_hi[:, ks].bitcast(F32), ALU.subtract).then_inc(tc_split, 1)
                dve.wait_ge(tc_split, n)

            def lo_part(it, s, part):
                b = s % 2
                sl = slice(b * ST_W, b * ST_W + GU) if part == 0 else slice(b * ST_W + GU, (b + 1) * ST_W)
                n = 2 * s + part + 1
                dve.wait_ge(st_hi_done, it * (4 * FC) + n)
                v.tensor_tensor(st_lo[:, sl], st_raw[:, sl], st_hi[:, sl].bitcast(F32), ALU.subtract).then_inc(st_split, 1)

            def swiglu_pair(it, more):
                for u in range(2):
                    t = it * 2 + u
                    for q in range(AC):
                        v.tensor_tensor(sel[:, q * GT * P:(q + 1) * GT * P].rearrange("p (b r) -> p b r", r=RA),
                                        mask_ad[:, bass.ds(t * BT + q * B, BT)].unsqueeze(2).broadcast_to([P, BT, RA]),
                                        same_r[:, :].unsqueeze(1).broadcast_to([P, BT, RA]), ALU.mult).then_inc(sel_done, 1)
                    lora_lo(it, u, 0, lambda: lo_part(it, u * FC, 0))
                    lora_lo(it, u, 1, lambda: lo_part(it, u * FC, 1))
                    for f in range(FC):
                        s = u * FC + f
                        b = s % 2
                        if f:
                            lo_part(it, s, 1)
                        if f + 1 < FC:
                            lo_part(it, s + 1, 0)
                        dve.wait_ge(up_ready, it * (2 * FC) + (s + 2))
                        dve.wait_ge(silu_done, it * (2 * FC) + (s + 2))
                        v.tensor_tensor(prod_s[:, :], bank[7][:, :], silu_s[:, :], ALU.mult).then_inc(prod_done, 1)
                        dve.wait_ge(acthi_done, it * (2 * FC) + (s + 1))
                        v.tensor_tensor(act_lo[:, b * TW:(b + 1) * TW], prod_s[:, :], act_hi[:, b * TW:(b + 1) * TW].bitcast(F32),
                                        ALU.subtract).then_inc(act_split, 1)
                        dve.wait_ge(act_split, it * (2 * FC) + (s + 1))
                        if f == 2:
                            dve.wait_ge(bd_hi_done, t + 1)
                            v.tensor_tensor(bd_lo[:, :], bd_raw[:, :], bd_hi[:, :].bitcast(F32), ALU.subtract).then_inc(bd_split, 1)
                    lora_lo(it, u, 2)
                    if u == 0 or more:
                        split_x(t + 1)

            for q in x1_out:
                dve.wait_ge(q, 16 * NT + 16)
            with dve.Fori(0, NT // 2 - 1) as it:
                swiglu_pair(it, True)
            swiglu_pair(NT // 2 - 1, False)

            def shared_lo(it, s, part):
                b = s % 2
                sl = slice(b * SH_W, b * SH_W + SGU) if part == 0 else slice(b * SH_W + SGU, (b + 1) * SH_W)
                dve.wait_ge(sw_hi_done, it * (4 * SC) + (2 * s + part + 1))
                v.tensor_tensor(sw_lo[:, sl], sw_raw[:, sl], sw_hi[:, sl].bitcast(F32), ALU.subtract).then_inc(sw_split, 1)

            def shared_base(it, u, r):
                j = (it * 2 + u) * 4
                dve.wait_ge(x1_in, (it * 2 + u) * 16 + 16)
                dve.wait_ge(base_ready, j + (r + 1))
                row = cT[:, bass.ds(j * D + r * D, D)]
                v.tensor_tensor(row, bank[r][:, :], row, ALU.add).then_inc(base_done, 1)

            def shared_x_lo(t):
                for c in range(DC):
                    cs = slice(c * TW, (c + 1) * TW)
                    dve.wait_ge(chi_done, t * DC + (c + 1))
                    v.tensor_tensor(x_lo[:, cs], cT[:, bass.ds(t * (DC * TW) + c * TW, TW)], x_hi[:, cs].bitcast(F32),
                                    ALU.subtract).then_inc(csplit, 1)

            shared_x_lo(0)
            for t in range(NT):
                dve.wait_ge(lf_ready, t + 1)
                v.tensor_copy(lf[0:E1, t * TW:(t + 1) * TW], bank[2 + t][0:E1, :]).then_inc(lf_evac, 1)
                if t == NT - 2:
                    shared_lo(0, 0, 0)

            def c_rows(j):
                dve.wait_ge(ctok_ready, j + 1)
                v.tensor_copy(c_tok[:, j * D:(j + 1) * D], bank[1 + j % 6][:, :]).then_inc(ctok_odd, 1)

            dve.wait_ge(lgt_ready, 1)
            link(v.tensor_copy(lgt[:, :], bank[0][:, 0:NJ * E1]))
            for j in range(NJ):
                last = v.max(mv1[:, 8 * j:8 * j + 8], lgt[:, E1 * j:E1 * j + E1])
            link(last)
            c_rows(1)
            for j in range(NJ):
                last = v.max_index(mi1[:, 8 * j:8 * j + 8], mv1[:, 8 * j:8 * j + 8], lgt[:, E1 * j:E1 * j + E1])
            link(last)
            c_rows(3)
            link(v.tensor_copy(j2[:, :].rearrange("p (k j) -> p k j", k=2),
                               mi1[:, :].rearrange("p (j k) -> p k j", k=8)[:, 0:2, :]))
            link(v.tensor_tensor(oh1[:, :].rearrange("p (x e) -> p x e", e=E1),
                                 j2[:, :].unsqueeze(2).broadcast_to([P, 2 * NJ, E1]),
                                 e_iota[:, :].unsqueeze(1).broadcast_to([P, 2 * NJ, E1]), ALU.is_equal))
            v.tensor_tensor(ohs[:, :], oh1[:, 0:NJ * E1], oh1[:, NJ * E1:2 * NJ * E1], ALU.add).then_inc(ohs_ready, 1)
            c_rows(5)
            mv4 = mv1[:, :].rearrange("p (j k) -> p k j", k=8)
            v.tensor_tensor(dl[:, 0:NJ], mv4[:, 0, :], mv4[:, 1, :], ALU.subtract).then_inc(dl_ready, 1)
            for j in range(7, NJ, 2):
                c_rows(j)
            dve.wait_ge(pos_ready, 2)
            for which, dst in ((0, pos1), (1, tot1)):
                v.tensor_copy(dst[:, :], bank[7][:, which * NJ * E1:(which + 1) * NJ * E1]).then_inc(pos_evac, 1)
            def shared_pair(it, more):
                for u in range(2):
                    if u == 1:
                        shared_x_lo(it * 2 + 1)
                        for s in range(4):
                            shared_base(it, 0, s)
                    for i in range(SC):
                        s = u * SC + i
                        b = s % 2
                        shared_lo(it, s, 1)
                        if s + 1 < 2 * SC:
                            shared_lo(it, s + 1, 0)
                        dve.wait_ge(sup_ready, it * (2 * SC) + (s + 2))
                        dve.wait_ge(ssilu_done, it * (2 * SC) + (s + 2))
                        v.tensor_tensor(prod_s[:, :], bank[5][:, :], silu_s[:, :], ALU.mult).then_inc(sprod_done, 1)
                        dve.wait_ge(sacthi_done, it * (2 * SC) + (s + 1))
                        v.tensor_tensor(act_lo[:, b * TW:(b + 1) * TW], prod_s[:, :], act_hi[:, b * TW:(b + 1) * TW].bitcast(F32),
                                        ALU.subtract).then_inc(sact_split, 1)
                        dve.wait_ge(sact_split, it * (2 * SC) + (s + 1))
                if more:
                    shared_lo(it + 1, 0, 0)
                    shared_x_lo(it * 2 + 2)
                for s in range(4):
                    shared_base(it, 1, s)

            with dve.Fori(0, NT // 2 - 1) as it:
                shared_pair(it, True)
            shared_pair(NT // 2 - 1, False)

            def act_e(b4, u):
                q = u % 4
                dve.wait_ge(es_done, b4 + (u + 1))
                v.tensor_tensor(eh[:, q * I1:(q + 1) * I1], bank[2 + u % 2][:, I1:2 * I1], es[:, q * I1:(q + 1) * I1],
                                ALU.mult).then_inc(eh_done, 1)

            def step_e(b4, u, bd4, nxt):
                q = u % 4
                dve.wait_ge(ehT_ready, b4 + (u + 1))
                v.tensor_copy(ehT[:, q * P:(q + 1) * P], bank[4][:, 0:P]).then_inc(ehT_evac, 1)
                if nxt:
                    act_e(b4, u + 1)
                dve.wait_ge(ey_ready, b4 + (u + 1))
                dve.wait_ge(y_out[q], bd4 + 16)
                v.tensor_copy(ys[:, q * D:(q + 1) * D], bank[5 + u % 2][:, :]).then_inc(ys_done, 1)

            act_e(0, 0)
            with dve.Fori(0, BQ) as it:
                for u in range(4):
                    step_e(it * 4, u, it * 16, True)
            for u in range(NB - 4 * BQ):
                step_e(4 * BQ, u, 16 * BQ, 4 * BQ + u + 1 < NB)

            for j in range(NJ):
                u = j % 4
                us = slice(u * D, (u + 1) * D)
                dve.wait_ge(y12_in[u], 32 * (j // 4 + 1))
                if j >= 4:
                    dve.wait_ge(fin_out[u], 16 * (j // 4))
                v.scalar_tensor_tensor(out=fin[:, us], in0=y1[:, us], scalar=gate1[:, j:j + 1],
                                       in1=cT[:, j * D:(j + 1) * D], op0=ALU.mult, op1=ALU.add).then_inc(fma_done, 1)
                dve.wait_ge(fma_done, 2 * j + 1)
                v.scalar_tensor_tensor(out=fin[:, us], in0=y2[:, us], scalar=gate1[:, NJ + j:NJ + j + 1],
                                       in1=fin[:, us], op0=ALU.mult, op1=ALU.add).then_inc(fma_done, 1)

        @block.tensor
        def _(pe):
            mm = nc.tensor.matmul

            def split3(o, w_hi, w_lo, x_hi_, x_lo_, start, stop):
                mm(o, w_hi, x_hi_, start=start, stop=False)
                mm(o, w_hi, x_lo_, start=False, stop=False)
                return mm(o, w_lo, x_hi_, start=False, stop=stop)

            pe.wait_ge(table_done, 2)
            for h in range(H):
                i, c = h // (H // 2), (h % (H // 2)) * RL
                last = mm(bank[i][0:QL, c:c + RL], coarse[:, h * QL:(h + 1) * QL], fine_t[:, h * RL:(h + 1) * RL],
                          start=True, stop=True)
                if h % (H // 2) == H // 2 - 1:
                    last.then_inc(k_ready, 1)

            x5 = xT[:, :].rearrange("p (g c h b) -> p g c h b", g=NG, c=DC, h=CH)
            pe.wait_ge(k_evac, 2)
            pe.wait_ge(x_in, 16 * NG + 16)
            with pe.Fori(0, NG // 2) as it:
                for u in range(2):
                    for pr in range(2):
                        pe.wait_ge(toep_in[2 * u + pr], it * 16 + 16)
                        pe.wait_ge(conv_free, it * 4 + (2 * u + pr + 1))
                        for h2 in range(2):
                            hh_ = 2 * pr + h2
                            for d in range(DC):
                                i0 = (u * CH + hh_) * D + D - P * (d + 1)
                                last = mm(bank[2 * u + pr][:, h2 * DC * B + d * B:(h2 + 1) * DC * B],
                                          toep[:, i0:i0 + P], x5[:, bass.ds(it * 2 + u, 1), 0:DC - d, hh_, :],
                                          start=(d == 0), stop=(d == DC - 1), skip_group_check=True)
                        last.then_inc(conv_done, 1)

            pe.wait_ge(conv_free, 2 * NG + 4)
            pe.wait_ge(small_in, 16 * SMALL_LOADS)
            for t in range(NT):
                for m in range(DC):
                    last = mm(h_bank[t][0:G0, :], gw1T[:, m * G0:(m + 1) * G0], yT[:, m * N + t * TW:m * N + (t + 1) * TW],
                              start=(m == 0), stop=(m == DC - 1))
                last.then_inc(hf_ready, 1)

            def w0m(part, c, m):
                return part[:, c * D + m * P:c * D + (m + 1) * P]

            A0, B0 = DC * D, DC * D + DC * P

            def lora_a0(t):
                pe.wait_ge(tf_done, t + 1)
                for c in range(DC):
                    cs = slice(c * TW, (c + 1) * TW)
                    pe.wait_ge(ysplit, t * DC + (c + 1))
                    last = split3(bank[3][:, :], w0_hi[:, A0 + c * P:A0 + (c + 1) * P], w0_lo[:, A0 + c * P:A0 + (c + 1) * P],
                                  y_hi[:, cs], y_lo[:, cs], c == 0, c == DC - 1)
                last.then_inc(t_ready, 1)

            def main_product(t):
                for m in range(DC):
                    pe.wait_ge(x1t_done, t * DC + (m + 1))
                    for c in range(DC):
                        cs = slice(c * TW, (c + 1) * TW)
                        last = split3(bank[4 + m][:, :], w0m(w0_hi, c, m), w0m(w0_lo, c, m), y_hi[:, cs], y_lo[:, cs],
                                      c == 0, False)
                last.then_inc(y_used, 1)

            def lora_b0(t):
                pe.wait_ge(tsplit, t + 1)
                for m in range(DC):
                    split3(bank[4 + m][:, :], w0_hi[:, B0 + m * P:B0 + (m + 1) * P], w0_lo[:, B0 + m * P:B0 + (m + 1) * P],
                           t_hi[:, :], t_lo[:, :], False, True).then_inc(x1_ready, 1)

            def turn_x1(t):
                pe.wait_ge(x1t_done, t * DC + (DC + 4))
                for s in range(4):
                    pe.wait_ge(x1tok_evac, t * 4 + (s + 1))
                    for m in range(DC):
                        last = nc.tensor.transpose(bank[s % 2][:, m * P:(m + 1) * P],
                                                   x1_t[:, m * TW + s * P:m * TW + (s + 1) * P], ident[:, :])
                    last.then_inc(x1tok_ready, 1)

            pe.wait_ge(w0_split, 1)
            lora_a0(0)
            pe.wait_ge(const_done, 4)
            for j in range(NJ):
                pe.wait_ge(hf_evac, j // 4 + 1)
                last = nc.tensor.transpose(bank[0][:, G0 * j:G0 * (j + 1)], hf[0:G0, j * P:(j + 1) * P], ident[0:G0, 0:G0])
            last.then_inc(h_ready, 1)
            pe.wait_ge(hf_evac, NT)
            main_product(0)
            pe.wait_ge(h_norm, 1)
            for i in range(4):
                last = nc.tensor.transpose(bank[1][:, i * P:(i + 1) * P], hh[:, i * P:(i + 1) * P], ident[:, :])
            last.then_inc(hT_ready, 1)
            pe.wait_ge(hT_evac, 1)
            for i in range(4):
                last = mm(bank[2][:, 4 * E0 * i:4 * E0 * (i + 1)], hT[:, i * P:(i + 1) * P], gw2bd[:, :], start=True, stop=True)
            last.then_inc(g_ready, 1)
            pe.wait_ge(oh_ready, 1)
            mm(bank[2][:, NJ * E0:3 * NJ * E0], ones[:, :], oh[:, :], start=True, stop=True).then_inc(cnt_ready, 1)
            pe.wait_ge(wexp_done, 2)
            for j in range(NJ):
                if j == 12:
                    pe.wait_ge(wT_evac, 1)
                last = nc.tensor.transpose(bank[(j // 4) % 3][:, (j % 4) * P:(j % 4 + 1) * P],
                                           w_exp[:, j * P:(j + 1) * P], ident[:, :])
                if j % 4 == 3:
                    last.then_inc(wT_ready, 1)

            pe.wait_ge(wT_evac, NT)
            with pe.Fori(0, NT - 1) as t:
                lora_b0(t)
                lora_a0(t + 1)
                turn_x1(t)
                main_product(t + 1)
            lora_b0(NT - 1)
            turn_x1(NT - 1)

            pe.wait_ge(la_split, 1)
            pe.wait_ge(x1tok_evac, 4 * NT + 2)

            def lora_a(it, u, q):
                t = it * 2 + u
                if q >= 2:
                    pe.wait_ge(c_evac, t * DC + (q - 1))
                for c in range(DC):
                    if q == 0:
                        pe.wait_ge(xsplit, t * DC + (c + 1))
                    cs = slice(c * TW, (c + 1) * TW)
                    ls = slice((c * 2 * AC + q) * P, (c * 2 * AC + q + 1) * P)
                    last = split3(RA_BANK[q][:, :], la_hi[:, ls], la_lo[:, ls], x_hi[:, cs], x_lo[:, cs], c == 0, c == DC - 1)
                last.then_inc(ra_ready, 1)

            def choose(it, u, k):
                t = it * 2 + u
                if k < 2:
                    pe.wait_ge(c_evac, t * DC + (k + 3))
                pe.wait_ge(sel_done, t * AC + AC)
                pe.wait_ge(ra_split, it * (2 * LQ) + (LQ * u + AC * k + AC))
                for gr in range(GT):
                    for q in range(AC):
                        pick = sel[:, (q * GT + gr) * P:(q * GT + gr + 1) * P]
                        for part, first, end in ((ra_hi, q == 0, False), (ra_lo, False, q == AC - 1)):
                            last = mm(TC_BANK[k][:, gr * GW:(gr + 1) * GW], pick, part[:, q * TW + gr * GW:q * TW + (gr + 1) * GW],
                                      start=first, stop=end)
                last.then_inc(tc_ready, 1)

            def gate_or_up(it, s, which, between=None):
                b = s % 2
                t = it * 2 + s // FC
                o = bank[6 + which]
                for c in range(DC):
                    if c == DC - 1:
                        if between:
                            between()
                        if s % FC == 0:
                            pe.wait_ge(tc_split, t * LK + (which + 1))
                        for gr in range(GT):
                            w0c = b * ST_W + XW + gr * BW + which * P
                            ts = slice(which * TW + gr * GW, which * TW + (gr + 1) * GW)
                            split3(o[:, gr * GW:(gr + 1) * GW], st_hi[:, w0c:w0c + P], st_lo[:, w0c:w0c + P],
                                   tc_hi[:, ts], tc_lo[:, ts], False, False)
                    w0c = b * ST_W + which * DC * P + c * P
                    cs = slice(c * TW, (c + 1) * TW)
                    last = split3(o[:, :], st_hi[:, w0c:w0c + P], st_lo[:, w0c:w0c + P], x_hi[:, cs], x_lo[:, cs],
                                  c == 0, c == DC - 1)
                return last

            def down_lora(it, s):
                b = s % 2
                f = s % FC
                pe.wait_ge(act_split, it * (2 * FC) + (s + 1))
                pe.wait_ge(st_split, it * (4 * FC) + (2 * s + 6))
                xs = slice(b * TW, (b + 1) * TW)
                for q in range(AC):
                    w0c = b * ST_W + GU + D + q * P
                    last = split3(bank[4 + q][:, :], st_hi[:, w0c:w0c + P], st_lo[:, w0c:w0c + P],
                                  act_hi[:, xs], act_lo[:, xs], f == 0, f == FC - 1)
                    if f == FC - 1:
                        last.then_inc(ra_ready, 1)

            def down_cols(it, s, first, end):
                b = s % 2
                f = s % FC
                xs = slice(b * TW, (b + 1) * TW)
                for m in range(first, end):
                    w0c = b * ST_W + GU + m * P
                    if f < FC - 1:
                        last = split3(bank[m][:, :], st_hi[:, w0c:w0c + P], st_lo[:, w0c:w0c + P],
                                      act_hi[:, xs], act_lo[:, xs], f == 0, False)
                    else:
                        mm(bank[m][:, :], st_hi[:, w0c:w0c + P], act_hi[:, xs], start=False, stop=False)
                        mm(bank[m][:, :], st_hi[:, w0c:w0c + P], act_lo[:, xs], start=False, stop=False)
                if f < FC - 1 and end == DC:
                    last.then_inc(st_used, 1)

            with pe.Fori(0, NT // 2) as it:
                for u in range(2):
                    t = it * 2 + u
                    for q in range(3):
                        lora_a(it, u, q)
                    choose(it, u, 0)
                    lora_a(it, u, 3)
                    for f in range(FC):
                        s = u * FC + f
                        pe.wait_ge(st_split, it * (4 * FC) + (2 * s + 5))
                        pe.wait_ge(silu_done, it * (2 * FC) + (s + 1))
                        gate_or_up(it, s, 0, (lambda: choose(it, u, 1)) if f == 0 else None).then_inc(gate_ready, 1)
                        pe.wait_ge(prod_done, it * (2 * FC) + (s + 1))
                        gate_or_up(it, s, 1).then_inc(up_ready, 1)
                        if 0 < f < FC - 1:
                            down_lora(it, s - 1)
                            down_cols(it, s - 1, 0, DC)
                    s = u * FC + FC - 1
                    down_lora(it, s - 1)
                    down_cols(it, s - 1, 0, 1)
                    down_lora(it, s)
                    down_cols(it, s - 1, 1, 3)
                    pe.wait_ge(silu_done, it * (2 * FC) + (s + 2))
                    choose(it, u, 2)
                    down_cols(it, s - 1, 3, DC)
                    down_cols(it, s, 0, DC)
                    pe.wait_ge(bd_split, t + 1)
                    pe.wait_ge(tc_split, t * LK + LK)
                    for m in range(DC):
                        for gr in range(GT):
                            ts = slice(gr * GW, (gr + 1) * GW)
                            bs = slice(gr * D + m * P, gr * D + (m + 1) * P)
                            split3(bank[m][:, ts], bd_hi[:, bs], bd_lo[:, bs], tc_hi[:, ts], tc_lo[:, ts], False, False)
                        b = (u * FC + FC - 1) % 2
                        w0c = b * ST_W + GU + m * P
                        mm(bank[m][:, :], st_lo[:, w0c:w0c + P], act_hi[:, b * TW:(b + 1) * TW],
                           start=False, stop=True).then_inc(c_ready, 1)

            def c_at(j, m):
                o = (j // 4) * DC * TW + m * TW + (j % 4) * P
                return cT[:, o:o + P]

            for t in range(NT):
                for m in range(DC):
                    if m == 0:
                        pe.wait_ge(c_evac, NT * DC + 4)
                    last = mm(bank[2 + t][0:E1, :], gwT[:, m * E1:(m + 1) * E1], cT[:, (t * DC + m) * TW:(t * DC + m + 1) * TW],
                              start=(m == 0), stop=(m == DC - 1))
                last.then_inc(lf_ready, 1)
            for j in range(NJ):
                if j == 1:
                    for i in range(NJ):
                        pe.wait_ge(lf_evac, i // 4 + 1)
                        last = nc.tensor.transpose(bank[0][:, E1 * i:E1 * (i + 1)], lf[0:E1, i * P:(i + 1) * P], ident[0:E1, 0:E1])
                    last.then_inc(lgt_ready, 1)
                if j >= 6:
                    pe.wait_ge([ctok_even, ctok_odd][j % 2], (j - 6) // 2 + 1)
                for m in range(DC):
                    last = nc.tensor.transpose(bank[1 + j % 6][:, m * P:(m + 1) * P], c_at(j, m), ident[:, :])
                last.then_inc(ctok_ready, 1)
            pe.wait_ge(ohs_ready, 1)
            mm(bank[7][:, 0:NJ * E1], before[:, :], ohs[:, :], start=True, stop=True).then_inc(pos_ready, 1)
            mm(bank[7][:, NJ * E1:2 * NJ * E1], ones[:, :], ohs[:, :], start=True, stop=True).then_inc(pos_ready, 1)

            pe.wait_ge(ctok_even, NJ // 2)
            pe.wait_ge(ctok_odd, NJ // 2)

            def shared_down(it, s):
                b = s % 2
                u, i = s // SC, s % SC
                pe.wait_ge(sact_split, it * (2 * SC) + (s + 1))
                pe.wait_ge(sw_split, it * (4 * SC) + (2 * s + 6))
                ws = slice(b * SH_W + SGU, (b + 1) * SH_W)
                for r in range(4):
                    xs = slice(b * TW + r * P, b * TW + (r + 1) * P)
                    if i == 0:
                        pe.wait_ge(base_done, (it * 2 + u) * 4 + (r + 1))
                    mm(bank[r][:, :], act_hi[:, xs], sw_hi[:, ws], start=(i == 0), stop=False)
                    mm(bank[r][:, :], act_hi[:, xs], sw_lo[:, ws], start=False, stop=False)
                    last = mm(bank[r][:, :], act_lo[:, xs], sw_hi[:, ws], start=False, stop=(i == SC - 1))
                    if i == SC - 1:
                        last.then_inc(base_ready, 1)
                    elif r == 3:
                        last.then_inc(sw_used, 1)

            with pe.Fori(0, NT // 2) as it:
                for u in range(2):
                    for i in range(SC):
                        s = u * SC + i
                        b = s % 2
                        pe.wait_ge(sw_split, it * (4 * SC) + (2 * s + 5))
                        for which, free, ready in ((0, ssilu_done, sgate_ready), (1, sprod_done, sup_ready)):
                            pe.wait_ge(free, it * (2 * SC) + (s + 1))
                            for c in range(DC):
                                if i == 0 and which == 0:
                                    pe.wait_ge(csplit, (it * 2 + u) * DC + (c + 1))
                                cs = slice(c * TW, (c + 1) * TW)
                                w0c = b * SH_W + which * DC * P + c * P
                                last = split3(bank[4 + which][:, :], sw_hi[:, w0c:w0c + P], sw_lo[:, w0c:w0c + P],
                                              x_hi[:, cs], x_lo[:, cs], c == 0, c == DC - 1)
                            last.then_inc(ready, 1)
                        if i:
                            shared_down(it, s - 1)
                    shared_down(it, u * SC + SC - 1)

            pe.wait_ge(base_done, NJ + 4)
            pe.wait_ge(eg_in, 16 * EG_PARTS)
            pe.wait_ge(ed_in, 16 * ED_PARTS)
            pe.wait_ge(blk_ready, 1)

            def turn_x(b4, u, n16):
                q = u % 4
                pe.wait_ge(xg_in[q], n16)
                pe.wait_ge(xgT_evac, b4 + (u + 1))
                for c in range(DC):
                    last = nc.tensor.transpose(bank[u % 2][:, c * P:(c + 1) * P], xg[:, q * D + c * P:q * D + (c + 1) * P],
                                               ident[:, :])
                last.then_inc(xgT_ready, 1)

            def expert_of(b4, u):
                return pe.value_load(blk_e[0:1, bass.ds(b4 + u, 1)], min_val=0, max_val=E1 - 1)

            def gate_up_e(b4, u, e):
                q = u % 4
                pe.wait_ge(xgT_evac, b4 + (u + 3))
                pe.wait_ge(eh_done, b4 + (u + 1))
                for c in range(DC):
                    last = mm(bank[2 + u % 2][:, 0:2 * I1], xgT[:, q * D + c * P:q * D + (c + 1) * P],
                              eg[:, bass.ds(e * (DC * 2 * I1) + c * 2 * I1, 2 * I1)], start=(c == 0), stop=(c == DC - 1))
                last.then_inc(egu_ready, 1)

            def turn_h(b4, u):
                q = u % 4
                pe.wait_ge(eh_done, b4 + (u + 3))
                pe.wait_ge(ehT_evac, b4 + (u + 1))
                nc.tensor.transpose(bank[4][:, 0:P], eh[:, q * I1:(q + 1) * I1], ident[:, :]).then_inc(ehT_ready, 1)

            def down_e(b4, u, e):
                q = u % 4
                pe.wait_ge(ehT_evac, b4 + (u + 2))
                pe.wait_ge(ys_done, b4 + (u + 1))
                mm(bank[5 + u % 2][:, :], ehT[:, q * P:(q + 1) * P], ed[:, bass.ds(e * D, D)],
                   start=True, stop=True).then_inc(ey_ready, 1)

            turn_x(0, 0, 16)
            turn_x(0, 1, 16)
            gate_up_e(0, 0, expert_of(0, 0))
            with pe.Fori(0, BQ) as it:
                e_next = expert_of(it * 4, 1)
                for u in range(4):
                    turn_x(it * 4, u + 2, it * 16 + 16 * (1 + (u + 2) // 4))
                    turn_h(it * 4, u)
                    gate_up_e(it * 4, u + 1, e_next)
                    e = expert_of(it * 4, u) if u == 0 else e_this
                    e_this = e_next
                    if u < 3:
                        e_next = expert_of(it * 4, u + 2)
                    down_e(it * 4, u, e)
            b4 = 4 * BQ
            e = [expert_of(b4, u) for u in range(NB - b4)]
            for u in range(NB - b4):
                if b4 + u + 2 < NB:
                    turn_x(b4, u + 2, 16 * (BQ + 1))
                turn_h(b4, u)
                if b4 + u + 1 < NB:
                    gate_up_e(b4, u + 1, e[u + 1])
                down_e(b4, u, e[u])


def kernel(**inputs):
    import numpy as np
    import concourse.bacc as _bacc
    from concourse.bass_utils import run_bass_kernel_spmd as _run

    i = {k: np.asarray(v) for k, v in inputs.items()}
    c = np.ascontiguousarray

    def rows(a, flip=False):
        a = a.reshape(DC, P, -1)
        return (a[:, ::-1] if flip else a).transpose(1, 0, 2)

    def pad(a, n, axis=0):
        w = [(0, 0)] * a.ndim
        w[axis] = (0, n - a.shape[axis])
        return np.pad(a, w)

    x = i["x"]
    arrays = {}
    arrays["x_heads"] = c(x.transpose(1, 2, 0).reshape(NG, CH, DC, P, B).transpose(0, 3, 2, 1, 4)).reshape(NG, P, DC * CH * B)
    s4 = [np.broadcast_to(i["L0_cond_log_dt"], (NS, H)), i["L0_cond_log_A_real"].T, i["L0_cond_A_imag"].T,
          i["L0_cond_C"][..., 0].T, i["L0_cond_C"][..., 1].T]
    arrays["s4_par"] = c(np.tile(np.concatenate(s4, axis=1), (2, 1)))
    arrays["s4_d"] = c(i["L0_cond_D"])
    arrays["lens"] = c(i["itok_B_8_3872"])
    arrays["adapters"] = c(i["itok_B_2_6"])
    la0 = i["L0_ffn_lora_A"].transpose(1, 0, 2).reshape(D, E0 * R0)
    arrays["w0"] = c(np.concatenate([rows(i["L0_ffn_weight"].T, True).reshape(P, -1), rows(la0, True).reshape(P, -1),
                                     i["L0_ffn_lora_B"].reshape(E0 * R0, D)], axis=1))
    arrays["gw1"] = c(rows(i["L0_ffn_gw1"].T, True)).reshape(P, -1)
    for k in ("gb1", "gb2"):
        arrays[k + "_d"] = c(i["L0_ffn_" + k])
    arrays["lng_d"], arrays["lnb_d"] = c(i["L0_ffn_ln_gamma"]), c(i["L0_ffn_ln_beta"])
    arrays["gw2"] = c(i["L0_ffn_gw2"].T)
    ag, au = (i["L1_cond_A_" + k][0].reshape(NA * RA, D).T for k in ("gate", "up"))
    arrays["w_la"] = c(np.concatenate([rows(ag), rows(au)], axis=2)).reshape(P, -1)
    FP = FC * P

    def w_of(k):
        return pad(i["L1_cond_W_" + k].T, FP, 1).reshape(DC, P, FC, P).transpose(2, 1, 0, 3).reshape(FC, P, -1)

    wd = pad(i["L1_cond_W_down"].T, FP).reshape(FC, P, D)
    ad = pad(i["L1_cond_A_down"][0].reshape(NA * RA, F).T, FP).reshape(FC, P, NA * RA)
    arrays["w_st"] = c(np.concatenate([w_of("gate"), w_of("up"), wd, ad], axis=2))
    bg, bu = (pad(i["L1_cond_B_" + k][0].transpose(0, 2, 1).reshape(NA * RA, F), FP, 1).reshape(NA * RA, FC, P).transpose(1, 0, 2)
              for k in ("gate", "up"))
    arrays["w_b"] = c(np.concatenate([bg, bu], axis=2)).reshape(FC * NA * RA, BW)
    arrays["w_bd"] = c(i["L1_cond_B_down"][0].transpose(0, 2, 1)).reshape(NA * RA, D)
    arrays["ad_rows"] = c(np.repeat(i["itok_B_2_6"].reshape(NGR, GB).T, RA, axis=0))
    sg = i["L1_ffn_shared_w_gate_up"].T.reshape(DC, P, 2, SC, P).transpose(3, 1, 2, 0, 4).reshape(SC, P, -1)
    arrays["w_sh"] = c(np.concatenate([sg, i["L1_ffn_shared_w_down"].T.reshape(SC, P, D)], axis=2))
    arrays["gw_d"] = c(rows(i["L1_ffn_gate_w"].T)).reshape(P, -1)
    arrays["w_eg"] = c(i["L1_ffn_w_gate_up"].transpose(2, 0, 1).reshape(DC, P, E1, 2 * I1).transpose(1, 2, 0, 3)).reshape(P, -1)
    arrays["w_ed"] = c(i["L1_ffn_w_down"].transpose(2, 0, 1)).reshape(P, -1)

    nc = _bacc.Bacc("TRN2", target_bir_lowering=False, num_devices=1)
    args = {n: nc.dram_tensor(n, a.shape, mybir.dt.from_np(a.dtype), kind="ExternalInput").ap() for n, a in arrays.items()}
    o = nc.dram_tensor("out", (N, D), F32, kind="ExternalOutput").ap()
    conditioned_blocks(nc, out=o, **args)
    r = _run(nc, [arrays], core_ids=[0])
    return r.results[0]["out"].reshape(B, H, D)
```
